# Optimizing a Trainium2 kernel written in Bass

```python
import numpy as np
import jax
import jax.numpy as jnp

def _softmax(x, axis=-1):
    return jax.nn.softmax(x, axis=axis)

def _gelu(x):
    return jax.nn.gelu(x, approximate=True)

def _silu(x):
    return jax.nn.silu(x)

def _sigmoid(x):
    return jax.nn.sigmoid(x)

def _layernorm(x, axis=-1, eps=1e-05):
    m = jnp.mean(x, axis=axis, keepdims=True)
    v = jnp.var(x, axis=axis, keepdims=True)
    return (x - m) / jnp.sqrt(v + eps)

def _scatter_add(tgt, idx, src, axis=0):
    return tgt.at[idx].add(src)

def _segment_sum(src, seg, n):
    return jax.ops.segment_sum(src, seg, n)
kernel_name = 'mk_lm_tower_d1_tok_ids1024_r4_c4b079'

def setup_inputs(seed: int=0):
    np.random.seed(seed)
    _w = jnp.asarray

    def _rec_inputs():
        import jax
        import jax.numpy as jnp
        _rk = jax.random.key(seed)
        x = jax.random.randint(jax.random.fold_in(_rk, 1), (4, 2048), 0, 12564, jnp.int32)
        return x
    x = _rec_inputs()

    def _L0_tok_setup():
        import jax, jax.numpy as jnp
        import numpy as np
        VOCAB = 50257
        NUM_DIM = 256
        BATCH = 4
        SEQ = 1024
        key = jax.random.key(seed)
        k_tok, k_w, k_b = jax.random.split(key, 3)
        tokens = jax.random.randint(k_tok, (BATCH, SEQ), 0, VOCAB)
        weight = jax.random.normal(k_w, (NUM_DIM, VOCAB), dtype=jnp.float32) * 0.02
        bias = jax.random.normal(k_b, (NUM_DIM,), dtype=jnp.float32) * 0.02
        return {'tokens': tokens, 'weight': weight, 'bias': bias}
    _L0_tok_all = _L0_tok_setup()
    _L0_tok_in = {k: v for k, v in _L0_tok_all.items() if k in ('weight', 'bias')}
    del _L0_tok_all

    def _L0_attn_setup():
        import jax, jax.numpy as jnp
        import numpy as np
        import math
        DIM = 256
        HEADS = 8
        DIM_HEAD = 64
        SEQ = 2048
        BATCH = 2
        WINDOW = 64
        NQ = 256
        NKV = 256
        FETCH_K_RATIO = 9.0 / 8.0
        N_ITERS = 20
        EPS = 0.03
        EPS_INIT = 4.0
        EPS_DECAY = 0.7
        HDIM = HEADS * DIM_HEAD

        def _layernorm(x, g, b, eps=1e-05):
            mu = x.mean(-1, keepdims=True)
            var = ((x - mu) ** 2).mean(-1, keepdims=True)
            return (x - mu) * jax.lax.rsqrt(var + eps) * g + b

        def _rmsnorm(x, gamma):
            normed = x / jnp.maximum(jnp.linalg.norm(x, axis=-1, keepdims=True), 1e-12)
            return normed * x.shape[-1] ** 0.5 * gamma

        def _rotate_half(x):
            x1, x2 = jnp.split(x, 2, axis=-1)
            return jnp.concatenate([-x2, x1], axis=-1)

        def _apply_rope(pos, t):
            return t * jnp.cos(pos) + _rotate_half(t) * jnp.sin(pos)

        def _coor_descent(s, k):
            logk = math.log(max(k, 1e-20))
            b = -s
            a = jnp.zeros_like(s[..., :1])
            cur = max(EPS_INIT, EPS)
            for _ in range(N_ITERS):
                sb = (s + b) / cur
                a = cur * (logk - jax.nn.logsumexp(sb, axis=-1, keepdims=True))
                b = -jax.nn.relu(s + a)
                cur = max(cur * EPS_DECAY, EPS)
            return jnp.exp((s + a + b) / cur)

        def _route(x, tok, num_tokens):
            s = jnp.einsum('bnd,d->bn', x, tok)
            eff_k = min(num_tokens * FETCH_K_RATIO, x.shape[1])
            scores = _coor_descent(s, eff_k)
            sel_scores, sel_idx = jax.lax.top_k(scores, num_tokens)
            sel_scores = sel_scores + jax.lax.stop_gradient(1.0 - sel_scores)
            routed = jnp.take_along_axis(x, sel_idx[..., None], axis=1)
            return (sel_idx, sel_scores, routed)

        def _light_attn(x, ln_g, ln_b, qkv_w, out_w):
            b, n, d = x.shape
            h, dh, w = (HEADS, DIM_HEAD, WINDOW)
            nw = n // w
            xn = _layernorm(x, ln_g, ln_b)
            q, k, v = jnp.split(xn @ qkv_w, 3, axis=-1)
            to_heads = lambda t: t.reshape(b, n, h, dh).transpose(0, 2, 1, 3)
            q, k, v = (to_heads(q), to_heads(k), to_heads(v))
            bq = q.reshape(b, h, nw, w, dh) * dh ** (-0.5)

            def look_around(t):
                tp = jnp.pad(t.reshape(b, h, nw, w, dh), ((0, 0), (0, 0), (1, 1), (0, 0), (0, 0)))
                return jnp.concatenate([tp[:, :, i:nw + i] for i in range(3)], axis=3)
            bk, bv = (look_around(k), look_around(v))
            sim = jnp.einsum('bhwid,bhwjd->bhwij', bq, bk)
            t_q = jnp.arange(n).reshape(nw, w)
            tpad = jnp.pad(t_q, ((1, 1), (0, 0)), constant_values=-1)
            t_k = jnp.concatenate([tpad[i:nw + i] for i in range(3)], axis=-1)
            valid = (t_k >= 0)[:, None, :] & (jnp.abs(t_q[:, :, None] - t_k[:, None, :]) <= w)
            sim = jnp.where(valid[None, None], sim, -jnp.finfo(sim.dtype).max)
            attn = jax.nn.softmax(sim, axis=-1)
            out = jnp.einsum('bhwij,bhwjd->bhwid', attn, bv)
            out = out.reshape(b, h, n, dh).transpose(0, 2, 1, 3).reshape(b, n, h * dh)
            return out @ out_w

        def _heavy_attn(xq, ctx, scores_kv, gamma, q_w, kv_w, null_kv, out_w, rope_q, rope_k):
            b = xq.shape[0]
            h, dh = (HEADS, DIM_HEAD)
            xq = _rmsnorm(xq, gamma)
            ctx = _rmsnorm(ctx, gamma)
            q = (xq @ q_w).reshape(b, -1, h, dh).transpose(0, 2, 1, 3)
            kv = jnp.einsum('hdi,bni->bhnd', kv_w, ctx)
            k, v = (kv[..., :dh], kv[..., dh:])
            v = v * scores_kv[:, None, :, None]
            q = _apply_rope(rope_q[:, None], q)
            k = _apply_rope(rope_k[:, None], k)
            nk = jnp.broadcast_to(null_kv[0][None, :, None, :], (b, h, 1, dh))
            nv = jnp.broadcast_to(null_kv[1][None, :, None, :], (b, h, 1, dh))
            k = jnp.concatenate([nk, k], axis=2)
            v = jnp.concatenate([nv, v], axis=2)
            sim = jnp.einsum('bhid,bhjd->bhij', q, k) * dh ** (-0.5)
            attn = jax.nn.softmax(sim, axis=-1)
            out = jnp.einsum('bhij,bhjd->bhid', attn, v)
            out = out.transpose(0, 2, 1, 3).reshape(b, -1, h * dh)
            return out @ out_w

        def _forward(x, ln_gamma, ln_beta, light_qkv_w, light_out_w, q_route_tok, kv_route_tok, heavy_gamma, heavy_q_w, heavy_kv_w, heavy_null_kv, heavy_out_w, null_q_token):
            b, n, d = x.shape
            light_out = _light_attn(x, ln_gamma, ln_beta, light_qkv_w, light_out_w)
            idx_q, sc_q, rt_q = _route(x, q_route_tok, NQ)
            idx_kv, sc_kv, rt_kv = _route(x, kv_route_tok, NKV)
            inv_freq = 1.0 / 10000.0 ** (jnp.arange(0, DIM_HEAD, 2, dtype=jnp.float32) / DIM_HEAD)
            freqs = jnp.arange(n, dtype=jnp.float32)[:, None] * inv_freq[None]
            pos = jnp.concatenate([freqs, freqs], axis=-1)
            rope_q = pos[idx_q]
            rope_k = pos[idx_kv]
            heavy_out = _heavy_attn(rt_q, rt_kv, sc_kv, heavy_gamma, heavy_q_w, heavy_kv_w, heavy_null_kv, heavy_out_w, rope_q, rope_k)
            heavy_out = heavy_out * sc_q[..., None]
            out = jnp.broadcast_to(null_q_token, x.shape)
            out = out.at[jnp.arange(b)[:, None], idx_q].set(heavy_out)
            return light_out + out
        ks = jax.random.split(jax.random.key(seed), 10)
        d = DIM
        return {'x': jax.random.normal(ks[0], (BATCH, SEQ, d), jnp.float32), 'ln_gamma': jnp.ones((d,), jnp.float32), 'ln_beta': jnp.zeros((d,), jnp.float32), 'light_qkv_w': jax.random.normal(ks[1], (d, 3 * HDIM), jnp.float32) * 0.02, 'light_out_w': jax.random.normal(ks[2], (HDIM, d), jnp.float32) * 0.02, 'q_route_tok': jax.random.normal(ks[3], (d,), jnp.float32), 'kv_route_tok': jax.random.normal(ks[4], (d,), jnp.float32), 'heavy_gamma': jnp.ones((d,), jnp.float32), 'heavy_q_w': jax.random.normal(ks[5], (d, HDIM), jnp.float32) * 0.02, 'heavy_kv_w': jax.random.normal(ks[6], (HEADS, 2 * DIM_HEAD, d), jnp.float32) * 0.02, 'heavy_null_kv': jax.random.normal(ks[7], (2, HEADS, DIM_HEAD), jnp.float32), 'heavy_out_w': jax.random.normal(ks[8], (HDIM, d), jnp.float32) * 0.02, 'null_q_token': jax.random.normal(ks[9], (d,), jnp.float32)}
    _L0_attn_all = _L0_attn_setup()
    _L0_attn_in = {k: v for k, v in _L0_attn_all.items() if k in ('ln_gamma', 'ln_beta', 'light_qkv_w', 'light_out_w', 'q_route_tok', 'kv_route_tok', 'heavy_gamma', 'heavy_q_w', 'heavy_kv_w', 'heavy_null_kv', 'heavy_out_w', 'null_q_token')}
    del _L0_attn_all

    def _L0_ffn_setup():
        import jax, jax.numpy as jnp
        import numpy as np
        from jax import lax
        T, B, I, M, O = (64, 64, 256, 256, 256)

        def _xavier(key, shape):
            fan_out, fan_in = shape
            limit = float(np.sqrt(6.0 / (fan_in + fan_out)))
            return jax.random.uniform(key, shape, jnp.float32, -limit, limit)
        key = jax.random.key(seed)
        ks = jax.random.split(key, 9)
        x = jax.random.normal(ks[0], (T, B, I), jnp.float32)
        return {'x': x, 'wf': _xavier(ks[1], (M, I)), 'uf': _xavier(ks[2], (M, M)), 'bf': jnp.zeros((M,), jnp.float32), 'wi': _xavier(ks[3], (M, I)), 'ui': _xavier(ks[4], (M, M)), 'bi': jnp.zeros((M,), jnp.float32), 'wc': _xavier(ks[5], (M, I)), 'uc': _xavier(ks[6], (M, M)), 'bc': jnp.zeros((M,), jnp.float32), 'wo': _xavier(ks[7], (O, I)), 'uo': _xavier(ks[8], (O, M)), 'bo': jnp.zeros((O,), jnp.float32), 'in_c': jnp.zeros((M,), jnp.float32)}
    _L0_ffn_all = _L0_ffn_setup()
    _L0_ffn_in = {k: v for k, v in _L0_ffn_all.items() if k in ('wf', 'uf', 'bf', 'wi', 'ui', 'bi', 'wc', 'uc', 'bc', 'wo', 'uo', 'bo', 'in_c')}
    del _L0_ffn_all
    return {'x': x, 'L0_tok_weight': _L0_tok_in['weight'], 'L0_tok_bias': _L0_tok_in['bias'], 'L0_attn_ln_gamma': _L0_attn_in['ln_gamma'], 'L0_attn_ln_beta': _L0_attn_in['ln_beta'], 'L0_attn_light_qkv_w': _L0_attn_in['light_qkv_w'], 'L0_attn_light_out_w': _L0_attn_in['light_out_w'], 'L0_attn_q_route_tok': _L0_attn_in['q_route_tok'], 'L0_attn_kv_route_tok': _L0_attn_in['kv_route_tok'], 'L0_attn_heavy_gamma': _L0_attn_in['heavy_gamma'], 'L0_attn_heavy_q_w': _L0_attn_in['heavy_q_w'], 'L0_attn_heavy_kv_w': _L0_attn_in['heavy_kv_w'], 'L0_attn_heavy_null_kv': _L0_attn_in['heavy_null_kv'], 'L0_attn_heavy_out_w': _L0_attn_in['heavy_out_w'], 'L0_attn_null_q_token': _L0_attn_in['null_q_token'], 'L0_ffn_wf': _L0_ffn_in['wf'], 'L0_ffn_uf': _L0_ffn_in['uf'], 'L0_ffn_bf': _L0_ffn_in['bf'], 'L0_ffn_wi': _L0_ffn_in['wi'], 'L0_ffn_ui': _L0_ffn_in['ui'], 'L0_ffn_bi': _L0_ffn_in['bi'], 'L0_ffn_wc': _L0_ffn_in['wc'], 'L0_ffn_uc': _L0_ffn_in['uc'], 'L0_ffn_bc': _L0_ffn_in['bc'], 'L0_ffn_wo': _L0_ffn_in['wo'], 'L0_ffn_uo': _L0_ffn_in['uo'], 'L0_ffn_bo': _L0_ffn_in['bo'], 'L0_ffn_in_c': _L0_ffn_in['in_c']}

def reference(x, L0_tok_weight, L0_tok_bias, L0_attn_ln_gamma, L0_attn_ln_beta, L0_attn_light_qkv_w, L0_attn_light_out_w, L0_attn_q_route_tok, L0_attn_kv_route_tok, L0_attn_heavy_gamma, L0_attn_heavy_q_w, L0_attn_heavy_kv_w, L0_attn_heavy_null_kv, L0_attn_heavy_out_w, L0_attn_null_q_token, L0_ffn_wf, L0_ffn_uf, L0_ffn_bf, L0_ffn_wi, L0_ffn_ui, L0_ffn_bi, L0_ffn_wc, L0_ffn_uc, L0_ffn_bc, L0_ffn_wo, L0_ffn_uo, L0_ffn_bo, L0_ffn_in_c):
    import jax
    import jax.numpy as jnp

    def _L0_tok_ref(tokens, weight, bias):
        import jax, jax.numpy as jnp
        import numpy as np
        VOCAB = 50257
        NUM_DIM = 256
        BATCH = 4
        SEQ = 1024
        table = weight.T
        return jnp.take(table, tokens, axis=0) + bias

    def _L0_attn_ref(x, ln_gamma, ln_beta, light_qkv_w, light_out_w, q_route_tok, kv_route_tok, heavy_gamma, heavy_q_w, heavy_kv_w, heavy_null_kv, heavy_out_w, null_q_token):
        import jax, jax.numpy as jnp
        import numpy as np
        import math
        DIM = 256
        HEADS = 8
        DIM_HEAD = 64
        SEQ = 2048
        BATCH = 2
        WINDOW = 64
        NQ = 256
        NKV = 256
        FETCH_K_RATIO = 9.0 / 8.0
        N_ITERS = 20
        EPS = 0.03
        EPS_INIT = 4.0
        EPS_DECAY = 0.7
        HDIM = HEADS * DIM_HEAD

        def _layernorm(x, g, b, eps=1e-05):
            mu = x.mean(-1, keepdims=True)
            var = ((x - mu) ** 2).mean(-1, keepdims=True)
            return (x - mu) * jax.lax.rsqrt(var + eps) * g + b

        def _rmsnorm(x, gamma):
            normed = x / jnp.maximum(jnp.linalg.norm(x, axis=-1, keepdims=True), 1e-12)
            return normed * x.shape[-1] ** 0.5 * gamma

        def _rotate_half(x):
            x1, x2 = jnp.split(x, 2, axis=-1)
            return jnp.concatenate([-x2, x1], axis=-1)

        def _apply_rope(pos, t):
            return t * jnp.cos(pos) + _rotate_half(t) * jnp.sin(pos)

        def _coor_descent(s, k):
            logk = math.log(max(k, 1e-20))
            b = -s
            a = jnp.zeros_like(s[..., :1])
            cur = max(EPS_INIT, EPS)
            for _ in range(N_ITERS):
                sb = (s + b) / cur
                a = cur * (logk - jax.nn.logsumexp(sb, axis=-1, keepdims=True))
                b = -jax.nn.relu(s + a)
                cur = max(cur * EPS_DECAY, EPS)
            return jnp.exp((s + a + b) / cur)

        def _route(x, tok, num_tokens):
            s = jnp.einsum('bnd,d->bn', x, tok)
            eff_k = min(num_tokens * FETCH_K_RATIO, x.shape[1])
            scores = _coor_descent(s, eff_k)
            sel_scores, sel_idx = jax.lax.top_k(scores, num_tokens)
            sel_scores = sel_scores + jax.lax.stop_gradient(1.0 - sel_scores)
            routed = jnp.take_along_axis(x, sel_idx[..., None], axis=1)
            return (sel_idx, sel_scores, routed)

        def _light_attn(x, ln_g, ln_b, qkv_w, out_w):
            b, n, d = x.shape
            h, dh, w = (HEADS, DIM_HEAD, WINDOW)
            nw = n // w
            xn = _layernorm(x, ln_g, ln_b)
            q, k, v = jnp.split(xn @ qkv_w, 3, axis=-1)
            to_heads = lambda t: t.reshape(b, n, h, dh).transpose(0, 2, 1, 3)
            q, k, v = (to_heads(q), to_heads(k), to_heads(v))
            bq = q.reshape(b, h, nw, w, dh) * dh ** (-0.5)

            def look_around(t):
                tp = jnp.pad(t.reshape(b, h, nw, w, dh), ((0, 0), (0, 0), (1, 1), (0, 0), (0, 0)))
                return jnp.concatenate([tp[:, :, i:nw + i] for i in range(3)], axis=3)
            bk, bv = (look_around(k), look_around(v))
            sim = jnp.einsum('bhwid,bhwjd->bhwij', bq, bk)
            t_q = jnp.arange(n).reshape(nw, w)
            tpad = jnp.pad(t_q, ((1, 1), (0, 0)), constant_values=-1)
            t_k = jnp.concatenate([tpad[i:nw + i] for i in range(3)], axis=-1)
            valid = (t_k >= 0)[:, None, :] & (jnp.abs(t_q[:, :, None] - t_k[:, None, :]) <= w)
            sim = jnp.where(valid[None, None], sim, -jnp.finfo(sim.dtype).max)
            attn = jax.nn.softmax(sim, axis=-1)
            out = jnp.einsum('bhwij,bhwjd->bhwid', attn, bv)
            out = out.reshape(b, h, n, dh).transpose(0, 2, 1, 3).reshape(b, n, h * dh)
            return out @ out_w

        def _heavy_attn(xq, ctx, scores_kv, gamma, q_w, kv_w, null_kv, out_w, rope_q, rope_k):
            b = xq.shape[0]
            h, dh = (HEADS, DIM_HEAD)
            xq = _rmsnorm(xq, gamma)
            ctx = _rmsnorm(ctx, gamma)
            q = (xq @ q_w).reshape(b, -1, h, dh).transpose(0, 2, 1, 3)
            kv = jnp.einsum('hdi,bni->bhnd', kv_w, ctx)
            k, v = (kv[..., :dh], kv[..., dh:])
            v = v * scores_kv[:, None, :, None]
            q = _apply_rope(rope_q[:, None], q)
            k = _apply_rope(rope_k[:, None], k)
            nk = jnp.broadcast_to(null_kv[0][None, :, None, :], (b, h, 1, dh))
            nv = jnp.broadcast_to(null_kv[1][None, :, None, :], (b, h, 1, dh))
            k = jnp.concatenate([nk, k], axis=2)
            v = jnp.concatenate([nv, v], axis=2)
            sim = jnp.einsum('bhid,bhjd->bhij', q, k) * dh ** (-0.5)
            attn = jax.nn.softmax(sim, axis=-1)
            out = jnp.einsum('bhij,bhjd->bhid', attn, v)
            out = out.transpose(0, 2, 1, 3).reshape(b, -1, h * dh)
            return out @ out_w

        def _forward(x, ln_gamma, ln_beta, light_qkv_w, light_out_w, q_route_tok, kv_route_tok, heavy_gamma, heavy_q_w, heavy_kv_w, heavy_null_kv, heavy_out_w, null_q_token):
            b, n, d = x.shape
            light_out = _light_attn(x, ln_gamma, ln_beta, light_qkv_w, light_out_w)
            idx_q, sc_q, rt_q = _route(x, q_route_tok, NQ)
            idx_kv, sc_kv, rt_kv = _route(x, kv_route_tok, NKV)
            inv_freq = 1.0 / 10000.0 ** (jnp.arange(0, DIM_HEAD, 2, dtype=jnp.float32) / DIM_HEAD)
            freqs = jnp.arange(n, dtype=jnp.float32)[:, None] * inv_freq[None]
            pos = jnp.concatenate([freqs, freqs], axis=-1)
            rope_q = pos[idx_q]
            rope_k = pos[idx_kv]
            heavy_out = _heavy_attn(rt_q, rt_kv, sc_kv, heavy_gamma, heavy_q_w, heavy_kv_w, heavy_null_kv, heavy_out_w, rope_q, rope_k)
            heavy_out = heavy_out * sc_q[..., None]
            out = jnp.broadcast_to(null_q_token, x.shape)
            out = out.at[jnp.arange(b)[:, None], idx_q].set(heavy_out)
            return light_out + out
        return _forward(x, ln_gamma, ln_beta, light_qkv_w, light_out_w, q_route_tok, kv_route_tok, heavy_gamma, heavy_q_w, heavy_kv_w, heavy_null_kv, heavy_out_w, null_q_token)

    def _L0_ffn_ref(x, wf, uf, bf, wi, ui, bi, wc, uc, bc, wo, uo, bo, in_c):
        import jax, jax.numpy as jnp
        import numpy as np
        from jax import lax
        T, B, I, M, O = (64, 64, 256, 256, 256)

        def _xavier(key, shape):
            fan_out, fan_in = shape
            limit = float(np.sqrt(6.0 / (fan_in + fan_out)))
            return jax.random.uniform(key, shape, jnp.float32, -limit, limit)
        batch = x.shape[1]
        c0 = jnp.broadcast_to(in_c, (batch, in_c.shape[0]))

        def step(c, xt):
            ft = jax.nn.sigmoid(xt @ wf.T + c @ uf.T + bf)
            it = jax.nn.sigmoid(xt @ wi.T + c @ ui.T + bi)
            gt = jnp.tanh(xt @ wc.T + c @ uc.T + bc)
            c = ft * c + it * gt
            return (c, None)
        c_final, _ = lax.scan(step, c0, x)
        h = jnp.tanh(jnp.einsum('tbi,oi->tbo', x, wo) + c_final @ uo.T + bo)
        return h
    h = _L0_tok_ref(x, L0_tok_weight, L0_tok_bias)
    h = h + _L0_attn_ref(_layernorm(h, axis=-1), L0_attn_ln_gamma, L0_attn_ln_beta, L0_attn_light_qkv_w, L0_attn_light_out_w, L0_attn_q_route_tok, L0_attn_kv_route_tok, L0_attn_heavy_gamma, L0_attn_heavy_q_w, L0_attn_heavy_kv_w, L0_attn_heavy_null_kv, L0_attn_heavy_out_w, L0_attn_null_q_token)
    h = h + _L0_ffn_ref(_layernorm(h, axis=-1), L0_ffn_wf, L0_ffn_uf, L0_ffn_bf, L0_ffn_wi, L0_ffn_ui, L0_ffn_bi, L0_ffn_wc, L0_ffn_uc, L0_ffn_bc, L0_ffn_wo, L0_ffn_uo, L0_ffn_bo, L0_ffn_in_c)
    return h

_drawn_inputs = setup_inputs


def setup_inputs(seed=0):
    import zlib

    import numpy as np

    out = dict(_drawn_inputs(seed))
    spreads = {'L0_attn_ln_gamma': (1.0, 0.6),
     'L0_attn_ln_beta': (0.0, 0.282),
     'L0_attn_heavy_gamma': (1.0, 0.2),
     'L0_ffn_bf': (0.0, 0.778),
     'L0_ffn_bi': (0.0, 0.572),
     'L0_ffn_bc': (0.0, 0.1),
     'L0_ffn_bo': (0.0, 0.1),
     'L0_ffn_in_c': (0.0, 0.316)}
    factors = {'L0_attn_kv_route_tok': 25.056, 'L0_attn_heavy_q_w': 8.0, 'L0_attn_heavy_null_kv': 8.0}
    for name, (base, spread) in spreads.items():
        noise = np.random.default_rng([zlib.crc32(name.encode()), seed]).standard_normal(out[name].shape)
        drawn = base * np.exp(spread * noise) if base else spread * noise
        out[name] = jnp.asarray(drawn.astype(out[name].dtype))
    for name, factor in factors.items():
        out[name] = (out[name] * factor).astype(out[name].dtype)
    return out
```

```python
from contextlib import ExitStack
import math

import numpy as np
import concourse.bass as bass
from concourse import mybir

P = 128
B, N, D = 4, 2048, 256
T = N // P
NT = B * T
DC = D // P
H, DH = 8, 64
HD = H * DH
HC = HD // P
KSEL = 256
W = 64
ITERS, EPS0, EPS_END, DECAY = 20, 4.0, 0.03, 0.7
SEARCH_BITS = 30
LOGK = math.log(min(KSEL * 9.0 / 8.0, N))
LN_EPS = 1e-5
SCALE = DH ** -0.5
R = 2 * B
NEG = -3.0e38

F32 = mybir.dt.float32
BF16 = mybir.dt.bfloat16
I32 = mybir.dt.int32
U32 = mybir.dt.uint32
ALU = mybir.AluOpType
ACT = mybir.ActivationFunctionType
AX = mybir.AxisListType.X


def descent_eps():
    out, cur = [], max(EPS0, EPS_END)
    for _ in range(ITERS):
        out.append(cur)
        cur = max(cur * DECAY, EPS_END)
    return out, cur


def past(v):
    return not (isinstance(v, int) and v < 1)


def lm_tower(nc, ap, out):
    with ExitStack() as top:
        def sb(name, shape, dt=F32, ctx=top):
            return ctx.enter_context(nc.sbuf_tensor(name, shape, dt))

        def dram(name, shape, dt=F32):
            return nc.dram_tensor(name, shape, dt, kind="Internal").ap()

        norm_rows = dram("norm_rows", [B * N, D])
        heavy_rows = dram("heavy_rows", [B * KSEL + 1, D])
        list_idx = dram("list_idx", [R * KSEL, 1], I32)
        list_gain = dram("list_gain", [R * KSEL, 1])

        hres = sb("hres", [P, NT, D])
        xn = sb("xn", [P, NT + 2, D])
        ident = sb("ident", [P, P])
        ident_bf = sb("ident_bf", [P, P], BF16)
        ones = sb("ones", [P, P])
        score_in = sb("score_in", [P, R, T])
        pos = sb("pos", [P, B, T], I32)
        sel_idx = sb("sel_idx", [P, R, KSEL // P], I32)
        sel_gain = sb("sel_gain", [P, R, KSEL // P])

        with ExitStack() as ctx:
            def sem(name):
                return ctx.enter_context(nc.semaphore(name))
            ids = sb("ids", [P, NT], I32, ctx)
            idc = sb("idc", [P, 4], I32, ctx)
            tokb = sb("tokb", [P, D], F32, ctx)
            rtok = sb("rtok", [P, 2, D], F32, ctx)
            epsc = sb("epsc", [P, 1], F32, ctx)
            raw = sb("raw", [P, 4, D], F32, ctx)
            hn = sb("hn", [P, 2, 4, D], F32, ctx)
            st = sb("st", [P, 4, 6], F32, ctx)
            mv = sb("mv", [P, 4, 2], F32, ctx)
            sd = sb("sd", [P, 4], F32, ctx)
            rstd = sb("rstd", [P, 4], F32, ctx)
            junk = sb("junk", [P, 8, D], F32, ctx)
            srow = sb("srow", [P, 2, 4], F32, ctx)
            loaded = sem("e_loaded")
            id_copied = sem("e_id_copied")
            id_settled = sem("e_id_settled")
            gathered = [sem(f"e_gathered{k}") for k in range(4)]
            normed = sem("e_normed")
            eps_set = sem("e_eps_set")
            var_ready = sem("e_var_ready")
            sd_ready = sem("e_sd_ready")
            hn_saved = sem("e_hn_saved")
            step = sem("e_step")
            STEPS = 15
            with nc.Block() as block:
                @block.sync
                def _(sp):
                    for dst, src in ((ids[:], ap["ids"]), (tokb[:], ap["tok_bias"]), (rtok[:], ap["route_tok"]),
                                     (ident[:], ap["ident"]), (ident_bf[:], ap["ident_bf"])):
                        sp.dma_start(dst, src).then_inc(loaded, 16)
                    with sp.Fori(0, NT // 4) as it:
                        sp.wait_ge(normed, it * 4 + 4)
                        sp.dma_start(norm_rows.rearrange("(g p) d -> p g d", p=P)[:, bass.ds(it * 4, 4), :],
                                     hn[:, 0, :, :]).then_inc(hn_saved, 16)
                    sp.wait_ge(hn_saved, 16 * (NT // 4))

                @block.gpsimd
                def _(pool):
                    pool.wait_ge(loaded, 16 * 5)
                    with pool.Fori(0, NT // 4) as it:
                        nc.gpsimd.tensor_copy(idc[:], ids[:, bass.ds(it * 4, 4)]).then_inc(id_copied, 1)
                        pool.wait_ge(id_copied, it + 1)
                        pool.sem_inc(id_settled, 1)
                        for k in range(4):
                            pool.indirect_dma_start(raw[:, k, :], None, ap["table"],
                                                    bass.IndirectOffsetOnAxis(ap=idc[:, k:k + 1], axis=0)
                                                    ).then_inc(gathered[k], 16)
                        pool.wait_ge(normed, it * 4 + 4)

                @block.scalar
                def _(act):
                    act.wait_ge(eps_set, 1)
                    with act.Fori(0, NT // 4) as it:
                        for ln in range(2):
                            act.wait_ge(var_ready, it * 2 + (ln + 1))
                            nc.scalar.activation(sd[:], mv[:, :, 1], ACT.Sqrt, bias=epsc[:, 0:1]).then_inc(sd_ready, 1)

                @block.vector
                def _(dve):
                    nc.vector.memset(epsc[:], LN_EPS).then_inc(eps_set, 1)
                    nc.vector.memset(ones[:], 1.0)
                    nc.vector.memset(xn[:, NT:NT + 2, :], 0.0)
                    dve.wait_ge(loaded, 16 * 5)
                    with dve.Fori(0, NT // 4) as it:
                        base = it * STEPS
                        for k in range(4):
                            dve.wait_ge(gathered[k], it * 16 + 16)
                            nc.vector.tensor_tensor(hres[:, bass.ds(it * 4 + k, 1), :].rearrange("p a d -> p (a d)"),
                                                    raw[:, k, :], tokb[:], ALU.add)
                            i = nc.vector.tensor_tensor(raw[:, k, :], raw[:, k, :], tokb[:], ALU.add)
                            i.then_inc(step, 1)
                        for k in range(4):
                            dve.wait_ge(step, base + (k + 1))
                            nc.vector.bn_stats(st[:, k, :], raw[:, k, :]).then_inc(step, 1)
                        dve.wait_ge(step, base + 8)
                        nc.vector.tensor_copy(rstd[:, 0:1], st[:, 0, 0:1])
                        for k in range(4):
                            i = nc.vector.bn_aggr(mv[:, k, :], st[:, k, :])
                        i.then_inc(var_ready, 1)
                        dve.wait_ge(sd_ready, it * 2 + 1)
                        nc.vector.reciprocal(rstd[:], sd[:]).then_inc(step, 1)
                        dve.wait_ge(step, base + 9)
                        for k in range(4):
                            i = nc.vector.tensor_scalar(hn[:, 0, k, :], raw[:, k, :], mv[:, k, 0:1], rstd[:, k:k + 1],
                                                        ALU.subtract, ALU.mult)
                            i.then_inc(normed, 1)
                        dve.wait_ge(normed, it * 4 + 4)
                        for k in range(4):
                            nc.vector.bn_stats(st[:, k, :], hn[:, 0, k, :]).then_inc(step, 1)
                        dve.wait_ge(step, base + 13)
                        nc.vector.tensor_copy(rstd[:, 0:1], st[:, 0, 0:1])
                        for k in range(4):
                            i = nc.vector.bn_aggr(mv[:, k, :], st[:, k, :])
                        i.then_inc(var_ready, 1)
                        for k in range(4):
                            for r in range(2):
                                i = nc.vector.tensor_tensor_reduce(junk[:, 2 * k + r, :], hn[:, 0, k, :], rtok[:, r, :], 1.0, 0.0,
                                                                   ALU.mult, ALU.add, srow[:, r, k:k + 1])
                        i.then_inc(step, 1)
                        dve.wait_ge(sd_ready, it * 2 + 2)
                        nc.vector.reciprocal(rstd[:], sd[:]).then_inc(step, 1)
                        dve.wait_ge(step, base + 15)
                        for r in range(2):
                            nc.vector.tensor_scalar(
                                score_in[:].rearrange("p r t -> p (r t)")[:, bass.ds(it * 4 + r * NT, 4)], srow[:, r, :],
                                1.0, None, ALU.mult)
                        for k in range(4):
                            nc.vector.tensor_scalar(xn[:, bass.ds(it * 4 + k, 1), :].rearrange("p a d -> p (a d)"),
                                                    hn[:, 0, k, :], mv[:, k, 0:1], rstd[:, k:k + 1],
                                                    ALU.subtract, ALU.mult)
                        dve.wait_ge(hn_saved, it * 16 + 16)

        with ExitStack() as ctx:
            def sem(name):
                return ctx.enter_context(nc.semaphore(name))

            def rt(name, shape, dt=F32):
                return sb(name, shape, dt, ctx)
            C = R * T
            eps_list, eps_last = descent_eps()
            dtab = rt("dtab", [P, 3, ITERS])
            bits = rt("bits", [P, SEARCH_BITS], U32)
            consts = rt("consts", [P, 2, C])
            tri = rt("tri", [P, P])
            iota16 = rt("iota16", [P, 16])
            tokid = rt("tokid", [P, C])
            smax = rt("smax", [P, R])
            smax1 = rt("smax1", [P, R])
            shift = rt("shift", [P, R])
            mk = rt("mk", [P, R])
            negu = rt("negu", [P, R, T])
            work = rt("work", [P, R, T])
            expo = rt("expo", [P, R, T])
            part = rt("part", [P, R])
            lse = rt("lse", [P, R])
            nega = rt("nega", [P, R])
            score = rt("score", [P, R, T])
            thr = rt("thr", [P, R])
            cand = rt("cand", [P, R])
            kept = rt("kept", [P, R])
            eq = rt("eq", [P, R, T])
            gt = rt("gt", [P, R, T])
            incl = rt("incl", [P, C])
            rank = rt("rank", [P, C])
            need = rt("need", [P, R])
            sel = rt("sel", [P, R, T])
            gain = rt("gain", [P, C])
            ri = rt("ri", [P, 3, C], I32)
            rf = rt("rf", [P, 2, C])
            hi1 = rt("hi1", [P, C, 16])
            lo1 = rt("lo1", [P, C, 32])
            lists_f = rt("lists_f", [16, R, 32])
            lists_i = rt("lists_i", [16, R, 16], I32)
            ps_tot = ctx.enter_context(nc.psum_tensor("ps_tot", [P, 512], F32))
            ps_pre = ctx.enter_context(nc.psum_tensor("ps_pre", [P, 512], F32))
            ps_lst = ctx.enter_context(nc.psum_tensor("ps_lst", [P, 512], F32))
            loaded = sem("r_loaded")
            part_max = sem("r_part_max")
            all_max = sem("r_all_max")
            v = sem("r_v")
            exp_ready = sem("r_exp_ready")
            sum_in = sem("r_sum_in")
            sum_done = sem("r_sum_done")
            ln_done = sem("r_ln_done")
            diff_ready = sem("r_diff_ready")
            score_args = sem("r_score_args")
            score_done = sem("r_score_done")
            cnt_in = sem("r_cnt_in")
            thr_ready = sem("r_thr_ready")
            cnt_done = sem("r_cnt_done")
            mask_in = sem("r_mask_in")
            pref_done = sem("r_pref_done")
            onehot = sem("r_onehot")
            list_done = sem("r_list_done")
            list_out = sem("r_list_out")
            list_saved = sem("r_list_saved")
            list_back = sem("r_list_back")
            null_saved = sem("r_null_saved")
            bc = lambda a: a.rearrange("p (r o) -> p r o", o=1).broadcast_to([P, R, T])
            with nc.Block() as block:
                @block.sync
                def _(sp):
                    for dst, src in ((dtab[:], ap["descent"]), (bits[:], ap["bits"]), (consts[:], ap["row_consts"]),
                                     (tri[:], ap["tri"]), (iota16[:], ap["iota16"]), (tokid[:], ap["tokid"])):
                        sp.dma_start(dst, src).then_inc(loaded, 16)
                    sp.dma_start(heavy_rows[B * KSEL:B * KSEL + 1, :], ap["null_q"]).then_inc(null_saved, 16)
                    sp.wait_ge(list_out, 2)
                    sp.dma_start(list_idx.rearrange("(r h l) o -> h r (l o)", r=R, h=16), lists_i[:]).then_inc(list_saved, 16)
                    sp.dma_start(list_gain.rearrange("(r h l) o -> h r (l o)", r=R, h=16),
                                 lists_f[:, :, 16:32]).then_inc(list_saved, 16)
                    sp.wait_ge(list_saved, 32)
                    with nc.allow_non_contiguous_dma(reason="2048 list entries, one per partition"):
                        for h in range(KSEL // P):
                            for src, dst in ((list_idx, sel_idx), (list_gain, sel_gain)):
                                sp.dma_start(dst[:, :, h], src.rearrange("(r h p) o -> h p (r o)", r=R, p=P)[h]
                                             ).then_inc(list_back, 16)
                    sp.wait_ge(list_back, 64)
                    sp.wait_ge(null_saved, 16)

                @block.gpsimd
                def _(pool):
                    pool.wait_ge(part_max, 1)
                    nc.gpsimd.partition_all_reduce(smax[:], smax1[:], P, bass.bass_isa.ReduceOp.max).then_inc(all_max, 1)

                @block.scalar
                def _(act):
                    act.wait_ge(loaded, 96)
                    with act.Fori(0, ITERS) as i:
                        act.wait_ge(diff_ready, i + 1)
                        nc.scalar.activation(expo[:], work[:], ACT.Exp, scale=dtab[:, 0, bass.ds(i, 1)]).then_inc(exp_ready, 1)
                        act.wait_ge(sum_done, i + 1)
                        nc.scalar.activation(lse[:], ps_tot[:, 0:R], ACT.Ln).then_inc(ln_done, 1)
                    act.wait_ge(score_args, 1)
                    nc.scalar.activation(score[:], work[:], ACT.Exp, scale=1.0 / eps_last).then_inc(score_done, 1)

                @block.tensor
                def _(pe):
                    with pe.Fori(0, ITERS) as i:
                        pe.wait_ge(sum_in, i + 1)
                        nc.tensor.matmul(ps_tot[:, 0:R], ones[:], part[:], start=True, stop=True).then_inc(sum_done, 1)
                    with pe.Fori(0, SEARCH_BITS) as i:
                        pe.wait_ge(cnt_in, i + 1)
                        nc.tensor.matmul(ps_tot[:, 0:R], ones[:], part[:], start=True, stop=True).then_inc(cnt_done, 1)
                    pe.wait_ge(cnt_in, SEARCH_BITS + 1)
                    nc.tensor.matmul(ps_tot[:, 0:R], ones[:], part[:], start=True, stop=True).then_inc(cnt_done, 1)
                    for j, m in enumerate((eq, sel)):
                        pe.wait_ge(mask_in, j + 1)
                        flat = m[:].rearrange("p r t -> p (r t)")
                        nc.tensor.matmul(ps_pre[:, 0:C], tri[:], flat, start=True, stop=True)
                        nc.tensor.matmul(ps_pre[:, C:2 * C], ones[:], flat, start=True, stop=True).then_inc(pref_done, 1)
                    pe.wait_ge(onehot, 1)
                    for r in range(R):
                        for t in range(T):
                            i = nc.tensor.matmul(ps_lst[0:16, r * 32:r * 32 + 32], hi1[:, r * T + t, :], lo1[:, r * T + t, :],
                                                 start=(t == 0), stop=(t == T - 1))
                    i.then_inc(list_done, 1)

                @block.vector
                def _(dve):
                    cnt = [0]

                    def link(i):
                        cnt[0] += 1
                        i.then_inc(v, 1)
                        dve.wait_ge(v, cnt[0])

                    dve.wait_ge(loaded, 96)
                    nc.vector.tensor_reduce(smax1[:], score_in[:], AX, ALU.max).then_inc(part_max, 1)
                    nc.vector.memset(mk[:], 0.0)
                    nc.vector.memset(work[:], 0.0).then_inc(diff_ready, 1)
                    dve.wait_ge(diff_ready, 1)
                    dve.wait_ge(all_max, 1)
                    DS = 7
                    with dve.Fori(0, ITERS) as i:
                        base = i * DS
                        nc.vector.tensor_scalar(shift[:], mk[:], dtab[:, 2, bass.ds(i, 1)], None, ALU.add).then_inc(v, 1)
                        dve.wait_ge(exp_ready, i + 1)
                        nc.vector.tensor_reduce(part[:], expo[:], AX, ALU.add).then_inc(sum_in, 1)
                        dve.wait_ge(ln_done, i + 1)
                        dve.wait_ge(v, base + 1)
                        nc.vector.scalar_tensor_tensor(out=nega[:], in0=lse[:], scalar=dtab[:, 1, bass.ds(i, 1)], in1=shift[:],
                                                       op0=ALU.mult, op1=ALU.add).then_inc(v, 1)
                        dve.wait_ge(v, base + 2)
                        nc.vector.tensor_tensor(work[:], score_in[:], bc(nega[:]), ALU.subtract).then_inc(v, 1)
                        nc.vector.tensor_tensor(mk[:], smax[:], nega[:], ALU.min).then_inc(v, 1)
                        dve.wait_ge(v, base + 4)
                        nc.vector.scalar_tensor_tensor(out=negu[:], in0=work[:], scalar=0.0, in1=score_in[:],
                                                       op0=ALU.max, op1=ALU.subtract).then_inc(v, 1)
                        nc.vector.tensor_scalar(gt[:], work[:], 0.0, None, ALU.min).then_inc(v, 1)
                        dve.wait_ge(v, base + 6)
                        nc.vector.tensor_tensor(work[:], negu[:], bc(mk[:]), ALU.add).then_inc(v, 1)
                        dve.wait_ge(v, base + 7)
                        nc.vector.tensor_copy(kept[:, 0:1], mk[:, 0:1]).then_inc(diff_ready, 1)
                    cnt[0] = ITERS * DS
                    link(nc.vector.tensor_copy(work[:], gt[:]))
                    nc.vector.memset(thr[:], 0.0).then_inc(score_args, 1)
                    dve.wait_ge(score_done, 1)
                    BS = 3
                    base0 = cnt[0]
                    with dve.Fori(0, SEARCH_BITS) as i:
                        base = i * BS + base0
                        nc.vector.tensor_tensor(cand[:].bitcast(U32), thr[:].bitcast(U32),
                                                bits[:, bass.ds(i, 1)].broadcast_to([P, R]), ALU.bitwise_or).then_inc(v, 1)
                        dve.wait_ge(v, base + 1)
                        nc.vector.tensor_tensor(eq[:], score[:], bc(cand[:]), ALU.is_ge).then_inc(v, 1)
                        dve.wait_ge(v, base + 2)
                        nc.vector.tensor_reduce(part[:], eq[:], AX, ALU.add).then_inc(cnt_in, 1)
                        dve.wait_ge(cnt_done, i + 1)
                        nc.vector.scalar_tensor_tensor(out=kept[:], in0=ps_tot[:, 0:R], scalar=float(KSEL), in1=cand[:],
                                                       op0=ALU.is_ge, op1=ALU.mult).then_inc(v, 1)
                        dve.wait_ge(v, base + 3)
                        nc.vector.tensor_tensor(thr[:], thr[:], kept[:], ALU.max).then_inc(thr_ready, 1)
                        dve.wait_ge(thr_ready, i + 1)
                    cnt[0] = base0 + BS * SEARCH_BITS
                    nc.vector.tensor_tensor(eq[:], score[:], bc(thr[:]), ALU.is_equal).then_inc(mask_in, 1)
                    link(nc.vector.tensor_tensor(gt[:], score[:], bc(thr[:]), ALU.is_gt))
                    nc.vector.tensor_reduce(part[:], gt[:], AX, ALU.add).then_inc(cnt_in, 1)
                    dve.wait_ge(cnt_done, SEARCH_BITS + 1)
                    link(nc.vector.tensor_scalar(need[:], ps_tot[:, 0:R], -1.0, float(KSEL), ALU.mult, ALU.add))

                    def prefix(mask, j):
                        flat = mask[:].rearrange("p r t -> p (r t)")
                        dve.wait_ge(pref_done, j + 1)
                        link(nc.vector.tensor_tensor_scan(incl[:], consts[:, 0, :], ps_pre[:, C:2 * C], 0.0, ALU.mult, ALU.add))
                        link(nc.vector.tensor_tensor(rank[:], ps_pre[:, 0:C], incl[:], ALU.add))
                        link(nc.vector.tensor_tensor(rank[:], rank[:], ps_pre[:, C:2 * C], ALU.subtract))

                    prefix(eq, 0)
                    rk = rank[:].rearrange("p (r t) -> p r t", r=R)
                    link(nc.vector.tensor_tensor(sel[:], rk, bc(need[:]), ALU.is_lt))
                    link(nc.vector.tensor_tensor(sel[:], sel[:], eq[:], ALU.mult))
                    nc.vector.tensor_tensor(sel[:], sel[:], gt[:], ALU.add).then_inc(mask_in, 1)
                    flat = score[:].rearrange("p r t -> p (r t)")
                    link(nc.vector.tensor_scalar(gain[:], flat, -1.0, 1.0, ALU.mult, ALU.add))
                    link(nc.vector.tensor_tensor(gain[:], gain[:], flat, ALU.add))
                    prefix(sel, 1)
                    selq = sel[:, 0:B, :].rearrange("p r t -> p (r t)")
                    CQ = B * T
                    link(nc.vector.tensor_tensor(rf[:, 0, 0:CQ], rank[:, 0:CQ], consts[:, 1, 0:CQ], ALU.add))
                    link(nc.vector.tensor_tensor(rf[:, 0, 0:CQ], rf[:, 0, 0:CQ], selq, ALU.mult))
                    link(nc.vector.tensor_scalar(pos[:].rearrange("p b t -> p (b t)"), rf[:, 0, 0:CQ], float(B * KSEL), None,
                                                 ALU.add))
                    sflat = sel[:].rearrange("p r t -> p (r t)")
                    link(nc.vector.tensor_scalar(incl[:], sflat, -4096.0, 4096.0, ALU.mult, ALU.add))
                    link(nc.vector.tensor_tensor(rank[:], rank[:], incl[:], ALU.add))
                    link(nc.vector.tensor_copy(ri[:, 0, :], rank[:]))
                    link(nc.vector.tensor_scalar(ri[:, 1, :], ri[:, 0, :], 4, None, ALU.logical_shift_right))
                    link(nc.vector.tensor_scalar(ri[:, 2, :], ri[:, 0, :], 15, None, ALU.bitwise_and))
                    link(nc.vector.tensor_copy(rf[:], ri[:, 1:3, :]))
                    io = iota16[:].rearrange("p (o s) -> p o s", o=1).broadcast_to([P, C, 16])
                    wide = lambda a: a.rearrange("p (c o) -> p c o", o=1).broadcast_to([P, C, 16])
                    link(nc.vector.tensor_tensor(hi1[:], io, wide(rf[:, 0, :]), ALU.is_equal))
                    link(nc.vector.tensor_tensor(lo1[:, :, 0:16], io, wide(rf[:, 1, :]), ALU.is_equal))
                    link(nc.vector.tensor_tensor(lo1[:, :, 16:32], lo1[:, :, 0:16], wide(gain[:]), ALU.mult))
                    nc.vector.tensor_tensor(lo1[:, :, 0:16], lo1[:, :, 0:16], wide(tokid[:]), ALU.mult).then_inc(onehot, 1)
                    dve.wait_ge(list_done, 1)
                    src = ps_lst[0:16, 0:R * 32].rearrange("p (r l) -> p r l", r=R)
                    nc.vector.tensor_copy(lists_f[:], src).then_inc(list_out, 1)
                    nc.vector.tensor_copy(lists_i[:], src[:, :, 0:16]).then_inc(list_out, 1)

        def light(ctx):
            def sem(name):
                return ctx.enter_context(nc.semaphore(name))

            def st(name, shape, dt=F32):
                return sb(name, shape, dt, ctx)
            wqkv = st("wqkv", [P, DC, 3 * HD])
            wo = st("wo", [P, HC, D])
            gb = st("gb", [P, 2, DC])
            masks = st("masks", [P, 8, 2 * P], BF16)
            stage = st("stage", [P, 2, D])
            xT = st("xT", [P, DC, P])
            qT = st("qT", [P, HC, 4, P])
            kT = st("kT", [P, HC, 4 * P])
            vown = st("vown", [P, 4, H, DH + 1])
            vnb = st("vnb", [P, 4, H, DH + 1])
            mx = st("mx", [P, 2, 4])
            nmx = st("nmx", [P, 2, 4])
            prob = st("prob", [P, 2, 4, 2 * P])
            probT = st("probT", [P, 2, 2, 4, P])
            rden = st("rden", [P, 2, 4])
            o = st("o", [P, H, DH])
            oT = st("oT", [P, HC, P])
            ps_sim = ctx.enter_context(nc.psum_tensor("ps_sim", [P, 2, 4, 2 * P], F32))
            ps_pT = ctx.enter_context(nc.psum_tensor("ps_pT", [P, 2, 4, P], F32))
            ps_a = ctx.enter_context(nc.psum_tensor("ps_a", [P, 512], F32))
            ps_b = ctx.enter_context(nc.psum_tensor("ps_b", [P, 512], F32))
            loaded = sem("l_loaded")
            zeroed = sem("l_zeroed")
            staged = sem("l_staged")
            xT_done, xT_ev = sem("l_xT_done"), sem("l_xT_ev")
            q_done, q_ev = sem("l_q_done"), sem("l_q_ev")
            k_done, k_ev = sem("l_k_done"), sem("l_k_ev")
            v_done, v_ev = sem("l_v_done"), sem("l_v_ev")
            sim_done, max_done, exp_done = sem("l_sim_done"), sem("l_max_done"), sem("l_exp_done")
            nmx_in = sem("l_nmx_in")
            ptA_done, ptB_done, ptA_ev, ptB_ev = sem("l_ptA_done"), sem("l_ptB_done"), sem("l_ptA_ev"), sem("l_ptB_ev")
            pv_done, pv_ev, rden_done = sem("l_pv_done"), sem("l_pv_ev"), sem("l_rden_done")
            oT_done, oT_ev = sem("l_oT_done"), sem("l_oT_ev")
            proj_done, proj_ev = sem("l_proj_done"), sem("l_proj_ev")

            def head(u, h):
                return 4 * u + 2 * (h % 2) + h // 2

            def pe_xT(pe, n, slot):
                pe.wait_ge(staged, n)
                for c in range(DC):
                    i = nc.tensor.transpose(ps_a[:, c * P:(c + 1) * P], stage[:, slot % 2, c * P:(c + 1) * P], ident[:])
                i.then_inc(xT_done, 1)

            def pool_stage(pool, g, slot):
                if past(g - 1):
                    pool.wait_ge(xT_done, g - 1)
                nc.gpsimd.tensor_copy(stage[:, slot % 2, :], xn[:, bass.ds(g, 1), :].rearrange("p a d -> p (a d)")
                                      ).then_inc(staged, 1)

            def pe_qk(pe, ps, col, done):
                for m in range(HC):
                    for c in range(DC):
                        i = nc.tensor.matmul(ps[:, m * P:(m + 1) * P], wqkv[:, c, col + m * P:col + (m + 1) * P], xT[:, c, :],
                                             start=(c == 0), stop=(c == DC - 1))
                i.then_inc(done, 1)

            def pe_v(pe):
                for c in range(DC):
                    i = nc.tensor.matmul(ps_b[:], xT[:, c, :], wqkv[:, c, 2 * HD:3 * HD], start=(c == 0), stop=(c == DC - 1))
                i.then_inc(v_done, 1)

            def pe_sim(pe, k, u, mask):
                nxt, prv = (k + 1) % 4, (k + 3) % 4
                for e in range(2):
                    bank = ps_sim[:, u, 2 * e:2 * e + 2, :]
                    nc.tensor.matmul(bank, ident_bf[:], mask.rearrange("p (o j) -> p o j", o=1).broadcast_to([P, 2, 2 * P]),
                                     start=True, stop=False)
                for l in range(2):
                    for src, n, at in ((k * P, P, 0), (nxt * P, DH, P), (prv * P + DH, DH, P + DH)):
                        for e in range(2):
                            c = 2 * u + l
                            i = nc.tensor.matmul(ps_sim[:, u, 2 * e + l, at:at + n], qT[64 * e:64 * e + 64, c, k, :],
                                                 kT[64 * e:64 * e + 64, c, src:src + n], start=False,
                                                 stop=(l == 1 and at == P + DH))
                i.then_inc(sim_done, 1)

            def pe_pT(pe, u):
                for blk, done in ((0, ptA_done), (1, ptB_done)):
                    for h in range(4):
                        i = nc.tensor.transpose(ps_pT[:, blk, h, :], prob[:, u, h, blk * P:(blk + 1) * P], ident[:])
                    i.then_inc(done, 1)

            def pe_pv(pe, ps, k, u):
                for h in range(4):
                    for blk, vals in ((0, vown), (1, vnb)):
                        i = nc.tensor.matmul(ps[:, (head(u, h) - 4 * u) * (DH + 1):(head(u, h) - 4 * u + 1) * (DH + 1)],
                                             probT[:, u, blk, h, :], vals[:, k, head(u, h), :],
                                             start=(blk == 0), stop=(blk == 1))
                i.then_inc(pv_done, 1)

            def pe_oT(pe):
                flat = o[:].rearrange("p h d -> p (h d)")
                for c in range(HC):
                    i = nc.tensor.transpose(ps_b[:, c * P:(c + 1) * P], flat[:, c * P:(c + 1) * P], ident[:])
                i.then_inc(oT_done, 1)

            def pe_proj(pe):
                for c in range(HC):
                    i = nc.tensor.matmul(ps_b[:, 0:D], oT[:, c, :], wo[:, c, :], start=(c == 0), stop=(c == HC - 1))
                i.then_inc(proj_done, 1)

            def pe_back(pe, g):
                pe.wait_ge(exp_done, 2 * g)
                pe_pT(pe, 1)

            def pe_tile(pe, g, k, mask):
                pe.wait_ge(k_ev, g + 2)
                pe_sim(pe, k, 0, mask)
                if past(g):
                    pe_back(pe, g)
                    pe.wait_ge(pv_ev, 2 * g - 1)
                pe_xT(pe, g + 3, k)
                pe.wait_ge(v_ev, g + 2)
                if past(g):
                    pe.wait_ge(ptA_ev, 2 * g)
                    pe.wait_ge(ptB_ev, 2 * g)
                    pe_pv(pe, ps_b, (k + 3) % 4, 1)
                pe.wait_ge(xT_ev, g + 3)
                pe_qk(pe, ps_a, 0, q_done)
                pe_sim(pe, k, 1, mask)
                if past(g):
                    pe.wait_ge(pv_ev, 2 * g)
                    pe_oT(pe)
                pe.wait_ge(exp_done, 2 * g + 1)
                pe_pT(pe, 0)
                pe.wait_ge(q_ev, g + 3)
                pe_qk(pe, ps_a, HD, k_done)
                if past(g):
                    pe.wait_ge(oT_ev, g)
                    pe_proj(pe)
                pe.wait_ge(ptA_ev, 2 * g + 1)
                pe.wait_ge(ptB_ev, 2 * g + 1)
                pe.wait_ge(k_ev, g + 3)
                pe_pv(pe, ps_a, k, 0)
                if past(g):
                    pe.wait_ge(proj_ev, g)
                pe_v(pe)

            def act_xT(act, n):
                act.wait_ge(xT_done, n)
                for c in range(DC):
                    i = nc.scalar.activation(xT[:, c, :], ps_a[:, c * P:(c + 1) * P], ACT.Identity,
                                             bias=gb[:, 1, c:c + 1], scale=gb[:, 0, c:c + 1])
                i.then_inc(xT_ev, 1)

            def act_q(act, n, slot):
                act.wait_ge(q_done, n)
                nc.scalar.copy(qT[:, :, slot, :], ps_a[:].rearrange("p (m j) -> p m j", m=HC)).then_inc(q_ev, 1)

            def act_k(act, n, slot):
                act.wait_ge(k_done, n)
                nc.scalar.copy(kT[:, :, slot * P:(slot + 1) * P], ps_a[:].rearrange("p (m j) -> p m j", m=HC)).then_inc(k_ev, 1)

            def act_exp(act, n, u):
                act.wait_ge(max_done, n)
                for h in range(4):
                    i = nc.scalar.activation(prob[:, u, h, :], ps_sim[:, u, h, :], ACT.Exp, bias=nmx[:, u, h:h + 1], scale=SCALE)
                i.then_inc(exp_done, 1)

            def act_ptB(act, n, u):
                act.wait_ge(ptB_done, n)
                nc.scalar.copy(probT[:, u, 1, :, :], ps_pT[:, 1, :, :]).then_inc(ptB_ev, 1)

            def act_tile(act, g, k):
                if past(g):
                    act_ptB(act, 2 * g, 1)
                act_xT(act, g + 3)
                act_exp(act, 2 * g + 1, 0)
                act_q(act, g + 3, (k + 2) % 4)
                act_exp(act, 2 * g + 2, 1)
                act_ptB(act, 2 * g + 1, 0)
                act_k(act, g + 3, (k + 2) % 4)

            def dve_max(dve, n, u):
                dve.wait_ge(sim_done, n)
                nc.vector.tensor_reduce(mx[:, u, :], ps_sim[:, u, :, :], AX, ALU.max).then_inc(nmx_in, 1)
                dve.wait_ge(nmx_in, n)
                nc.vector.tensor_scalar(nmx[:, u, :], mx[:, u, :], -SCALE, None, ALU.mult).then_inc(max_done, 1)

            def dve_ptA(dve, n, u):
                dve.wait_ge(ptA_done, n)
                nc.vector.tensor_copy(probT[:, u, 0, :, :], ps_pT[:, 0, :, :]).then_inc(ptA_ev, 1)

            def dve_pv(dve, ps, n, u):
                dve.wait_ge(pv_done, n)
                view = ps[:, 0:4 * (DH + 1)].rearrange("p (h d) -> p h d", h=4)
                nc.vector.reciprocal(rden[:, u, :], view[:, :, DH]).then_inc(rden_done, 1)
                dve.wait_ge(rden_done, n)
                nc.vector.tensor_tensor(o[:, 4 * u:4 * u + 4, :], view[:, :, 0:DH],
                                        rden[:, u, :].rearrange("p (h o) -> p h o", o=1).broadcast_to([P, 4, DH]),
                                        ALU.mult).then_inc(pv_ev, 1)

            def dve_v(dve, n, slot):
                dve.wait_ge(v_done, n)
                src = ps_b[:].rearrange("p (h d) -> p h d", h=H)
                nc.vector.tensor_copy(vnb[0:DH, (slot + 3) % 4, :, 0:DH], src[0:DH])
                nc.vector.tensor_copy(vnb[DH:P, (slot + 1) % 4, :, 0:DH], src[DH:P])
                nc.vector.tensor_copy(vown[:, slot, :, 0:DH], src).then_inc(v_ev, 1)

            def dve_oT(dve, n):
                dve.wait_ge(oT_done, n)
                nc.vector.tensor_copy(oT[:].rearrange("p c j -> p (c j)"), ps_b[:]).then_inc(oT_ev, 1)

            def dve_proj(dve, n, g):
                dve.wait_ge(proj_done, n)
                row = hres[:, bass.ds(g, 1), :].rearrange("p a d -> p (a d)")
                nc.vector.tensor_tensor(row, ps_b[:, 0:D], row, ALU.add).then_inc(proj_ev, 1)

            def dve_tile(dve, g, k):
                dve_max(dve, 2 * g + 1, 0)
                if past(g):
                    dve_ptA(dve, 2 * g, 1)
                    dve_pv(dve, ps_b, 2 * g, 1)
                dve_max(dve, 2 * g + 2, 1)
                if past(g):
                    dve_oT(dve, g)
                dve_ptA(dve, 2 * g + 1, 0)
                if past(g):
                    dve_proj(dve, g, g - 1)
                dve_pv(dve, ps_a, 2 * g + 1, 0)
                dve_v(dve, g + 3, (k + 2) % 4)

            with nc.Block() as block:
                @block.sync
                def _(sp):
                    for dst, src in ((wqkv[:], ap["wqkv"].rearrange("(c p) n -> p c n", p=P)),
                                     (wo[:], ap["light_out_w"].rearrange("(c p) n -> p c n", p=P)),
                                     (gb[:], ap["ln_affine"]), (masks[:], ap["masks"])):
                        sp.dma_start(dst, src).then_inc(loaded, 16)

                @block.gpsimd
                def _(pool):
                    for g in range(4):
                        pool_stage(pool, g, g)
                    with pool.Fori(1, NT // 4) as it:
                        for k in range(4):
                            pool_stage(pool, it * 4 + k, k)
                    for g in range(NT, NT + 2):
                        pool_stage(pool, g, g)

                @block.tensor
                def _(pe):
                    pe.wait_ge(loaded, 64)
                    pe.wait_ge(zeroed, 1)
                    for g in range(2):
                        if g:
                            pe.wait_ge(k_ev, g)
                        pe_xT(pe, g + 1, g)
                        pe.wait_ge(xT_ev, g + 1)
                        pe_qk(pe, ps_a, 0, q_done)
                        pe.wait_ge(q_ev, g + 1)
                        pe_qk(pe, ps_a, HD, k_done)
                        if g:
                            pe.wait_ge(v_ev, g)
                        pe_v(pe)
                    for k in range(4):
                        pe_tile(pe, k, k, masks[:, 0 if k == 0 else 1, :])
                    with pe.Fori(1, NT // 4) as it:
                        for k in range(4):
                            mask = masks[:, bass.ds(it % 4 + (0 if k == 0 else 4), 1), :].rearrange("p a j -> p (a j)") \
                                if k in (0, 3) else masks[:, 1, :]
                            pe_tile(pe, it * 4 + k, k, mask)
                    pe_back(pe, NT)
                    pe.wait_ge(ptA_ev, 2 * NT)
                    pe.wait_ge(ptB_ev, 2 * NT)
                    pe.wait_ge(v_ev, NT + 2)
                    pe_pv(pe, ps_b, 3, 1)
                    pe.wait_ge(pv_ev, 2 * NT)
                    pe_oT(pe)
                    pe.wait_ge(oT_ev, NT)
                    pe_proj(pe)

                @block.scalar
                def _(act):
                    act.wait_ge(loaded, 64)
                    for g in range(2):
                        act_xT(act, g + 1)
                        act_q(act, g + 1, g)
                        act_k(act, g + 1, g)
                    for k in range(4):
                        act_tile(act, k, k)
                    with act.Fori(1, NT // 4) as it:
                        for k in range(4):
                            act_tile(act, it * 4 + k, k)
                    act_ptB(act, 2 * NT, 1)

                @block.vector
                def _(dve):
                    nc.vector.memset(kT[:, :, 2 * P:4 * P], 0.0)
                    nc.vector.memset(vown[:], 1.0)
                    nc.vector.memset(vnb[:], 1.0).then_inc(zeroed, 1)
                    dve.wait_ge(zeroed, 1)
                    for g in range(2):
                        dve_v(dve, g + 1, g)
                    for k in range(4):
                        dve_tile(dve, k, k)
                    with dve.Fori(1, NT // 4) as it:
                        for k in range(4):
                            dve_tile(dve, it * 4 + k, k)
                    dve_ptA(dve, 2 * NT, 1)
                    dve_pv(dve, ps_b, 2 * NT, 1)
                    dve_oT(dve, NT)
                    dve_proj(dve, NT, NT - 1)

        with ExitStack() as ctx:
            light(ctx)

        def heavy(ctx):
            def sem(name):
                return ctx.enter_context(nc.semaphore(name))

            def st(name, shape, dt=F32):
                return sb(name, shape, dt, ctx)
            S = KSEL // P
            HH = DH // 2
            wq = st("hwq", [P, DC, HD])
            wkv = st("hwkv", [P, DC, 2 * HD])
            wo = st("hwo", [P, HC, D])
            gam = st("hgam", [P, DC])
            idx = st("hidx", [P, 4 * S], I32)
            ridx = st("hridx", [P, 4 * S], I32)
            rows = st("hrows", [P, 2 * S, D])
            rope = st("hrope", [P, 2 * S, DH])
            sq = st("hsq", [P, 2 * S, D])
            gain_k, gain_q = st("hgain_k", [P, S]), st("hgain_q", [P, S])
            tick = st("htick", [P, 2 * S])
            ss = st("hss", [P, 2 * S])
            nrm = st("hnrm", [P, 2 * S])
            rn = st("hrn", [P, 2 * S])
            xT = st("hxT", [P, DC, 2 * KSEL])
            qk = st("hqk", [P, 2 * S, H, 2, HH])
            rot = st("hrot", [P, H, 2, HH])
            val = st("hval", [P, S, H, DH + 1])
            nval = st("hnval", [1, H, DH + 1])
            qT = st("hqT", [P, HC, KSEL])
            kT = st("hkT", [P, HC, KSEL + 1])
            mx = st("hmx", [P, 2])
            nmx = st("hnmx", [P, 2])
            prob = st("hprob", [P, 2, KSEL + 1])
            probT = st("hprobT", [P, S, 2, P])
            probN = st("hprobN", [1, 2, P])
            rden = st("hrden", [P, 2])
            o = st("ho", [P, H, DH])
            oT = st("hoT", [P, HC, P])
            res = st("hres_rows", [P, D])
            ps_x = ctx.enter_context(nc.psum_tensor("hps_x", [P, 2, 512], F32))
            ps_s = ctx.enter_context(nc.psum_tensor("hps_s", [P, 2, 512], F32))
            ps_p = ctx.enter_context(nc.psum_tensor("hps_p", [P, 512], F32))
            ps_n = ctx.enter_context(nc.psum_tensor("hps_n", [P, 512], F32))
            ps_v = ctx.enter_context(nc.psum_tensor("hps_v", [P, 512], F32))
            loaded = sem("h_loaded")
            idx_ready = sem("h_idx_ready")
            idx_settled = sem("h_idx_settled")
            got_rows, got_rope = sem("h_got_rows"), sem("h_got_rope")
            ss_done, sqrt_done, rows_ready = sem("h_ss_done"), sem("h_sqrt_done"), sem("h_rows_ready")
            tr_done, tr_ev = sem("h_tr_done"), sem("h_tr_ev")
            qkv_done, qkv_ev = sem("h_qkv_done"), sem("h_qkv_ev")
            sim_done, max_done, exp_done = sem("h_sim_done"), sem("h_max_done"), sem("h_exp_done")
            pT_done, pT_ev, pN_ev = sem("h_pT_done"), sem("h_pT_ev"), sem("h_pN_ev")
            pv_done, pv_ev = sem("h_pv_done"), sem("h_pv_ev")
            oT_done, oT_ev = sem("h_oT_done"), sem("h_oT_ev")
            pr_done, pr_ev, saved = sem("h_pr_done"), sem("h_pr_ev"), sem("h_saved")
            v = sem("h_v")
            gained = sem("h_gained")
            NQKV = 3 * S
            NU = S * H // 2
            with nc.Block() as block:
                @block.sync
                def _(sp):
                    for dst, src in ((wq[:], ap["heavy_q_w"].rearrange("(c p) n -> p c n", p=P)),
                                     (wkv[:], ap["heavy_kv_w"].rearrange("(c p) n -> p c n", p=P)),
                                     (wo[:], ap["heavy_out_w"].rearrange("(c p) n -> p c n", p=P)),
                                     (gam[:], ap["heavy_gamma"]), (nval[:, :, 0:DH], ap["null_v"])):
                        sp.dma_start(dst, src).then_inc(loaded, 16)
                    with nc.allow_non_contiguous_dma(reason="one null key column of 4 words a partition"):
                        sp.dma_start(kT[:, :, KSEL:KSEL + 1], ap["null_kT"]).then_inc(loaded, 16)
                    with sp.Fori(0, B) as b:
                        for s in range(S):
                            sp.wait_ge(pr_ev, b * S + (s + 1))
                            sp.dma_start(heavy_rows[bass.ds(b * KSEL + s * P, P), :], res[:]).then_inc(saved, 16)
                    sp.wait_ge(saved, 16 * B * S)

                @block.gpsimd
                def _(pool):
                    with pool.Fori(0, B) as b:
                        pool.wait_ge(idx_ready, b + 1)
                        pool.sem_inc(idx_settled, 1)
                        for j in range(2 * S):
                            pool.indirect_dma_start(rows[:, j, :], None, norm_rows,
                                                    bass.IndirectOffsetOnAxis(ap=idx[:, j:j + 1], axis=0)
                                                    ).then_inc(got_rows, 16)
                            pool.indirect_dma_start(rope[:, j, :], None, ap["rope"],
                                                    bass.IndirectOffsetOnAxis(ap=ridx[:, j:j + 1], axis=0)
                                                    ).then_inc(got_rope, 16)

                @block.scalar
                def _(act):
                    with act.Fori(0, B) as b:
                        act.wait_ge(ss_done, b + 1)
                        nc.scalar.activation(nrm[:], ss[:], ACT.Sqrt).then_inc(sqrt_done, 1)
                        for u in range(NU):
                            act.wait_ge(max_done, b * NU + (u + 1))
                            for e in range(2):
                                i = nc.scalar.activation(prob[:, e, :], ps_s[:, e, 0:KSEL + 1], ACT.Exp,
                                                         bias=nmx[:, e:e + 1], scale=SCALE)
                            i.then_inc(exp_done, 1)
                            act.wait_ge(pT_done, b * NU + (u + 1))
                            nc.scalar.copy(probN[:], ps_n[0:1, 0:2 * P].rearrange("p (e j) -> p e j", e=2)).then_inc(pN_ev, 1)

                @block.tensor
                def _(pe):
                    pe.wait_ge(loaded, 96)
                    NTR = DC + 2 * S
                    with pe.Fori(0, B) as b:
                        tr = b * NTR
                        pe.wait_ge(rows_ready, b + 1)
                        for c in range(DC):
                            for j in range(2 * S):
                                i = nc.tensor.transpose(ps_x[:, c, j * P:(j + 1) * P], rows[:, j, c * P:(c + 1) * P], ident[:])
                            i.then_inc(tr_done, 1)
                        pe.wait_ge(tr_ev, tr + DC)
                        for n in range(NQKV):
                            kind, s = divmod(n, S)
                            w = wq[:, :, :] if kind == 0 else wkv[:, :, (kind - 1) * HD:kind * HD]
                            at = (0 if kind == 0 else KSEL) + s * P
                            if n >= 2:
                                pe.wait_ge(qkv_ev, b * NQKV + (n - 1))
                            for c in range(DC):
                                i = nc.tensor.matmul(ps_x[:, n % 2, :], xT[:, c, at:at + P], w[:, c, :],
                                                     start=(c == 0), stop=(c == DC - 1))
                            i.then_inc(qkv_done, 1)
                        pe.wait_ge(qkv_ev, b * NQKV + NQKV)
                        for j in range(2 * S):
                            if j >= 2:
                                pe.wait_ge(tr_ev, tr + (DC + j - 1))
                            flat = qk[:, j].rearrange("p h a d -> p (h a d)")
                            for c in range(HC):
                                i = nc.tensor.transpose(ps_x[:, j % 2, c * P:(c + 1) * P], flat[:, c * P:(c + 1) * P], ident[:])
                            i.then_inc(tr_done, 1)
                        pe.wait_ge(tr_ev, tr + NTR)
                        for s in range(S):
                            for c in range(HC):
                                u = b * NU + (s * HC + c)
                                for e in range(2):
                                    i = nc.tensor.matmul(ps_s[:, e, 0:KSEL + 1], qT[64 * e:64 * e + 64, c, s * P:(s + 1) * P],
                                                         kT[64 * e:64 * e + 64, c, :], start=True, stop=True)
                                i.then_inc(sim_done, 1)
                                pe.wait_ge(exp_done, u + 1)
                                for e in range(2):
                                    for j in range(S):
                                        nc.tensor.transpose(ps_p[:, (j * 2 + e) * P:(j * 2 + e + 1) * P],
                                                            prob[:, e, j * P:(j + 1) * P], ident[:])
                                    i = nc.tensor.transpose(ps_n[0:1, e * P:(e + 1) * P], prob[:, e, KSEL:KSEL + 1], ident[:])
                                i.then_inc(pT_done, 1)
                                pe.wait_ge(pT_ev, u + 1)
                                pe.wait_ge(pN_ev, u + 1)
                                if s or c:
                                    pe.wait_ge(pv_ev, u)
                                for e in range(2):
                                    dst = ps_v[:, e * (DH + 1):(e + 1) * (DH + 1)]
                                    for j in range(S):
                                        nc.tensor.matmul(dst, probT[:, j, e, :], val[:, j, 2 * c + e, :],
                                                         start=(j == 0), stop=False)
                                    i = nc.tensor.matmul(dst, probN[:, e, :], nval[:, 2 * c + e, :], start=False, stop=True)
                                i.then_inc(pv_done, 1)
                            pe.wait_ge(pv_ev, b * NU + (s + 1) * HC)
                            flat = o[:].rearrange("p h d -> p (h d)")
                            for c in range(HC):
                                i = nc.tensor.transpose(ps_p[:, c * P:(c + 1) * P], flat[:, c * P:(c + 1) * P], ident[:])
                            i.then_inc(oT_done, 1)
                            pe.wait_ge(oT_ev, b * S + (s + 1))
                            for c in range(HC):
                                i = nc.tensor.matmul(ps_v[:, 0:D], oT[:, c, :], wo[:, c, :], start=(c == 0), stop=(c == HC - 1))
                            i.then_inc(pr_done, 1)
                            pe.wait_ge(pr_ev, b * S + (s + 1))

                @block.vector
                def _(dve):
                    NV = [0]

                    def link(i, base):
                        NV[0] += 1
                        i.then_inc(v, 1)
                        dve.wait_ge(v, base + NV[0])
                    PER = 5 + 3 * 2 * S + 2 * NU
                    NTR = DC + 2 * S
                    nc.vector.memset(val[:], 1.0)
                    nc.vector.memset(nval[:, :, DH:DH + 1], 1.0)
                    dve.wait_ge(loaded, 96)
                    with dve.Fori(0, B) as b:
                        NV[0] = 0
                        base = b * PER
                        tr = b * NTR
                        for r in range(2):
                            i = nc.vector.tensor_copy(idx[:, r * S:(r + 1) * S],
                                                      sel_idx[:, bass.ds(b + r * B, 1), :].rearrange("p a s -> p (a s)"))
                        link(i, base)
                        nc.vector.tensor_scalar(ridx[:, 0:2 * S], idx[:, 0:2 * S], N - 1, None, ALU.bitwise_and
                                                ).then_inc(idx_ready, 1)
                        dve.wait_ge(got_rows, (b + 1) * (16 * 2 * S))
                        for j in range(2 * S):
                            i = nc.vector.tensor_tensor_reduce(sq[:, j, :], rows[:, j, :], rows[:, j, :], 1.0, 0.0, ALU.mult,
                                                               ALU.add, ss[:, j:j + 1])
                        i.then_inc(ss_done, 1)
                        dve.wait_ge(sqrt_done, b + 1)
                        link(nc.vector.tensor_scalar(nrm[:], nrm[:], 1e-12, None, ALU.max), base)
                        link(nc.vector.reciprocal(rn[:], nrm[:]), base)
                        for j in range(2 * S):
                            i = nc.vector.tensor_scalar(rows[:, j, :], rows[:, j, :], rn[:, j:j + 1], float(D) ** 0.5,
                                                        ALU.mult, ALU.mult)
                        i.then_inc(rows_ready, 1)
                        for c in range(DC):
                            dve.wait_ge(tr_done, tr + (c + 1))
                            nc.vector.tensor_scalar(xT[:, c, :], ps_x[:, c, :], gam[:, c:c + 1], None, ALU.mult
                                                    ).then_inc(tr_ev, 1)
                        dve.wait_ge(got_rope, (b + 1) * (16 * 2 * S))
                        for n in range(2 * S):
                            dve.wait_ge(qkv_done, b * NQKV + (n + 1))
                            src = ps_x[:, n % 2, :].rearrange("p (h a d) -> p h a d", h=H, a=2)
                            cos = rope[:, n, 0:HH].rearrange("p (o d) -> p o d", o=1)
                            sin = rope[:, n, HH:DH].rearrange("p (o d) -> p o d", o=1).broadcast_to([P, H, HH])
                            link(nc.vector.tensor_tensor(qk[:, n].rearrange("p h a d -> p (h a) d"),
                                                         src.rearrange("p h a d -> p (h a) d"),
                                                         cos.broadcast_to([P, 2 * H, HH]), ALU.mult), base)
                            nc.vector.tensor_tensor(rot[:, :, 0, :], src[:, :, 1, :], sin, ALU.mult)
                            link(nc.vector.tensor_tensor(rot[:, :, 1, :], src[:, :, 0, :], sin, ALU.mult), base)
                            nc.vector.tensor_tensor(qk[:, n, :, 0, :], qk[:, n, :, 0, :], rot[:, :, 0, :], ALU.subtract)
                            i = nc.vector.tensor_tensor(qk[:, n, :, 1, :], qk[:, n, :, 1, :], rot[:, :, 1, :], ALU.add)
                            link(i, base)
                            nc.vector.tensor_copy(tick[:, n:n + 1], rot[:, 0, 0, 0:1]).then_inc(qkv_ev, 1)
                        link(nc.vector.tensor_scalar(gain_k[:], sel_gain[:, bass.ds(b + B, 1), :].rearrange("p a s -> p (a s)"),
                                                     1.0, None, ALU.mult), base)
                        for s in range(S):
                            n = 2 * S + s
                            dve.wait_ge(qkv_done, b * NQKV + (n + 1))
                            nc.vector.tensor_scalar(val[:, s, :, 0:DH], ps_x[:, n % 2, :].rearrange("p (h d) -> p h d", h=H),
                                                    gain_k[:, s:s + 1], None, ALU.mult).then_inc(qkv_ev, 1)
                        link(nc.vector.tensor_scalar(gain_q[:], sel_gain[:, bass.ds(b, 1), :].rearrange("p a s -> p (a s)"),
                                                     1.0, None, ALU.mult), base)
                        for j in range(2 * S):
                            dve.wait_ge(tr_done, tr + (DC + j + 1))
                            dst = qT if j < S else kT
                            nc.vector.tensor_copy(dst[:, :, (j % S) * P:(j % S + 1) * P],
                                                  ps_x[:, j % 2, :].rearrange("p (c j) -> p c j", c=HC)).then_inc(tr_ev, 1)
                        for s in range(S):
                            for c in range(HC):
                                u = b * NU + (s * HC + c)
                                dve.wait_ge(sim_done, u + 1)
                                link(nc.vector.tensor_reduce(mx[:], ps_s[:, :, 0:KSEL + 1], AX, ALU.max), base)
                                nc.vector.tensor_scalar(nmx[:], mx[:], -SCALE, None, ALU.mult).then_inc(max_done, 1)
                                dve.wait_ge(pT_done, u + 1)
                                nc.vector.tensor_copy(probT[:].rearrange("p j e q -> p (j e q)"), ps_p[:]).then_inc(pT_ev, 1)
                                dve.wait_ge(pv_done, u + 1)
                                view = ps_v[:, 0:2 * (DH + 1)].rearrange("p (h d) -> p h d", h=2)
                                link(nc.vector.reciprocal(rden[:], view[:, :, DH]), base)
                                nc.vector.tensor_tensor(o[:, 2 * c:2 * c + 2, :], view[:, :, 0:DH],
                                                        rden[:].rearrange("p (h o) -> p h o", o=1).broadcast_to([P, 2, DH]),
                                                        ALU.mult).then_inc(pv_ev, 1)
                            dve.wait_ge(oT_done, b * S + (s + 1))
                            nc.vector.tensor_copy(oT[:].rearrange("p c j -> p (c j)"), ps_p[:]).then_inc(oT_ev, 1)
                            dve.wait_ge(pr_done, b * S + (s + 1))
                            nc.vector.tensor_scalar(res[:], ps_v[:, 0:D], gain_q[:, s:s + 1], None, ALU.mult).then_inc(pr_ev, 1)
                            dve.wait_ge(saved, (b * S + (s + 1)) * 16)
                        assert NV[0] == PER, NV[0]

        with ExitStack() as ctx:
            heavy(ctx)

        with ExitStack() as ctx:
            def sem(name):
                return ctx.enter_context(nc.semaphore(name))
            idc = sb("m_idc", [P, 4], I32, ctx)
            epsc = sb("m_epsc", [P, 1], F32, ctx)
            raw = sb("m_raw", [P, 4, D], F32, ctx)
            st = sb("m_st", [P, 4, 6], F32, ctx)
            mv = sb("m_mv", [P, 4, 2], F32, ctx)
            sd = sb("m_sd", [P, 4], F32, ctx)
            rstd = sb("m_rstd", [P, 4], F32, ctx)
            id_copied = sem("m_id_copied")
            id_settled = sem("m_id_settled")
            gathered = [sem(f"m_gathered{k}") for k in range(4)]
            raw_used, eps_set, var_ready, sd_ready, step = (sem("m_raw_used"), sem("m_eps_set"), sem("m_var_ready"),
                                                            sem("m_sd_ready"), sem("m_step"))
            STEPS = 9
            with nc.Block() as block:
                @block.gpsimd
                def _(pool):
                    flat = pos[:].rearrange("p b t -> p (b t)")
                    with pool.Fori(0, NT // 4) as it:
                        nc.gpsimd.tensor_copy(idc[:], flat[:, bass.ds(it * 4, 4)]).then_inc(id_copied, 1)
                        pool.wait_ge(id_copied, it + 1)
                        pool.sem_inc(id_settled, 1)
                        for k in range(4):
                            pool.indirect_dma_start(raw[:, k, :], None, heavy_rows,
                                                    bass.IndirectOffsetOnAxis(ap=idc[:, k:k + 1], axis=0)
                                                    ).then_inc(gathered[k], 16)
                        pool.wait_ge(raw_used, it + 1)

                @block.scalar
                def _(act):
                    act.wait_ge(eps_set, 1)
                    with act.Fori(0, NT // 4) as it:
                        act.wait_ge(var_ready, it + 1)
                        nc.scalar.activation(sd[:], mv[:, :, 1], ACT.Sqrt, bias=epsc[:, 0:1]).then_inc(sd_ready, 1)

                @block.vector
                def _(dve):
                    nc.vector.memset(epsc[:], LN_EPS).then_inc(eps_set, 1)
                    with dve.Fori(0, NT // 4) as it:
                        base = it * STEPS
                        row = lambda k: hres[:, bass.ds(it * 4 + k, 1), :].rearrange("p a d -> p (a d)")
                        for k in range(4):
                            dve.wait_ge(gathered[k], it * 16 + 16)
                            nc.vector.tensor_tensor(raw[:, k, :], row(k), raw[:, k, :], ALU.add).then_inc(step, 1)
                        for k in range(4):
                            dve.wait_ge(step, base + (k + 1))
                            nc.vector.tensor_scalar(row(k), raw[:, k, :], 1.0, None, ALU.mult)
                            i = nc.vector.bn_stats(st[:, k, :], raw[:, k, :])
                            i.then_inc(step, 1)
                        dve.wait_ge(step, base + 8)
                        nc.vector.tensor_copy(rstd[:, 0:1], st[:, 0, 0:1])
                        for k in range(4):
                            i = nc.vector.bn_aggr(mv[:, k, :], st[:, k, :])
                        i.then_inc(var_ready, 1)
                        dve.wait_ge(sd_ready, it + 1)
                        nc.vector.reciprocal(rstd[:], sd[:]).then_inc(step, 1)
                        dve.wait_ge(step, base + 9)
                        for k in range(4):
                            i = nc.vector.tensor_scalar(xn[:, bass.ds(it * 4 + k, 1), :].rearrange("p a d -> p (a d)"), raw[:, k, :],
                                                        mv[:, k, 0:1], rstd[:, k:k + 1], ALU.subtract, ALU.mult)
                        i.then_inc(raw_used, 1)

        def ffn(ctx):
            def sem(name):
                return ctx.enter_context(nc.semaphore(name))

            def st(name, shape, dt=F32):
                return sb(name, shape, dt, ctx)
            GT = 4
            GN = GT * P
            NG = T // GT
            w = st("fw", [P, 8, DC, D])
            bias = st("fbias", [P, 4, DC])
            bo = st("fbo", [P, D])
            stage = st("fstage", [P, 2, GT, D])
            xT = st("fxT", [P, B, DC, GN])
            cT = st("fcT", [P, DC, GN])
            gates = st("fgates", [P, 3, GN])
            t1 = st("ft1", [P, GN])
            cf = st("fcf", [P, GT, D])
            z = st("fz", [P, 2, 2, D])
            y = st("fy", [P, 2, 2, D])
            ps_g = ctx.enter_context(nc.psum_tensor("fps_g", [P, 6, 512], F32))
            ps_t = ctx.enter_context(nc.psum_tensor("fps_t", [P, 2, 512], F32))
            loaded, c_init = sem("f_loaded"), sem("f_c_init")
            xT_done, xT_ev = sem("f_xT_done"), sem("f_xT_ev")
            gate_done, gate_ev = sem("f_gate_done"), sem("f_gate_ev")
            c_ready, v = sem("f_c_ready"), sem("f_v")
            staged = sem("f_staged")
            cf_done, cf_ev = sem("f_cf_done"), sem("f_cf_ev")
            out_done, z_ready, tanh_done, y_ready = (sem("f_out_done"), sem("f_z_ready"), sem("f_tanh_done"),
                                                     sem("f_y_ready"))
            saved = [sem(f"f_saved{parity}") for parity in range(2)]
            NO = B * GT // 2
            with nc.Block() as block:
                @block.sync
                def _(sp):
                    for dst, src in ((w[:], ap["ffn_w"]), (bias[:], ap["ffn_bias"]), (bo[:], ap["ffn_bo"])):
                        sp.dma_start(dst, src).then_inc(loaded, 16)
                    rows = out.rearrange("b (t p) d -> p (b t) d", p=P)
                    with sp.Fori(0, NG) as g:
                        for n in range(NO):
                            b, h = divmod(n, GT // 2)
                            sp.wait_ge(y_ready, g * NO + (n + 1))
                            sp.dma_start(rows[:, bass.ds(g * GT + (b * T + 2 * h), 2), :], y[:, n % 2]).then_inc(saved[n % 2], 16)
                    for parity in range(2):
                        sp.wait_ge(saved[parity], 8 * NG * NO)

                @block.tensor
                def _(pe):
                    pe.wait_ge(loaded, 48)
                    with pe.Fori(0, NG) as g:
                        def x_transposes(b):
                            pe.wait_ge(staged, g * B + (b + 1))
                            for c in range(DC):
                                if b:
                                    pe.wait_ge(xT_ev, g * (B * DC) + ((b - 1) * DC + c + 1))
                                for t in range(GT):
                                    i = nc.tensor.transpose(ps_t[:, c, t * P:(t + 1) * P],
                                                            stage[:, b % 2, t, c * P:(c + 1) * P], ident[:])
                                i.then_inc(xT_done, 1)

                        def x_part(b):
                            pe.wait_ge(xT_ev, g * (B * DC) + (b + 1) * DC)
                            for m in range(DC):
                                for q in range(3):
                                    if b:
                                        pe.wait_ge(gate_ev, g * (B * 6) + ((b - 1) * 6 + m * 3 + q + 1))
                                    for c in range(DC):
                                        nc.tensor.matmul(ps_g[:, m * 3 + q, :], w[:, q, c, m * P:(m + 1) * P], xT[:, b, c, :],
                                                         start=(c == 0), stop=False)

                        def c_part(b):
                            pe.wait_ge(c_ready, g * (B + 1) + (b + 1))
                            for m in range(DC):
                                for q in range(3):
                                    for c in range(DC):
                                        i = nc.tensor.matmul(ps_g[:, m * 3 + q, :], w[:, 4 + q, c, m * P:(m + 1) * P],
                                                             cT[:, c, :], start=False, stop=(c == DC - 1))
                                    i.then_inc(gate_done, 1)

                        x_transposes(0)
                        x_part(0)
                        for b in range(B):
                            if b + 1 < B:
                                x_transposes(b + 1)
                            c_part(b)
                            if b + 1 < B:
                                x_part(b + 1)
                        pe.wait_ge(c_ready, g * (B + 1) + (B + 1))
                        pe.wait_ge(xT_ev, g * (B * DC) + B * DC)
                        for h in range(GT // 2):
                            for t in range(2):
                                for c in range(DC):
                                    j = 2 * h + t
                                    i = nc.tensor.matmul(ps_t[:, h, t * D:(t + 1) * D], cT[:, c, j * P:(j + 1) * P], w[:, 7, c, :],
                                                         start=(c == 0), stop=(c == DC - 1))
                            i.then_inc(cf_done, 1)
                        for n in range(NO):
                            b, h = divmod(n, GT // 2)
                            if n < 2:
                                pe.wait_ge(cf_ev, g * 2 + (n + 1))
                            else:
                                pe.wait_ge(z_ready, g * NO + (n - 1))
                            for t in range(2):
                                for c in range(DC):
                                    j = 2 * h + t
                                    i = nc.tensor.matmul(ps_t[:, n % 2, t * D:(t + 1) * D], xT[:, b, c, j * P:(j + 1) * P],
                                                         w[:, 3, c, :], start=(c == 0), stop=(c == DC - 1))
                            i.then_inc(out_done, 1)
                        pe.wait_ge(z_ready, g * NO + NO)
                        pe.wait_ge(gate_ev, g * (B * 6) + B * 6)

                @block.scalar
                def _(act):
                    act.wait_ge(loaded, 48)
                    with act.Fori(0, NG) as g:
                        for b in range(B):
                            for m in range(DC):
                                for q in range(3):
                                    n = b * 6 + m * 3 + q
                                    act.wait_ge(gate_done, g * (B * 6) + (n + 1))
                                    if q == 0 and n:
                                        act.wait_ge(v, g * (B * DC * 3) + (b * DC + m) * 3)
                                    nc.scalar.activation(gates[:, q, :], ps_g[:, m * 3 + q, :],
                                                         ACT.Tanh if q == 2 else ACT.Sigmoid, bias=bias[:, q, m:m + 1]
                                                         ).then_inc(gate_ev, 1)
                        for n in range(NO):
                            act.wait_ge(z_ready, g * NO + (n + 1))
                            nc.scalar.activation(z[:, n % 2], z[:, n % 2], ACT.Tanh).then_inc(tanh_done, 1)
                        act.wait_ge(v, (g + 1) * (B * DC * 3))

                @block.vector
                def _(dve):
                    dve.wait_ge(loaded, 48)
                    with dve.Fori(0, NG) as g:
                        nc.vector.memset(t1[:], 0.0).then_inc(c_init, 1)
                        dve.wait_ge(c_init, g + 1)
                        for c in range(DC):
                            i = nc.vector.tensor_scalar(cT[:, c, :], t1[:], bias[:, 3, c:c + 1], None, ALU.add)
                        i.then_inc(c_ready, 1)

                        def evacuate_x(b):
                            for c in range(DC):
                                dve.wait_ge(xT_done, g * (B * DC) + (b * DC + c + 1))
                                nc.vector.tensor_copy(xT[:, b, c, :], ps_t[:, c, :]).then_inc(xT_ev, 1)

                        evacuate_x(0)
                        for b in range(B):
                            if b + 1 < B:
                                evacuate_x(b + 1)
                            dve.wait_ge(gate_done, g * (B * 6) + (b + 1) * 6)
                            for m in range(DC):
                                k = (b * DC + m) * 3
                                dve.wait_ge(gate_ev, g * (B * 6) + (b * 6 + m * 3 + 3))
                                nc.vector.tensor_tensor(t1[:], gates[:, 1, :], gates[:, 2, :], ALU.mult).then_inc(v, 1)
                                nc.vector.tensor_tensor(cT[:, m, :], cT[:, m, :], gates[:, 0, :], ALU.mult).then_inc(v, 1)
                                dve.wait_ge(v, g * (B * DC * 3) + (k + 2))
                                i = nc.vector.tensor_tensor(cT[:, m, :], cT[:, m, :], t1[:], ALU.add)
                                i.then_inc(v, 1)
                            dve.wait_ge(v, g * (B * DC * 3) + (b + 1) * DC * 3)
                            nc.vector.tensor_copy(t1[:, 0:1], cT[:, 0, 0:1]).then_inc(c_ready, 1)
                        for h in range(GT // 2):
                            dve.wait_ge(cf_done, g * 2 + (h + 1))
                            nc.vector.tensor_tensor(cf[:, 2 * h:2 * h + 2, :], ps_t[:, h, :].rearrange("p (t d) -> p t d", t=2),
                                                    bo[:].rearrange("p (o d) -> p o d", o=1).broadcast_to([P, 2, D]), ALU.add
                                                    ).then_inc(cf_ev, 1)
                        dve.wait_ge(cf_ev, g * 2 + 2)
                        for n in range(NO):
                            b, h = divmod(n, GT // 2)
                            dve.wait_ge(out_done, g * NO + (n + 1))
                            if n >= 2:
                                dve.wait_ge(y_ready, g * NO + (n - 1))
                            nc.vector.tensor_tensor(z[:, n % 2], ps_t[:, n % 2, :].rearrange("p (t d) -> p t d", t=2),
                                                    cf[:, 2 * h:2 * h + 2, :], ALU.add).then_inc(z_ready, 1)
                        dve.wait_ge(y_ready, g * NO + NO)

                @block.gpsimd
                def _(pool):
                    with pool.Fori(0, NG) as g:
                        for b in range(B):
                            if b >= 2:
                                pool.wait_ge(xT_done, g * (B * DC) + (b - 1) * DC)
                            nc.gpsimd.tensor_copy(stage[:, b % 2], xn[:, bass.ds(g * GT + b * T, GT), :]).then_inc(staged, 1)
                        for n in range(NO):
                            b, h = divmod(n, GT // 2)
                            pool.wait_ge(tanh_done, g * NO + (n + 1))
                            if n >= 2:
                                pool.wait_ge(saved[n % 2], g * (8 * NO) + 16 * (n // 2))
                            nc.gpsimd.tensor_tensor(y[:, n % 2].rearrange("p t d -> p (t d)"),
                                                    z[:, n % 2].rearrange("p t d -> p (t d)"),
                                                    hres[:, bass.ds(g * GT + (b * T + 2 * h), 2), :].rearrange("p t d -> p (t d)"),
                                                    ALU.add).then_inc(y_ready, 1)
                        for parity in range(2):
                            pool.wait_ge(saved[parity], (g + 1) * (8 * NO))

        with ExitStack() as ctx:
            ffn(ctx)


def constants():
    f = np.float32
    eps, _ = descent_eps()
    e = np.array(eps, np.float64)
    descent = np.stack([-1.0 / e, e, -e * LOGK]).astype(f)
    bits = np.array([1 << (SEARCH_BITS - 1 - i) for i in range(SEARCH_BITS)], np.uint32)
    col = np.arange(R * T)
    not_first = (col % T != 0).astype(f)
    row_base = ((col // T) * KSEL - B * KSEL).astype(f)
    p = np.arange(P)[:, None]
    tokid = (((col // T) % B) * N + (col % T) * P + p).astype(f)
    masks = np.zeros((P, 8, 2 * P), f)
    q = np.arange(P)[:, None]
    own = np.abs(q - np.arange(P)[None]) > W
    nxt = (P + np.arange(W)[None] - q) > W
    prv = (q - (np.arange(W)[None] + W - P)) > W
    for m in range(8):
        masks[:, m, 0:P][own] = NEG
        masks[:, m, P:P + W][nxt | (np.zeros_like(nxt) | (m == 7))] = NEG
        masks[:, m, P + W:][prv | (np.zeros_like(prv) | (m == 0))] = NEG
    ang = (np.arange(N, dtype=f)[:, None] * (1.0 / (10000.0 ** (np.arange(0, DH, 2) / DH))).astype(f)[None]).astype(f)
    bcast = lambda a: np.ascontiguousarray(np.broadcast_to(a, (P,) + a.shape))
    return {
        "descent": bcast(descent), "bits": bcast(bits), "row_consts": bcast(np.stack([not_first, row_base])),
        "tri": np.triu(np.ones((P, P), f), 1), "iota16": bcast(np.arange(16, dtype=f)), "tokid": tokid,
        "ident": np.eye(P, dtype=f), "ident_bf": np.eye(P).astype(np.dtype("bfloat16")),
        "masks": masks.astype(np.dtype("bfloat16")),
        "rope": np.concatenate([np.cos(ang.astype(np.float64)), np.sin(ang.astype(np.float64))], 1).astype(f),
    }


def kernel(**inputs):
    import concourse.bacc as bacc
    from concourse.bass_utils import run_bass_kernel_spmd as run

    a = {k: np.asarray(v) for k, v in inputs.items()}
    at = lambda n: a["L0_attn_" + n]
    ff = lambda n: a["L0_ffn_" + n]
    rows = lambda v: np.ascontiguousarray(np.broadcast_to(v, (P,) + v.shape))
    chunks = lambda v: v.reshape(DC, P).T
    mats = [ff("wf").T, ff("wi").T, ff("wc").T, ff("wo").T, ff("uf").T, ff("ui").T, ff("uc").T, ff("uo").T]
    kv = at("heavy_kv_w").reshape(H, 2, DH, D)
    null = at("heavy_null_kv")
    arrays = {
        "ids": a["x"].reshape(NT, P).T,
        "table": a["L0_tok_weight"].T,
        "tok_bias": rows(a["L0_tok_bias"]),
        "route_tok": rows(np.stack([at("q_route_tok"), at("kv_route_tok")])),
        "null_q": at("null_q_token").reshape(1, D),
        "wqkv": at("light_qkv_w"),
        "light_out_w": at("light_out_w"),
        "ln_affine": np.stack([chunks(at("ln_gamma")), chunks(at("ln_beta"))], 1),
        "heavy_q_w": at("heavy_q_w"),
        "heavy_kv_w": kv.transpose(3, 1, 0, 2).reshape(D, 2 * HD),
        "heavy_out_w": at("heavy_out_w"),
        "heavy_gamma": chunks(at("heavy_gamma")),
        "null_kT": null[0].reshape(HC, P).T.reshape(P, HC, 1),
        "null_v": null[1].reshape(1, H, DH),
        "ffn_w": np.stack([m.reshape(DC, P, D).transpose(1, 0, 2) for m in mats], 1),
        "ffn_bias": np.stack([chunks(ff("bf")), chunks(ff("bi")), chunks(ff("bc")), chunks(ff("in_c"))], 1),
        "ffn_bo": rows(ff("bo")),
    }
    arrays.update(constants())
    nc = bacc.Bacc("TRN2", target_bir_lowering=False, num_devices=1)
    ap, feeds = {}, {}
    for name, v in arrays.items():
        v = np.ascontiguousarray(v)
        feeds[f"in_{name}"] = v
        ap[name] = nc.dram_tensor(f"in_{name}", v.shape, mybir.dt.from_np(v.dtype), kind="ExternalInput").ap()
    out = nc.dram_tensor("out", (B, N, D), F32, kind="ExternalOutput").ap()
    lm_tower(nc, ap, out)
    return run(nc, [feeds], core_ids=[0]).results[0]["out"]
```

```python
from contextlib import ExitStack
import math

import numpy as np
import concourse.bass as bass
from concourse import mybir

P = 128
B, N, D = 4, 2048, 256
T = N // P
NT = B * T
DC = D // P
H, DH = 8, 64
HD = H * DH
HC = HD // P
KSEL = 256
W = 64
ITERS, EPS0, EPS_END, DECAY = 20, 4.0, 0.03, 0.7
SEARCH_BITS = 30
EB = 4
NB = B * (N // P) // EB
LOGK = math.log(min(KSEL * 9.0 / 8.0, N))
LN_EPS = 1e-5
SCALE = DH ** -0.5
R = 2 * B
NEG = -3.0e38

F32 = mybir.dt.float32
BF16 = mybir.dt.bfloat16
I32 = mybir.dt.int32
U32 = mybir.dt.uint32
ALU = mybir.AluOpType
ACT = mybir.ActivationFunctionType
AX = mybir.AxisListType.X


def descent_eps():
    out, cur = [], max(EPS0, EPS_END)
    for _ in range(ITERS):
        out.append(cur)
        cur = max(cur * DECAY, EPS_END)
    return out, cur


def past(v):
    return not (isinstance(v, int) and v < 1)


def lm_tower(nc, ap, out):
    with ExitStack() as top:
        def sb(name, shape, dt=F32, ctx=top):
            return ctx.enter_context(nc.sbuf_tensor(name, shape, dt))

        def dram(name, shape, dt=F32):
            return nc.dram_tensor(name, shape, dt, kind="Internal").ap()

        norm_rows = dram("norm_rows", [B * N, D])
        light_rows = dram("light_rows", [B * N, D])
        heavy_rows = dram("heavy_rows", [B * KSEL + 1, D])
        list_idx = dram("list_idx", [R * KSEL, 1], I32)
        list_gain = dram("list_gain", [R * KSEL, 1])

        hres = sb("hres", [P, NT, D])
        ident = sb("ident", [P, P])
        pos = sb("pos", [P, B, T], I32)
        sel_idx = sb("sel_idx", [P, R, KSEL // P], I32)
        sel_gain = sb("sel_gain", [P, R, KSEL // P])

        def light(ctx):
            def sem(name):
                return ctx.enter_context(nc.semaphore(name))

            def st(name, shape, dt=F32):
                return sb(name, shape, dt, ctx)
            wqkv = st("wqkv", [P, DC, 3 * HD])
            wo = st("wo", [P, HC, D])
            gb = st("gb", [P, 2, DC])
            masks = st("masks", [P, 5, 2 * P], BF16)
            stage = st("stage", [P, 2, D])
            xT = st("xT", [P, DC, P])
            qT = st("qT", [P, HC, 2, P])
            kT = st("kT", [P, HC, 4, 2 * P])
            vown = st("vown", [P, 4, H, DH + 1])
            vnb = st("vnb", [P, 4, H, DH + 1])
            edge = st("edge", [P, 2, 2 * P], BF16)
            carry = st("carry", [P, 16])
            ids = st("ids", [P, NT], I32)
            idc = st("idc", [P, 2, EB], I32)
            tokb = st("tokb", [P, D])
            rtok = st("rtok", [P, 2, D])
            epsc = st("epsc", [P, 1])
            raw = st("raw", [P, 2, EB, D])
            hn = st("hn", [P, 2, EB, D])
            xnb = st("xnb", [P, EB, D])
            stats1 = st("stats1", [P, EB, 6])
            stats2 = st("stats2", [P, EB, 6])
            mv = st("mv", [P, 2 * EB, 2])
            sd = st("sd", [P, 2 * EB])
            rstd = st("rstd", [P, 2 * EB])
            nmr = st("nmr", [P, EB])
            srow = st("srow", [P, 2, EB])
            C = R * T
            eps_list, eps_last = descent_eps()
            dtab = st("dtab", [P, 3, ITERS])
            bits = st("bits", [P, SEARCH_BITS + 1], U32)
            consts = st("consts", [P, 2, C])
            tri = st("tri", [P, P])
            ones = st("ones", [P, P])
            iota16 = st("iota16", [P, 16])
            tokid = st("tokid", [P, C])
            score_in = st("score_in", [P, R, T])
            smax, smax1 = st("smax", [P, R]), st("smax1", [P, R])
            shift, mk, part, lsum, lse, nega = (st(n, [P, R]) for n in ("shift", "mk", "part", "lsum", "lse", "nega"))
            thr, cand, kept, need = (st(n, [P, R]) for n in ("thr", "cand", "kept", "need"))
            work, expo, negu, score, eq, gt, sel = (st(n, [P, R, T]) for n in ("work", "expo", "negu", "score", "eq", "gt", "sel"))
            incl, rank, gain = st("incl", [P, C]), st("rank", [P, C]), st("gain", [P, C])
            pre = st("pre", [P, 2 * C])
            ri = st("ri", [P, 3, C], I32)
            rf = st("rf", [P, 2, C])
            hi1 = st("hi1", [P, C, 16])
            lo1 = st("lo1", [P, C, 32])
            junk = hi1[:].rearrange("p c s -> p (c s)").rearrange("p (a d) -> p a d", d=D)
            lists_f = st("lists_f", [16, R, 32])
            lists_i = st("lists_i", [16, R, 16], I32)
            mx = st("mx", [P, 2, 4])
            nmx = st("nmx", [P, 2, 4])
            prob = st("prob", [P, 2, 4, 2 * P])
            probT = st("probT", [P, 2, 2, 4, P])
            rden = st("rden", [P, 2, 4])
            o = st("o", [P, H, DH])
            oT = st("oT", [P, HC, P])
            ps_sim = ctx.enter_context(nc.psum_tensor("ps_sim", [P, 2, 4, 2 * P], F32))
            ps_pT = ctx.enter_context(nc.psum_tensor("ps_pT", [P, 2, 4, P], F32))
            ps_a = ctx.enter_context(nc.psum_tensor("ps_a", [P, 512], F32))
            ps_b = ctx.enter_context(nc.psum_tensor("ps_b", [P, 512], F32))
            loaded, first_loaded, sp_settled = sem("l_loaded"), sem("l_first_loaded"), sem("l_sp_settled")
            zeroed = sem("l_zeroed")
            edge_ready = sem("l_edge_ready")
            staged = [sem(f"l_staged{k}") for k in range(2)]
            xT_done, xT_ev = sem("l_xT_done"), sem("l_xT_ev")
            q_done, q_ev = sem("l_q_done"), sem("l_q_ev")
            k_done, k_ev = sem("l_k_done"), sem("l_k_ev")
            v_done, v_ev = sem("l_v_done"), sem("l_v_ev")
            sim_done, max_done, exp_done = sem("l_sim_done"), sem("l_max_done"), sem("l_exp_done")
            nmx_in = sem("l_nmx_in")
            ptA_done, ptB_done, ptA_ev, ptB_ev = sem("l_ptA_done"), sem("l_ptB_done"), sem("l_ptA_ev"), sem("l_ptB_ev")
            pv_done, pv_ev, rden_done = sem("l_pv_done"), sem("l_pv_ev"), sem("l_rden_done")
            oT_done, oT_ev = sem("l_oT_done"), sem("l_oT_ev")
            proj_done, proj_ev = sem("l_proj_done"), sem("l_proj_ev")
            id_copied, id_settled, added = sem("e_id_copied"), sem("e_id_settled"), sem("e_added")
            gathered = [[sem(f"e_gathered{par}{k}") for k in range(EB)] for par in range(2)]
            eps_set, stats1_in, stats2_in = sem("e_eps_set"), sem("e_stats1_in"), sem("e_stats2_in")
            var_ready, sd_ready, rstd_ready, nmr_ready = sem("e_var_ready"), sem("e_sd_ready"), sem("e_rstd_ready"), sem("e_nmr_ready")
            normed, xn_done, dots = sem("e_normed"), sem("e_xn_done"), sem("e_dots")
            hn_saved, xn_saved = sem("e_hn_saved"), sem("e_xn_saved")
            part_max, all_max, v = sem("r_part_max"), sem("r_all_max"), sem("r_v")
            diff_ready, exp_ready, sum_in = sem("r_diff_ready"), sem("r_exp_ready"), sem("r_sum_in")
            sum_out, ln_done = sem("r_sum_out"), sem("r_ln_done")
            score_args, score_done = sem("r_score_args"), sem("r_score_done")
            cnt_in, cnt_done, thr_ready = sem("r_cnt_in"), sem("r_cnt_done"), sem("r_thr_ready")
            mask_in, pref_out = sem("r_mask_in"), sem("r_pref_out")
            onehot, list_out, list_saved, list_back = sem("r_onehot"), sem("r_list_out"), sem("r_list_saved"), sem("r_list_back")
            null_saved = sem("r_null_saved")
            bc = lambda a: a.rearrange("p (r o) -> p r o", o=1).broadcast_to([P, R, T])
            flat2 = lambda a: a.rearrange("p r t -> p (r t)")

            def head(u, h):
                return 4 * u + 2 * (h % 2) + h // 2

            def pe_xT(pe, n, slot):
                pe.wait_ge(staged[slot % 2], n * 8 + (16 - 8 * (slot % 2)))
                for c in range(DC):
                    i = nc.tensor.transpose(ps_a[:, c * P:(c + 1) * P], stage[:, slot % 2, c * P:(c + 1) * P], ident[:])
                i.then_inc(xT_done, 1)

            def sp_stage(sp, n, slot):
                if past(n - 1):
                    sp.wait_ge(xT_done, n - 1)
                    sp.sem_inc(sp_settled, 1)
                sp.dma_start(stage[:, slot % 2, :].rearrange("p (a d) -> p a d", a=1),
                             rows_of(light_rows, n, 1)).then_inc(staged[slot % 2], 16)

            def rows_of(tensor, first, count):
                return tensor.rearrange("(g p) d -> p g d", p=P)[:, bass.ds(first, count), :]

            def pe_qk(pe, ps, col, done):
                for m in range(HC):
                    for c in range(DC):
                        i = nc.tensor.matmul(ps[:, m * P:(m + 1) * P], wqkv[:, c, col + m * P:col + (m + 1) * P], xT[:, c, :],
                                             start=(c == 0), stop=(c == DC - 1))
                i.then_inc(done, 1)

            def pe_v(pe):
                for c in range(DC):
                    i = nc.tensor.matmul(ps_b[:], xT[:, c, :], wqkv[:, c, 2 * HD:3 * HD], start=(c == 0), stop=(c == DC - 1))
                i.then_inc(v_done, 1)

            def pe_sim(pe, k, u):
                for l in range(2):
                    for e in range(2):
                        c = 2 * u + l
                        i = nc.tensor.matmul(ps_sim[:, u, 2 * e + l, :], qT[64 * e:64 * e + 64, c, k % 2, :],
                                             kT[64 * e:64 * e + 64, c, k, :], start=True, stop=True)
                i.then_inc(sim_done, 1)

            def pe_pT(pe, u):
                for blk, done in ((0, ptA_done), (1, ptB_done)):
                    for h in range(4):
                        i = nc.tensor.transpose(ps_pT[:, blk, h, :], prob[:, u, h, blk * P:(blk + 1) * P], ident[:])
                    i.then_inc(done, 1)

            def pe_pv(pe, ps, k, u, more=None):
                for h in range(4):
                    for blk, vals in ((0, vown), (1, vnb)):
                        i = nc.tensor.matmul(ps[:, (head(u, h) - 4 * u) * (DH + 1):(head(u, h) - 4 * u + 1) * (DH + 1)],
                                             probT[:, u, blk, h, :], vals[:, k, head(u, h), :],
                                             start=(blk == 0), stop=(blk == 1))
                if more:
                    i = more(pe)
                i.then_inc(pv_done, 1)

            def pe_oT(pe):
                flat = o[:].rearrange("p h d -> p (h d)")
                for c in range(HC):
                    i = nc.tensor.transpose(ps_b[:, c * P:(c + 1) * P], flat[:, c * P:(c + 1) * P], ident[:])
                i.then_inc(oT_done, 1)

            def pe_proj(pe, more=None):
                for c in range(HC):
                    i = nc.tensor.matmul(ps_b[:, 0:D], oT[:, c, :], wo[:, c, :], start=(c == 0), stop=(c == HC - 1))
                if more:
                    i = more(pe)
                i.then_inc(proj_done, 1)

            def upto(n):
                return min(n, NT) if isinstance(n, int) else n

            def pe_back(pe, g):
                pe.wait_ge(exp_done, 2 * g)
                pe_pT(pe, 1)

            def pe_tile(pe, g, k, extra=None, qkv=True):
                pe.wait_ge(k_ev, upto(g + 2))
                pe_sim(pe, k, 0)
                if past(g):
                    pe_back(pe, g)
                    pe.wait_ge(pv_ev, 2 * g - 1)
                if qkv:
                    pe_xT(pe, g + 2, k)
                pe_sim(pe, k, 1)
                pe.wait_ge(v_ev, upto(g + 2))
                if past(g):
                    pe.wait_ge(ptA_ev, 2 * g)
                    pe.wait_ge(ptB_ev, 2 * g)
                    pe_pv(pe, ps_b, (k + 3) % 4, 1)
                if qkv:
                    pe.wait_ge(xT_ev, g + 3)
                    pe_qk(pe, ps_a, 0, q_done)
                if past(g):
                    pe.wait_ge(pv_ev, 2 * g)
                    pe_oT(pe)
                pe.wait_ge(exp_done, 2 * g + 1)
                pe_pT(pe, 0)
                if qkv:
                    pe.wait_ge(q_ev, g + 3)
                    pe_qk(pe, ps_a, HD, k_done)
                if past(g):
                    pe.wait_ge(oT_ev, g)
                    pe_proj(pe, extra and extra.pe_proj)
                pe.wait_ge(ptA_ev, 2 * g + 1)
                pe.wait_ge(ptB_ev, 2 * g + 1)
                if qkv:
                    pe.wait_ge(k_ev, g + 3)
                pe_pv(pe, ps_a, k, 0, extra and extra.pe_pv)
                if past(g):
                    pe.wait_ge(proj_ev, g)
                if qkv:
                    pe_v(pe)

            def act_xT(act, n):
                act.wait_ge(xT_done, n)
                for c in range(DC):
                    i = nc.scalar.activation(xT[:, c, :], ps_a[:, c * P:(c + 1) * P], ACT.Identity,
                                             bias=gb[:, 1, c:c + 1], scale=gb[:, 0, c:c + 1])
                i.then_inc(xT_ev, 1)

            def act_q(act, n, slot):
                act.wait_ge(q_done, n)
                nc.scalar.copy(qT[:, :, slot % 2, :], ps_a[:].rearrange("p (m j) -> p m j", m=HC)).then_inc(q_ev, 1)

            def act_k(act, n, slot):
                act.wait_ge(k_done, n)
                src = ps_a[:].rearrange("p (m j) -> p m j", m=HC)
                nc.scalar.copy(kT[:, :, (slot + 3) % 4, P:P + DH], src[:, :, 0:DH])
                nc.scalar.copy(kT[:, :, (slot + 1) % 4, P + DH:2 * P], src[:, :, DH:P])
                nc.scalar.copy(kT[:, :, slot, 0:P], src).then_inc(k_ev, 1)

            def act_exp(act, n, u):
                act.wait_ge(max_done, n)
                for h in range(4):
                    i = nc.scalar.activation(prob[:, u, h, :], prob[:, u, h, :], ACT.Exp, bias=nmx[:, u, h:h + 1], scale=SCALE)
                i.then_inc(exp_done, 1)

            def act_ptB(act, n, u):
                act.wait_ge(ptB_done, n)
                nc.scalar.copy(probT[:, u, 1, :, :], ps_pT[:, 1, :, :]).then_inc(ptB_ev, 1)

            def act_tile(act, g, k, extra=None, qkv=True):
                if past(g):
                    act_ptB(act, 2 * g, 1)
                if qkv:
                    act_xT(act, g + 3)
                act_exp(act, 2 * g + 1, 0)
                if extra and extra.act_early:
                    extra.act_early(act)
                if qkv:
                    act_q(act, g + 3, (k + 2) % 4)
                act_exp(act, 2 * g + 2, 1)
                if extra and extra.act_mid:
                    extra.act_mid(act)
                act_ptB(act, 2 * g + 1, 0)
                if qkv:
                    act_k(act, g + 3, (k + 2) % 4)
                if extra and extra.act_end:
                    extra.act_end(act)

            def dve_max(dve, n, u, mask):
                dve.wait_ge(sim_done, n)
                nc.vector.memset(carry[:, u:u + 1], 0.0)
                for h in range(4):
                    i = nc.vector.tensor_tensor_reduce(prob[:, u, h, :], ps_sim[:, u, h, :], mask, 1.0, -3.4e38, ALU.add,
                                                       ALU.max, mx[:, u, h:h + 1])
                i.then_inc(nmx_in, 1)
                dve.wait_ge(nmx_in, n)
                nc.vector.tensor_scalar(nmx[:, u, :], mx[:, u, :], -SCALE, None, ALU.mult).then_inc(max_done, 1)

            def dve_ptA(dve, n, u):
                dve.wait_ge(ptA_done, n)
                nc.vector.tensor_copy(probT[:, u, 0, :, :], ps_pT[:, 0, :, :]).then_inc(ptA_ev, 1)

            def dve_pv(dve, ps, n, u, more=None):
                dve.wait_ge(pv_done, n)
                view = ps[:, 0:4 * (DH + 1)].rearrange("p (h d) -> p h d", h=4)
                nc.vector.reciprocal(rden[:, u, :], view[:, :, DH]).then_inc(rden_done, 1)
                dve.wait_ge(rden_done, n)
                i = nc.vector.tensor_tensor(o[:, 4 * u:4 * u + 4, :], view[:, :, 0:DH],
                                        rden[:, u, :].rearrange("p (h o) -> p h o", o=1).broadcast_to([P, 4, DH]),
                                        ALU.mult)
                i = more(dve) if more else i
                i.then_inc(pv_ev, 1)

            def dve_v(dve, n, slot):
                dve.wait_ge(v_done, n)
                src = ps_b[:].rearrange("p (h d) -> p h d", h=H)
                nc.vector.tensor_copy(vnb[0:DH, (slot + 3) % 4, :, 0:DH], src[0:DH])
                nc.vector.tensor_copy(vnb[DH:P, (slot + 1) % 4, :, 0:DH], src[DH:P])
                nc.vector.tensor_copy(vown[:, slot, :, 0:DH], src).then_inc(v_ev, 1)

            def dve_oT(dve, n):
                dve.wait_ge(oT_done, n)
                nc.vector.tensor_copy(oT[:].rearrange("p c j -> p (c j)"), ps_b[:]).then_inc(oT_ev, 1)

            def dve_proj(dve, n, g, more=None):
                dve.wait_ge(proj_done, n)
                if more:
                    more(dve)
                row = hres[:, bass.ds(g, 1), :].rearrange("p a d -> p (a d)")
                nc.vector.tensor_tensor(row, ps_b[:, 0:D], row, ALU.add).then_inc(proj_ev, 1)

            def dve_tile(dve, g, k, mask, extra=None, qkv=True):
                dve_max(dve, 2 * g + 1, 0, mask)
                if past(g):
                    dve_ptA(dve, 2 * g, 1)
                if extra and extra.dve_1:
                    extra.dve_1(dve)
                if past(g):
                    dve_pv(dve, ps_b, 2 * g, 1)
                dve_max(dve, 2 * g + 2, 1, mask)
                if extra and extra.dve_2:
                    extra.dve_2(dve)
                if past(g):
                    dve_oT(dve, g)
                dve_ptA(dve, 2 * g + 1, 0)
                if extra and extra.dve_3:
                    extra.dve_3(dve)
                if past(g):
                    dve_proj(dve, g, g - 1, extra and extra.dve_proj)
                if extra and extra.dve_4:
                    extra.dve_4(dve)
                dve_pv(dve, ps_a, 2 * g + 1, 0, extra and extra.dve_pv)
                if extra and extra.dve_5:
                    extra.dve_5(dve)
                if qkv:
                    dve_v(dve, g + 3, (k + 2) % 4)

            class Extra:
                pe_proj = pe_pv = act_early = act_mid = act_end = None
                dve_1 = dve_2 = dve_3 = dve_4 = dve_5 = dve_proj = dve_pv = None

            def pool_gather(pool, n, par):
                if past(n - 1):
                    pool.wait_ge(added, (n - 1) * EB)
                nc.gpsimd.tensor_copy(idc[:, par, :], ids[:, bass.ds(n * EB, EB)]).then_inc(id_copied, 1)
                pool.wait_ge(id_copied, n + 1)
                pool.sem_inc(id_settled, 1)
                for k in range(EB):
                    pool.indirect_dma_start(raw[:, par, k, :], None, ap["table"],
                                            bass.IndirectOffsetOnAxis(ap=idc[:, par, k:k + 1], axis=0)
                                            ).then_inc(gathered[par][k], 16)

            def pool_add(pool, n, par):
                for k in range(EB):
                    pool.wait_ge(gathered[par][k], n * 8 + (16 - 8 * par))
                    nc.gpsimd.tensor_tensor(hres[:, bass.ds(n * EB + k, 1), :].rearrange("p a d -> p (a d)"),
                                            raw[:, par, k, :], tokb[:], ALU.add).then_inc(added, 1)

            def tail(n):
                return isinstance(n, int) and n == NB

            def dve_stats(dve, n):
                if tail(n):
                    nc.vector.memset(carry[:, 2:3], 0.0).then_inc(var_ready, 1)
                    return
                dve.wait_ge(added, n * EB + EB)
                nc.vector.memset(carry[:, 3:4], 0.0)
                for k in range(EB):
                    i = nc.vector.bn_stats(stats1[:, k, :], hres[:, bass.ds(n * EB + k, 1), :].rearrange("p a d -> p (a d)"))
                i.then_inc(stats1_in, 1)
                dve.wait_ge(stats1_in, n + 1)
                nc.vector.memset(carry[:, 4:5], 0.0)
                for k in range(EB):
                    i = nc.vector.bn_aggr(mv[:, k, :], stats1[:, k, :])
                i.then_inc(var_ready, 1)

            def act_root(act, n):
                act.wait_ge(var_ready, n + 1)
                nc.scalar.activation(sd[:], mv[:, :, 1], ACT.Sqrt, bias=epsc[:, 0:1]).then_inc(sd_ready, 1)

            def dve_norm(dve, n, par):
                dve.wait_ge(sd_ready, n + 1)
                if past(n - 1):
                    dve.wait_ge(xn_done, n - 1)
                nc.vector.reciprocal(rstd[:], sd[:]).then_inc(rstd_ready, 1)
                dve.wait_ge(rstd_ready, n + 1)
                nc.vector.scalar_tensor_tensor(out=nmr[:], in0=mv[:, EB:2 * EB, 0], scalar=-1.0, in1=rstd[:, EB:2 * EB],
                                               op0=ALU.mult, op1=ALU.mult).then_inc(nmr_ready, 1)
                if tail(n):
                    return
                if past(n):
                    dve.wait_ge(hn_saved, n * 16)
                for k in range(EB):
                    i = nc.vector.tensor_scalar(hn[:, par, k, :], hres[:, bass.ds(n * EB + k, 1), :].rearrange("p a d -> p (a d)"),
                                                mv[:, k, 0:1], rstd[:, k:k + 1], ALU.subtract, ALU.mult)
                i.then_inc(normed, 1)

            def dve_stats2(dve, n, par):
                dve.wait_ge(normed, n + 1)
                nc.vector.memset(carry[:, 5:6], 0.0)
                for k in range(EB):
                    i = nc.vector.bn_stats(stats2[:, k, :], hn[:, par, k, :])
                i.then_inc(stats2_in, 1)
                dve.wait_ge(nmr_ready, n + 1)
                dve.wait_ge(stats2_in, n + 1)
                nc.vector.memset(carry[:, 6:7], 0.0)
                for k in range(EB):
                    nc.vector.bn_aggr(mv[:, EB + k, :], stats2[:, k, :])

            def dve_dots(dve, n, par, half):
                for k in range(2 * half, 2 * half + 2):
                    for r in range(2):
                        i = nc.vector.tensor_tensor_reduce(junk[:, 2 * k + r, :], hn[:, par, k, :], rtok[:, r, :], 1.0, 0.0,
                                                           ALU.mult, ALU.add, srow[:, r, k:k + 1])
                if half:
                    i.then_inc(dots, 1)
                    dve.wait_ge(dots, n + 1)
                    for r in range(2):
                        nc.vector.tensor_scalar(flat2(score_in[:])[:, bass.ds(n * EB + r * NT, EB)], srow[:, r, :], 1.0,
                                                None, ALU.mult)

            def act_norm2(act, n, par):
                act.wait_ge(nmr_ready, n + 1)
                if past(n - 1):
                    act.wait_ge(xn_saved, (n - 1) * 16)
                for k in range(EB):
                    i = nc.scalar.activation(xnb[:, k, :], hn[:, 1 - par, k, :], ACT.Identity, bias=nmr[:, k:k + 1],
                                             scale=rstd[:, EB + k:EB + k + 1])
                i.then_inc(xn_done, 1)

            def sp_embed(sp, n, par):
                if not tail(n):
                    sp.wait_ge(normed, n + 1)
                    sp.sem_inc(sp_settled, 1)
                    sp.dma_start(rows_of(norm_rows, n * EB, EB), hn[:, par, :, :]).then_inc(hn_saved, 16)
                if past(n):
                    sp.wait_ge(xn_done, n)
                    sp.sem_inc(sp_settled, 1)
                    sp.dma_start(rows_of(light_rows, (n - 1) * EB, EB), xnb[:]).then_inc(xn_saved, 16)

            def embed(n, k):
                e, par = Extra(), k % 2
                e.dve_1 = lambda dve: dve_stats(dve, n)
                e.act_early = lambda act: act_root(act, n)
                e.dve_2 = lambda dve: dve_dots(dve, n - 1, 1 - par, 0)
                e.dve_3 = lambda dve: dve_norm(dve, n, par)
                e.act_end = lambda act: act_norm2(act, n, par)
                if not tail(n):
                    e.dve_4 = lambda dve: dve_stats2(dve, n, par)
                e.dve_5 = lambda dve: dve_dots(dve, n - 1, 1 - par, 1)
                return e

            def pe_sum(pe, ps, at, n, given):
                pe.wait_ge(given, n)
                return nc.tensor.matmul(ps[:, at:at + R], ones[:], part[:], start=True, stop=True)

            def first_max():
                e = Extra()
                e.dve_1 = lambda dve: nc.vector.tensor_reduce(smax1[:], score_in[:], AX, ALU.max).then_inc(part_max, 1)

                def state(dve):
                    nc.vector.memset(mk[:], 0.0)
                    nc.vector.memset(thr[:], 0.0)
                    dve.wait_ge(all_max, 1)
                    nc.vector.memset(work[:], 0.0).then_inc(diff_ready, 1)
                e.dve_5 = state
                return e

            DS = 7

            def descend(i):
                e = Extra()
                base = i * DS

                def exps(act):
                    act.wait_ge(diff_ready, i + 1)
                    nc.scalar.activation(expo[:], work[:], ACT.Exp, scale=dtab[:, 0, bass.ds(i, 1)]).then_inc(exp_ready, 1)

                def sums(dve):
                    nc.vector.tensor_scalar(shift[:], mk[:], dtab[:, 2, bass.ds(i, 1)], None, ALU.add).then_inc(v, 1)
                    dve.wait_ge(exp_ready, i + 1)
                    nc.vector.tensor_reduce(part[:], expo[:], AX, ALU.add).then_inc(sum_in, 1)

                def logs(act):
                    act.wait_ge(sum_out, i + 1)
                    nc.scalar.activation(lse[:], lsum[:], ACT.Ln).then_inc(ln_done, 1)

                def update(dve):
                    dve.wait_ge(ln_done, i + 1)
                    dve.wait_ge(v, base + 1)
                    nc.vector.scalar_tensor_tensor(out=nega[:], in0=lse[:], scalar=dtab[:, 1, bass.ds(i, 1)], in1=shift[:],
                                                   op0=ALU.mult, op1=ALU.add).then_inc(v, 1)
                    dve.wait_ge(v, base + 2)
                    nc.vector.tensor_tensor(work[:], score_in[:], bc(nega[:]), ALU.subtract).then_inc(v, 1)
                    nc.vector.tensor_tensor(mk[:], smax[:], nega[:], ALU.min).then_inc(v, 1)
                    dve.wait_ge(v, base + 4)
                    nc.vector.scalar_tensor_tensor(out=negu[:], in0=work[:], scalar=0.0, in1=score_in[:],
                                                   op0=ALU.max, op1=ALU.subtract).then_inc(v, 1)
                    nc.vector.tensor_scalar(gt[:], work[:], 0.0, None, ALU.min).then_inc(v, 1)
                    dve.wait_ge(v, base + 6)
                    nc.vector.tensor_tensor(work[:], negu[:], bc(mk[:]), ALU.add).then_inc(v, 1)
                    dve.wait_ge(v, base + 7)
                    nc.vector.tensor_copy(carry[:, 15:16], mk[:, 0:1]).then_inc(diff_ready, 1)
                e.act_mid, e.dve_3, e.act_end, e.dve_5 = exps, sums, logs, update
                e.pe_proj = lambda pe: pe_sum(pe, ps_b, D, i + 1, sum_in)
                e.dve_proj = lambda dve: nc.vector.tensor_copy(lsum[:], ps_b[:, D:D + R]).then_inc(sum_out, 1)
                return e

            BS = 3
            PV_END = 4 * (DH + 1)

            def dve_test(dve, i):
                base = i * BS + ITERS * DS
                nc.vector.tensor_tensor(cand[:].bitcast(U32), thr[:].bitcast(U32),
                                        bits[:, bass.ds(i, 1)].broadcast_to([P, R]), ALU.bitwise_or).then_inc(v, 1)
                dve.wait_ge(v, base + 1)
                nc.vector.tensor_tensor(eq[:], score[:], bc(cand[:]), ALU.is_ge).then_inc(v, 1)
                dve.wait_ge(v, base + 2)
                nc.vector.tensor_reduce(part[:], eq[:], AX, ALU.add).then_inc(cnt_in, 1)

            def dve_decide(dve, i, counts):
                base = i * BS + ITERS * DS
                j = nc.vector.scalar_tensor_tensor(out=kept[:], in0=counts, scalar=float(KSEL), in1=cand[:],
                                                   op0=ALU.is_ge, op1=ALU.mult)
                return j

            def dve_next(dve, i):
                dve.wait_ge(v, i * BS + ITERS * DS + 3)
                nc.vector.tensor_tensor(thr[:], thr[:], kept[:], ALU.max).then_inc(thr_ready, 1)
                dve.wait_ge(thr_ready, i + 1)
                dve_test(dve, i + 1)

            def search(i, two):
                e = Extra()
                e.pe_proj = lambda pe: pe_sum(pe, ps_b, D, i + 1, cnt_in)
                e.dve_proj = lambda dve: dve_decide(dve, i, ps_b[:, D:D + R]).then_inc(v, 1)
                e.dve_4 = lambda dve: dve_next(dve, i)
                if two:
                    e.pe_pv = lambda pe: pe_sum(pe, ps_a, PV_END, i + 2, cnt_in)
                    e.dve_5 = lambda dve: dve_next(dve, i + 1)

                    def decide(dve):
                        j = dve_decide(dve, i + 1, ps_a[:, PV_END:PV_END + R])
                        j.then_inc(v, 1)
                        return nc.vector.memset(carry[:, 7:8], 0.0)
                    e.dve_pv = decide
                return e

            cnt = [0]

            def link(dve, i):
                cnt[0] += 1
                i.then_inc(v, 1)
                dve.wait_ge(v, cnt[0])

            def masks_of(dve):
                cnt[0] = ITERS * DS + SEARCH_BITS * BS + 2
                dve.wait_ge(cnt_in, SEARCH_BITS + 1)
                nc.vector.tensor_tensor(eq[:], score[:], bc(thr[:]), ALU.is_equal).then_inc(mask_in, 1)
                link(dve, nc.vector.tensor_tensor(gt[:], score[:], bc(thr[:]), ALU.is_gt))
                nc.vector.tensor_reduce(part[:], gt[:], AX, ALU.add).then_inc(cnt_in, 1)

            def pe_prefix(pe, mask, j):
                pe.wait_ge(mask_in, j)
                nc.tensor.matmul(ps_b[:, D:D + C], tri[:], flat2(mask[:]), start=True, stop=True)
                return nc.tensor.matmul(ps_b[:, D + C:D + 2 * C], ones[:], flat2(mask[:]), start=True, stop=True)

            def dve_prefix(dve, j):
                dve.wait_ge(pref_out, j)
                link(dve, nc.vector.tensor_tensor_scan(incl[:], consts[:, 0, :], pre[:, C:2 * C], 0.0, ALU.mult, ALU.add))
                link(dve, nc.vector.tensor_tensor(rank[:], pre[:, 0:C], incl[:], ALU.add))
                link(dve, nc.vector.tensor_tensor(rank[:], rank[:], pre[:, C:2 * C], ALU.subtract))

            def take_prefix(dve):
                nc.vector.tensor_copy(pre[:], ps_b[:, D:D + 2 * C]).then_inc(pref_out, 1)

            def select_1():
                e = Extra()
                e.pe_proj = lambda pe: pe_prefix(pe, eq, 1)
                e.dve_proj = take_prefix
                e.pe_pv = lambda pe: pe_sum(pe, ps_a, PV_END, SEARCH_BITS + 2, cnt_in)

                def wanted(dve):
                    nc.vector.tensor_scalar(need[:], ps_a[:, PV_END:PV_END + R], -1.0, float(KSEL), ALU.mult, ALU.add)
                    return nc.vector.memset(carry[:, 8:9], 0.0)
                e.dve_pv = wanted

                def choose(dve):
                    dve_prefix(dve, 1)
                    rk = rank[:].rearrange("p (r t) -> p r t", r=R)
                    link(dve, nc.vector.tensor_tensor(sel[:], rk, bc(need[:]), ALU.is_lt))
                    link(dve, nc.vector.tensor_tensor(sel[:], sel[:], eq[:], ALU.mult))
                    nc.vector.tensor_tensor(sel[:], sel[:], gt[:], ALU.add).then_inc(mask_in, 1)
                    flat = flat2(score[:])
                    link(dve, nc.vector.tensor_scalar(gain[:], flat, -1.0, 1.0, ALU.mult, ALU.add))
                    link(dve, nc.vector.tensor_tensor(gain[:], gain[:], flat, ALU.add))
                e.dve_5 = choose
                return e

            io = iota16[:].rearrange("p (o s) -> p o s", o=1).broadcast_to([P, C, 16])
            wide = lambda a: a.rearrange("p (c o) -> p c o", o=1).broadcast_to([P, C, 16])

            def select_2():
                e = Extra()
                e.pe_proj = lambda pe: pe_prefix(pe, sel, 2)
                e.dve_proj = take_prefix

                def ranks(dve):
                    dve_prefix(dve, 2)
                    selq = sel[:, 0:B, :].rearrange("p r t -> p (r t)")
                    CQ = B * T
                    link(dve, nc.vector.tensor_tensor(rf[:, 0, 0:CQ], rank[:, 0:CQ], consts[:, 1, 0:CQ], ALU.add))
                    link(dve, nc.vector.tensor_tensor(rf[:, 0, 0:CQ], rf[:, 0, 0:CQ], selq, ALU.mult))
                    link(dve, nc.vector.tensor_scalar(pos[:].rearrange("p b t -> p (b t)"), rf[:, 0, 0:CQ],
                                                      float(B * KSEL), None, ALU.add))
                    link(dve, nc.vector.tensor_scalar(incl[:], flat2(sel[:]), -4096.0, 4096.0, ALU.mult, ALU.add))
                    link(dve, nc.vector.tensor_tensor(rank[:], rank[:], incl[:], ALU.add))
                    link(dve, nc.vector.tensor_copy(ri[:, 0, :], rank[:]))
                    link(dve, nc.vector.tensor_scalar(ri[:, 1, :], ri[:, 0, :], 4, None, ALU.logical_shift_right))
                    link(dve, nc.vector.tensor_scalar(ri[:, 2, :], ri[:, 0, :], 15, None, ALU.bitwise_and))
                    link(dve, nc.vector.tensor_copy(rf[:], ri[:, 1:3, :]))
                e.dve_5 = ranks
                return e

            def select_3():
                e = Extra()
                e.dve_1 = lambda dve: link(dve, nc.vector.tensor_tensor(hi1[:], io, wide(rf[:, 0, :]), ALU.is_equal))
                e.dve_2 = lambda dve: link(dve, nc.vector.tensor_tensor(lo1[:, :, 0:16], io, wide(rf[:, 1, :]), ALU.is_equal))
                e.dve_3 = lambda dve: link(dve, nc.vector.tensor_tensor(lo1[:, :, 16:32], lo1[:, :, 0:16], wide(gain[:]),
                                                                        ALU.mult))
                e.dve_5 = lambda dve: nc.vector.tensor_tensor(lo1[:, :, 0:16], lo1[:, :, 0:16], wide(tokid[:]),
                                                              ALU.mult).then_inc(onehot, 1)
                return e

            def select_4():
                e = Extra()

                def products(pe):
                    pe.wait_ge(onehot, 1)
                    for r in range(R):
                        for t in range(T):
                            i = nc.tensor.matmul(ps_b[0:16, D + r * 32:D + r * 32 + 32], hi1[:, r * T + t, :],
                                                 lo1[:, r * T + t, :], start=(t == 0), stop=(t == T - 1))
                    return i

                def take(dve):
                    src = ps_b[0:16, D:D + R * 32].rearrange("p (r l) -> p r l", r=R)
                    nc.vector.tensor_copy(lists_f[:], src).then_inc(list_out, 1)
                    nc.vector.tensor_copy(lists_i[:], src[:, :, 0:16]).then_inc(list_out, 1)
                e.pe_proj, e.dve_proj = products, take
                return e

            def sp_lists(sp):
                sp.wait_ge(list_out, 2)
                sp.dma_start(list_idx.rearrange("(r h l) o -> h r (l o)", r=R, h=16), lists_i[:]).then_inc(list_saved, 16)
                sp.dma_start(list_gain.rearrange("(r h l) o -> h r (l o)", r=R, h=16),
                             lists_f[:, :, 16:32]).then_inc(list_saved, 16)
                sp.wait_ge(list_saved, 32)
                with nc.allow_non_contiguous_dma(reason="2048 list entries, one per partition"):
                    for h in range(KSEL // P):
                        for src, dst in ((list_idx, sel_idx), (list_gain, sel_gain)):
                            sp.dma_start(dst[:, :, h], src.rearrange("(r h p) o -> h p (r o)", r=R, p=P)[h]
                                         ).then_inc(list_back, 16)
                sp.wait_ge(list_back, 64)

            FIRST = 4
            EMBED_END = NB // 4
            G_DESCENT = NB // 4
            G_SEARCH = G_DESCENT + ITERS // 4
            PER_GROUP = (2, 2, 1, 1)
            G_SELECT = G_SEARCH + SEARCH_BITS // sum(PER_GROUP)
            between = {3: {0: lambda: embed(NB, 0), 1: first_max},
                       G_SELECT: {0: select_1, 1: select_2, 2: select_3, 3: select_4}}

            def extra_of(it, k):
                if it == 0:
                    return embed(FIRST + k, k)
                return between[it][k]() if k in between.get(it, {}) else None

            def in_embed(it, k):
                return embed(it * 4 + (FIRST + k), k)

            def in_descent(it, k):
                return descend(it * 4 + (k - 4 * G_DESCENT))

            def in_search(it, k):
                return search(it * 6 + (sum(PER_GROUP[:k]) - 6 * G_SEARCH), PER_GROUP[k] == 2)

            def groups(eng, tile, before_search=None, before_select=None, group=None):
                def alone(it):
                    if group:
                        group(it)
                    for k in range(4):
                        tile(it, k, extra_of(it, k), it < NT // 4 - 1 or k < 2)

                def loop(first, end, kind):
                    with eng.Fori(first, end) as it:
                        if group:
                            group(it)
                        for k in range(4):
                            tile(it, k, kind(it, k), True)
                alone(0)
                loop(1, EMBED_END - 1, in_embed)
                alone(EMBED_END - 1)
                loop(G_DESCENT, G_SEARCH, in_descent)
                if before_search:
                    before_search()
                loop(G_SEARCH, G_SELECT, in_search)
                if before_select:
                    before_select()
                for it in range(G_SELECT, NT // 4):
                    alone(it)

            with nc.Block() as block:
                @block.sync
                def _(sp):
                    for dst, src in ((ids[:], ap["ids"]), (tokb[:], ap["tok_bias"]), (rtok[:], ap["route_tok"])):
                        sp.dma_start(dst, src).then_inc(first_loaded, 16)
                    for dst, src in ((ident[:], ap["ident"]),
                                     (wqkv[:], ap["wqkv"].rearrange("(c p) n -> p c n", p=P)),
                                     (wo[:], ap["light_out_w"].rearrange("(c p) n -> p c n", p=P)),
                                     (gb[:], ap["ln_affine"]), (masks[:], ap["masks"]),
                                     (dtab[:], ap["descent"]), (bits[:], ap["bits"]), (consts[:], ap["row_consts"]),
                                     (tri[:], ap["tri"]), (iota16[:], ap["iota16"]), (tokid[:], ap["tokid"])):
                        sp.dma_start(dst, src).then_inc(loaded, 16)
                    sp.dma_start(heavy_rows[B * KSEL:B * KSEL + 1, :], ap["null_q"]).then_inc(null_saved, 16)
                    for n in range(FIRST):
                        if n == 2:
                            sp.wait_ge(xn_saved, 16)
                            sp_stage(sp, 0, 0)
                            sp_stage(sp, 1, 1)
                        sp_embed(sp, n, n % 2)
                    sp_stage(sp, 2, 2)

                    def sp_group(first, end, embeds):
                        with sp.Fori(first, end) as it:
                            for k in range(4):
                                sp_tile(sp, it * 4 + k, k, embeds)

                    def sp_tile(sp, g, k, embeds):
                        if embeds:
                            sp.wait_ge(xn_saved, g * 16 + (FIRST - 1) * 16)
                            sp.sem_inc(sp_settled, 1)
                        sp_stage(sp, g + 3, k + 3)
                        if embeds:
                            sp_embed(sp, g + FIRST, k % 2)
                    for k in range(4):
                        sp_tile(sp, k, k, True)
                    sp_group(1, EMBED_END - 1, True)
                    sp.wait_ge(xn_saved, (NB - 1) * 16)
                    sp_tile(sp, (EMBED_END - 1) * 4, 0, False)
                    sp_embed(sp, NB, 0)
                    sp.wait_ge(xn_saved, NB * 16)
                    for k in range(1, 4):
                        sp_tile(sp, (EMBED_END - 1) * 4 + k, k, False)
                    sp_group(EMBED_END, NT // 4 - 1, False)
                    sp_stage(sp, NT - 1, NT - 1)
                    sp_lists(sp)
                    sp.wait_ge(null_saved, 16)
                    sp.wait_ge(hn_saved, NB * 16)

                @block.gpsimd
                def _(pool):
                    pool.wait_ge(first_loaded, 48)
                    pool_gather(pool, 0, 0)
                    for n in range(2):
                        pool_gather(pool, n + 1, 1 - n)
                        pool_add(pool, n, n)
                    with pool.Fori(1, NB // 2 - 1) as it:
                        for par in range(2):
                            pool_gather(pool, it * 2 + (par + 1), 1 - par)
                            pool_add(pool, it * 2 + par, par)
                    pool_gather(pool, NB - 1, 1)
                    pool_add(pool, NB - 2, 0)
                    pool_add(pool, NB - 1, 1)
                    pool.wait_ge(part_max, 1)
                    nc.gpsimd.partition_all_reduce(smax[:], smax1[:], P, bass.bass_isa.ReduceOp.max).then_inc(all_max, 1)

                @block.tensor
                def _(pe):
                    pe.wait_ge(loaded, 16 * 11)
                    pe.wait_ge(zeroed, 1)
                    for g in range(2):
                        if g:
                            pe.wait_ge(k_ev, g)
                        pe_xT(pe, g, g)
                        pe.wait_ge(xT_ev, g + 1)
                        pe_qk(pe, ps_a, 0, q_done)
                        pe.wait_ge(q_ev, g + 1)
                        pe_qk(pe, ps_a, HD, k_done)
                        if g:
                            pe.wait_ge(v_ev, g)
                        pe_v(pe)
                    groups(pe, lambda it, k, extra, qkv: pe_tile(pe, it * 4 + k, k, extra, qkv))
                    pe_back(pe, NT)
                    pe.wait_ge(ptA_ev, 2 * NT)
                    pe.wait_ge(ptB_ev, 2 * NT)
                    pe.wait_ge(v_ev, NT)
                    pe_pv(pe, ps_b, 3, 1)
                    pe.wait_ge(pv_ev, 2 * NT)
                    pe_oT(pe)
                    pe.wait_ge(oT_ev, NT)
                    pe_proj(pe)

                @block.scalar
                def _(act):
                    act.wait_ge(eps_set, 1)
                    act.wait_ge(zeroed, 1)
                    for n in range(FIRST):
                        act_root(act, n)
                        if n:
                            act_norm2(act, n, n % 2)
                    act.wait_ge(loaded, 16 * 11)
                    for g in range(2):
                        act_xT(act, g + 1)
                        act_q(act, g + 1, g)
                        act_k(act, g + 1, g)

                    def scores():
                        act.wait_ge(score_args, 1)
                        nc.scalar.activation(score[:], gt[:], ACT.Exp, scale=1.0 / eps_last).then_inc(score_done, 1)
                    groups(act, lambda it, k, extra, qkv: act_tile(act, it * 4 + k, k, extra, qkv), scores)
                    act_ptB(act, 2 * NT, 1)

                @block.vector
                def _(dve):
                    nc.vector.memset(mv[:], 1.0)
                    nc.vector.memset(epsc[:], LN_EPS).then_inc(eps_set, 1)
                    nc.vector.memset(ones[:], 1.0)
                    nc.vector.memset(kT[:], 0.0)
                    nc.vector.memset(vown[:], 1.0)
                    nc.vector.memset(vnb[:], 1.0).then_inc(zeroed, 1)
                    dve.wait_ge(zeroed, 1)
                    dve.wait_ge(first_loaded, 48)
                    for n in range(FIRST):
                        dve_stats(dve, n)
                        dve_norm(dve, n, n % 2)
                        dve_stats2(dve, n, n % 2)
                        if n < FIRST - 1:
                            for half in range(2):
                                dve_dots(dve, n, n % 2, half)
                    dve.wait_ge(loaded, 16 * 11)
                    for g in range(2):
                        dve_v(dve, g + 1, g)

                    def edges(it):
                        if isinstance(it, int) and it == 0:
                            return
                        for m in range(2):
                            i = nc.vector.tensor_copy(edge[:, m, :], masks[:, bass.ds(it % 4 + m, 1), :]
                                                      .rearrange("p a j -> p (a j)"))
                        i.then_inc(edge_ready, 1)
                        dve.wait_ge(edge_ready, it)

                    def tile(it, k, extra, qkv):
                        if isinstance(it, int) and it == 0:
                            mask = masks[:, 0 if k == 0 else 1, :]
                        else:
                            mask = edge[:, k // 3, :] if k in (0, 3) else masks[:, 1, :]
                        dve_tile(dve, it * 4 + k, k, mask, extra, qkv)

                    def first_test():
                        nc.vector.memset(carry[:, 14:15], 0.0).then_inc(score_args, 1)
                        dve.wait_ge(score_done, 1)
                        dve_test(dve, 0)
                    groups(dve, tile, first_test, lambda: masks_of(dve), edges)
                    dve_ptA(dve, 2 * NT, 1)
                    dve_pv(dve, ps_b, 2 * NT, 1)
                    dve_oT(dve, NT)
                    dve_proj(dve, NT, NT - 1)

        with ExitStack() as ctx:
            light(ctx)

        def heavy(ctx):
            def sem(name):
                return ctx.enter_context(nc.semaphore(name))

            def st(name, shape, dt=F32):
                return sb(name, shape, dt, ctx)
            S = KSEL // P
            HH = DH // 2
            UB = S * HC
            UNITS = B * UB
            TILES = B * S
            TASKS = ["x0", "x1", "q0", "q1", "k0", "k1", "v0", "tq0", "tq1", "v1", "tk0", "tk1"]
            SPREAD = [2, 1, 1, 1, 2, 2, 2, 1]
            EACH = len(TASKS) // 2
            wq = st("hwq", [P, DC, HD])
            wkv = st("hwkv", [P, DC, 2 * HD])
            wo = st("hwo", [P, HC, D])
            gam = st("hgam", [P, DC])
            ridx = st("hridx", [P, R, S], I32)
            rows = st("hrows", [P, B, 2 * S, D])
            rope = st("hrope", [P, B, 2 * S, DH])
            sq = st("hsq", [P, 2 * S, D])
            ss = st("hss", [P, B, 2 * S])
            rn = st("hrn", [P, B, 2 * S])
            xT = st("hxT", [P, DC, 2 * KSEL])
            qk = st("hqk", [P, 2 * S, H, 2, HH])
            rot = st("hrot", [P, 2, H, 2, HH])
            val = st("hval", [P, 2, S, H, DH + 1])
            nval = st("hnval", [P, H, DH + 1])
            qT = st("hqT", [P, 2, HC, KSEL])
            kT = st("hkT", [P, 2, HC, KSEL + 1])
            mx = st("hmx", [P, 2, 2])
            nmx = st("hnmx", [P, 2, 2])
            prob = st("hprob", [P, 4, 2, KSEL + 1])
            probT = st("hprobT", [P, 2, S, 2, P])
            acc = st("hacc", [P, 2, 2, DH + 1])
            rden = st("hrden", [P, 2, 2])
            o = st("ho", [P, 2, H, DH])
            oT = st("hoT", [P, HC, P])
            res = st("hres_rows", [P, 2, D])
            ps_s = ctx.enter_context(nc.psum_tensor("hps_s", [P, 2, 2, 512], F32))
            ps_x = ctx.enter_context(nc.psum_tensor("hps_x", [P, 2, 512], F32))
            ps_p = ctx.enter_context(nc.psum_tensor("hps_p", [P, 512], F32))
            ps_v = ctx.enter_context(nc.psum_tensor("hps_v", [P, 512], F32))
            loaded, idx_ready = sem("h_loaded"), sem("h_idx_ready")
            got_rows = [sem(f"h_got_rows{b}") for b in range(B)]
            got_rope = [sem(f"h_got_rope{b}") for b in range(B)]
            ss_done, sqrt_done, rows_ready = sem("h_ss_done"), sem("h_sqrt_done"), sem("h_rows_ready")
            front_done = [sem(f"h_front_done{k}") for k in range(2)]
            front_ev = [sem(f"h_front_ev{k}") for k in range(2)]
            roped = sem("h_roped")
            sim_done, max_done, exp_done = sem("h_sim_done"), sem("h_max_done"), sem("h_exp_done")
            pT_done, pT_ev = sem("h_pT_done"), sem("h_pT_ev")
            pv_done, pv_ev = sem("h_pv_done"), sem("h_pv_ev")
            oT_done, oT_ev = sem("h_oT_done"), sem("h_oT_ev")
            pr_done, pr_ev = sem("h_pr_done"), sem("h_pr_ev")
            saved = [sem(f"h_saved{k}") for k in range(2)]
            v = sem("h_v")

            def unit(u):
                return u // UB, u % UB // HC, u % HC

            def front_tasks(step):
                b, i = divmod(step, UB)
                if b + 1 >= B:
                    return []
                first = sum(SPREAD[:i])
                return [(b + 1, n) for n in range(first, first + SPREAD[i])]

            def pe_front(pe, b, n):
                name, k = TASKS[n], n % 2
                j = int(name[-1])
                count = b * EACH + n // 2
                if count:
                    pe.wait_ge(front_ev[k], count)
                if name[0] == "x":
                    pe.wait_ge(rows_ready, b + 1)
                    for t in range(2 * S):
                        i = nc.tensor.transpose(ps_x[:, k, t * P:(t + 1) * P], rows[:, b, t, j * P:(j + 1) * P], ident[:])
                elif name[0] == "t":
                    t = j + (S if name[1] == "k" else 0)
                    pe.wait_ge(roped, b * 2 * S + t + 1)
                    flat = qk[:, t].rearrange("p h a d -> p (h a d)")
                    for c in range(HC):
                        i = nc.tensor.transpose(ps_x[:, k, c * P:(c + 1) * P], flat[:, c * P:(c + 1) * P], ident[:])
                else:
                    for bank in range(2):
                        pe.wait_ge(front_ev[bank], b * EACH + 1)
                    w = {"q": wq[:], "k": wkv[:, :, 0:HD], "v": wkv[:, :, HD:2 * HD]}[name[0]]
                    at = (0 if name[0] == "q" else KSEL) + j * P
                    for c in range(DC):
                        i = nc.tensor.matmul(ps_x[:, k, :], xT[:, c, at:at + P], w[:, c, :], start=(c == 0), stop=(c == DC - 1))
                i.then_inc(front_done[k], 1)

            def act_front(act, b, n):
                name, k = TASKS[n], n % 2
                if name[0] not in "vt":
                    return
                act.wait_ge(front_done[k], b * EACH + n // 2 + 1)
                j = int(name[-1])
                if name[0] == "v":
                    i = nc.scalar.activation(val[:, b % 2, j, :, 0:DH], ps_x[:, k, :].rearrange("p (h d) -> p h d", h=H),
                                             ACT.Copy, scale=sel_gain[:, B + b, j:j + 1])
                else:
                    dst = qT if name[1] == "q" else kT
                    i = nc.scalar.copy(dst[:, b % 2, :, j * P:(j + 1) * P], ps_x[:, k, :].rearrange("p (c j) -> p c j", c=HC))
                i.then_inc(front_ev[k], 1)

            with nc.Block() as block:
                @block.sync
                def _(sp):
                    for dst, src in ((wq[:], ap["heavy_q_w"].rearrange("(c p) n -> p c n", p=P)),
                                     (wkv[:], ap["heavy_kv_w"].rearrange("(c p) n -> p c n", p=P)),
                                     (wo[:], ap["heavy_out_w"].rearrange("(c p) n -> p c n", p=P)),
                                     (gam[:], ap["heavy_gamma"]), (nval[:, :, 0:DH], ap["null_v"])):
                        sp.dma_start(dst, src).then_inc(loaded, 16)
                    with nc.allow_non_contiguous_dma(reason="one null key column of 4 words a partition"):
                        for k in range(2):
                            sp.dma_start(kT[:, k, :, KSEL:KSEL + 1], ap["null_kT"]).then_inc(loaded, 16)
                    for e in range(TILES):
                        sp.wait_ge(pr_ev, e + 1)
                        sp.dma_start(heavy_rows[e * P:(e + 1) * P, :], res[:, e % 2, :]).then_inc(saved[e % 2], 16)
                    for k in range(2):
                        sp.wait_ge(saved[k], 16 * TILES // 2)

                @block.gpsimd
                def _(pool):
                    pool.wait_ge(idx_ready, 1)
                    for b in range(B):
                        for r in range(2):
                            for s in range(S):
                                pool.indirect_dma_start(rows[:, b, r * S + s, :], None, norm_rows,
                                                        bass.IndirectOffsetOnAxis(ap=sel_idx[:, r * B + b, s:s + 1], axis=0)
                                                        ).then_inc(got_rows[b], 16)
                        for r in range(2):
                            for s in range(S):
                                pool.indirect_dma_start(rope[:, b, r * S + s, :], None, ap["rope"],
                                                        bass.IndirectOffsetOnAxis(ap=ridx[:, r * B + b, s:s + 1], axis=0)
                                                        ).then_inc(got_rope[b], 16)

                @block.scalar
                def _(act):
                    def act_norm(n, b0, b1):
                        act.wait_ge(ss_done, n)
                        nc.scalar.activation(ss[:, b0:b1], ss[:, b0:b1], ACT.Sqrt).then_inc(sqrt_done, 1)
                    act.wait_ge(loaded, 112)
                    act.wait_ge(idx_ready, 1)
                    act_norm(1, 0, 1)
                    for n in range(len(TASKS)):
                        act_front(act, 0, n)
                    act_norm(2, 1, B)
                    for step in range(UNITS):
                        act.wait_ge(max_done, step + 1)
                        if step >= 4:
                            act.wait_ge(pv_ev, step - 3)
                        for e in range(2):
                            i = nc.scalar.activation(prob[:, step % 4, e, :], ps_s[:, step % 2, e, 0:KSEL + 1], ACT.Exp,
                                                     bias=nmx[:, step % 2, e:e + 1], scale=SCALE)
                        i.then_inc(exp_done, 1)
                        for b, n in front_tasks(step):
                            act_front(act, b, n)

                @block.tensor
                def _(pe):
                    pe.wait_ge(loaded, 112)
                    for n in range(len(TASKS)):
                        pe_front(pe, 0, n)
                    for step in range(UNITS + 4):
                        if step < UNITS:
                            b, s, c = unit(step)
                            if step % UB == 0:
                                for k in range(2):
                                    pe.wait_ge(front_ev[k], (b + 1) * EACH)
                            for e in range(2):
                                i = nc.tensor.matmul(ps_s[:, step % 2, e, 0:KSEL + 1],
                                                     qT[64 * e:64 * e + 64, b % 2, c, s * P:(s + 1) * P],
                                                     kT[64 * e:64 * e + 64, b % 2, c, :], start=True, stop=True)
                            i.then_inc(sim_done, 1)
                        if 1 <= step <= UNITS:
                            u = step - 1
                            pe.wait_ge(exp_done, u + 1)
                            if u:
                                pe.wait_ge(pT_ev, u)
                            if step >= 7 and (step - 7) % HC == 0:
                                pe.wait_ge(oT_ev, (step - 7) // HC + 1)
                            for e in range(2):
                                for j in range(S):
                                    i = nc.tensor.transpose(ps_p[:, (j * 2 + e) * P:(j * 2 + e + 1) * P],
                                                            prob[:, u % 4, e, j * P:(j + 1) * P], ident[:])
                            i.then_inc(pT_done, 1)
                        for b, n in front_tasks(step) if step < UNITS else []:
                            pe_front(pe, b, n)
                        if 2 <= step <= UNITS + 1:
                            u = step - 2
                            b, s, c = unit(u)
                            pe.wait_ge(pT_ev, u + 1)
                            if u:
                                pe.wait_ge(pv_ev, u)
                            if step >= 8 and (step - 8) % HC == 0:
                                pe.wait_ge(pr_ev, (step - 8) // HC + 1)
                            for e in range(2):
                                for j in range(S):
                                    i = nc.tensor.matmul(ps_v[:, e * (DH + 1):(e + 1) * (DH + 1)], probT[:, u % 2, j, e, :],
                                                         val[:, b % 2, j, 2 * c + e, :], start=(j == 0), stop=(j == S - 1))
                            i.then_inc(pv_done, 1)
                        if step >= 6 and (step - 6) % HC == 0:
                            e = (step - 6) // HC
                            pe.wait_ge(pv_ev, (e + 1) * HC)
                            pe.wait_ge(pT_ev, min(step, UNITS))
                            flat = o[:, e % 2].rearrange("p h d -> p (h d)")
                            for c in range(HC):
                                i = nc.tensor.transpose(ps_p[:, c * P:(c + 1) * P], flat[:, c * P:(c + 1) * P], ident[:])
                            i.then_inc(oT_done, 1)
                        if step >= 7 and (step - 7) % HC == 0:
                            e = (step - 7) // HC
                            pe.wait_ge(oT_ev, e + 1)
                            pe.wait_ge(pv_ev, min(step - 1, UNITS))
                            for c in range(HC):
                                i = nc.tensor.matmul(ps_v[:, 0:D], oT[:, c, :], wo[:, c, :], start=(c == 0), stop=(c == HC - 1))
                            i.then_inc(pr_done, 1)

                @block.vector
                def _(dve):
                    cnt = [0]

                    def link(i):
                        cnt[0] += 1
                        i.then_inc(v, 1)
                        dve.wait_ge(v, cnt[0])

                    def dve_norm(n, b0, b1):
                        for b in range(b0, b1):
                            dve.wait_ge(got_rows[b], 16 * 2 * S)
                            for t in range(2 * S):
                                i = nc.vector.tensor_tensor_reduce(sq[:, t, :], rows[:, b, t, :], rows[:, b, t, :], 1.0, 0.0,
                                                                   ALU.mult, ALU.add, ss[:, b, t:t + 1])
                            if b < b1 - 1:
                                link(i)
                        i.then_inc(ss_done, 1)
                        dve.wait_ge(sqrt_done, n)
                        link(nc.vector.tensor_scalar(ss[:, b0:b1], ss[:, b0:b1], 1e-12, None, ALU.max))
                        link(nc.vector.reciprocal(rn[:, b0:b1], ss[:, b0:b1]))
                        for b in range(b0, b1):
                            for t in range(2 * S):
                                i = nc.vector.tensor_scalar(rows[:, b, t, :], rows[:, b, t, :], rn[:, b, t:t + 1],
                                                            float(D) ** 0.5, ALU.mult, ALU.mult)
                            i.then_inc(rows_ready, 1)

                    def dve_front(b, n):
                        name, k = TASKS[n], n % 2
                        if name[0] not in "xqk":
                            return
                        dve.wait_ge(front_done[k], b * EACH + n // 2 + 1)
                        j = int(name[-1])
                        if name[0] == "x":
                            nc.vector.tensor_scalar(xT[:, j, :], ps_x[:, k, :], gam[:, j:j + 1], None, ALU.mult
                                                    ).then_inc(front_ev[k], 1)
                            return
                        t = j + (S if name[0] == "k" else 0)
                        if t == 0:
                            dve.wait_ge(got_rope[b], 16 * 2 * S)
                        src = ps_x[:, k, :].rearrange("p (h a d) -> p h a d", h=H, a=2)
                        cos = rope[:, b, t, 0:HH].rearrange("p (o d) -> p o d", o=1)
                        sin = rope[:, b, t, HH:DH].rearrange("p (o d) -> p o d", o=1).broadcast_to([P, H, HH])
                        turned = rot[:, t % 2]
                        nc.vector.tensor_tensor(qk[:, t].rearrange("p h a d -> p (h a) d"),
                                                src.rearrange("p h a d -> p (h a) d"),
                                                cos.broadcast_to([P, 2 * H, HH]), ALU.mult)
                        nc.vector.tensor_tensor(turned[:, :, 0, :], src[:, :, 1, :], sin, ALU.mult)
                        count = b * EACH + n // 2
                        nc.vector.tensor_tensor(turned[:, :, 1, :], src[:, :, 0, :], sin, ALU.mult).then_inc(front_ev[k], 1)
                        dve.wait_ge(front_ev[k], count + 1)
                        nc.vector.tensor_tensor(qk[:, t, :, 0, :], qk[:, t, :, 0, :], turned[:, :, 0, :], ALU.subtract)
                        nc.vector.tensor_tensor(qk[:, t, :, 1, :], qk[:, t, :, 1, :], turned[:, :, 1, :], ALU.add
                                                ).then_inc(roped, 1)

                    nc.vector.memset(val[:], 1.0)
                    nc.vector.memset(nval[:, :, DH:DH + 1], 1.0)
                    nc.vector.tensor_scalar(ridx[:], sel_idx[:], N - 1, None, ALU.bitwise_and).then_inc(idx_ready, 1)
                    dve.wait_ge(loaded, 112)
                    dve_norm(1, 0, 1)
                    for n in range(len(TASKS)):
                        dve_front(0, n)
                    dve_norm(2, 1, B)
                    for step in range(UNITS + 4):
                        if step < UNITS:
                            dve.wait_ge(sim_done, step + 1)
                            link(nc.vector.tensor_reduce(mx[:, step % 2, :], ps_s[:, step % 2, :, 0:KSEL + 1], AX, ALU.max))
                            nc.vector.tensor_scalar(nmx[:, step % 2, :], mx[:, step % 2, :], -SCALE, None, ALU.mult
                                                    ).then_inc(max_done, 1)
                        if 1 <= step <= UNITS:
                            u = step - 1
                            dve.wait_ge(pT_done, u + 1)
                            nc.vector.tensor_copy(probT[:, u % 2].rearrange("p j e q -> p (j e q)"), ps_p[:]).then_inc(pT_ev, 1)
                        for b, n in front_tasks(step) if step < UNITS else []:
                            dve_front(b, n)
                        if 2 <= step <= UNITS + 1:
                            u = step - 2
                            _, s, c = unit(u)
                            dve.wait_ge(pv_done, u + 1)
                            for e in range(2):
                                i = nc.vector.scalar_tensor_tensor(out=acc[:, u % 2, e, :], in0=nval[:, 2 * c + e, :],
                                                                   scalar=prob[:, u % 4, e, KSEL:KSEL + 1],
                                                                   in1=ps_v[:, e * (DH + 1):(e + 1) * (DH + 1)],
                                                                   op0=ALU.mult, op1=ALU.add)
                            link(i)
                            link(nc.vector.reciprocal(rden[:, u % 2, :], acc[:, u % 2, :, DH]))
                            nc.vector.tensor_tensor(o[:, (u // HC) % 2, 2 * c:2 * c + 2, :], acc[:, u % 2, :, 0:DH],
                                                    rden[:, u % 2, :].rearrange("p (h o) -> p h o", o=1)
                                                    .broadcast_to([P, 2, DH]), ALU.mult).then_inc(pv_ev, 1)
                        if step >= 6 and (step - 6) % HC == 0:
                            e = (step - 6) // HC
                            dve.wait_ge(oT_done, e + 1)
                            nc.vector.tensor_copy(oT[:].rearrange("p c j -> p (c j)"), ps_p[:]).then_inc(oT_ev, 1)
                        if step >= 7 and (step - 7) % HC == 0:
                            e = (step - 7) // HC
                            b, s = divmod(e, S)
                            dve.wait_ge(pr_done, e + 1)
                            if e >= 2:
                                dve.wait_ge(saved[e % 2], 16 * (e // 2))
                            nc.vector.tensor_scalar(res[:, e % 2, :], ps_v[:, 0:D], sel_gain[:, b, s:s + 1], None, ALU.mult
                                                    ).then_inc(pr_ev, 1)

        with ExitStack() as ctx:
            heavy(ctx)

        def ffn(ctx):
            def sem(name):
                return ctx.enter_context(nc.semaphore(name))

            def st(name, shape, dt=F32):
                return sb(name, shape, dt, ctx)
            GT = 4
            ZB = 4
            GN = GT * P
            NG = T // GT
            w = st("fw", [P, 8, DC, D])
            bias = st("fbias", [P, 4, DC])
            bo = st("fbo", [P, D])
            idc = st("fidc", [P, B, GT], I32)
            raw = st("fraw", [P, B, GT, D])
            stats = st("fstats", [P, B * GT, 6])
            mv = st("fmv", [P, B * GT, 2])
            epsc = st("fepsc", [P, 1])
            sd = st("fsd", [P, B * GT])
            rstd = st("frstd", [P, B * GT])
            carry = st("fcarry", [P, 1])
            stage = st("fstage", [P, 2, GT, D])
            xT = st("fxT", [P, B, DC, GN])
            cT = st("fcT", [P, DC, GN])
            gates = st("fgates", [P, 3, GN])
            t1 = st("ft1", [P, GN])
            cf = st("fcf", [P, GT, D])
            z = st("fz", [P, ZB, 2, D])
            y = st("fy", [P, ZB, 2, D])
            ps_g = ctx.enter_context(nc.psum_tensor("fps_g", [P, 6, 512], F32))
            ps_t = ctx.enter_context(nc.psum_tensor("fps_t", [P, 2, 512], F32))
            loaded, c_init = sem("f_loaded"), sem("f_c_init")
            idx_copied, idx_settled = sem("f_idx_copied"), sem("f_idx_settled")
            got = [sem(f"f_got{b}") for b in range(B)]
            merged, stats_done, var_ready = sem("f_merged"), sem("f_stats_done"), sem("f_var_ready")
            eps_set, sd_ready, rstd_ready = sem("f_eps_set"), sem("f_sd_ready"), sem("f_rstd_ready")
            xT_done, xT_ev = sem("f_xT_done"), sem("f_xT_ev")
            gate_done, gate_ev = sem("f_gate_done"), sem("f_gate_ev")
            c_ready, v = sem("f_c_ready"), sem("f_v")
            staged = sem("f_staged")
            cf_done, cf_ev = sem("f_cf_done"), sem("f_cf_ev")
            out_done, z_ready, tanh_done, y_ready = (sem("f_out_done"), sem("f_z_ready"), sem("f_tanh_done"),
                                                     sem("f_y_ready"))
            saved = [sem(f"f_saved{k}") for k in range(ZB)]
            NO = B * GT // 2
            M = B * GT
            FREE = ZB
            pos_v = pos[:]

            def x_bank(b, c):
                return ps_t[:, c, :] if b else ps_g[:, 4 + c, :]

            def out_bank(n):
                return ps_t[:, n % 4, :] if n % 4 < 2 else ps_g[:, n % 4, :]

            def pe_transposes(pe, g, b):
                pe.wait_ge(staged, g * B + (b + 1))
                for c in range(DC):
                    if b > 1:
                        pe.wait_ge(xT_ev, g * (B * DC) + ((b - 1) * DC + c + 1))
                    for t in range(GT):
                        i = nc.tensor.transpose(x_bank(b, c)[:, t * P:(t + 1) * P],
                                                stage[:, b % 2, t, c * P:(c + 1) * P], ident[:])
                    i.then_inc(xT_done, 1)

            def pe_group(pe, g, last):

                def x_part(b):
                    pe.wait_ge(xT_ev, g * (B * DC) + (b + 1) * DC)
                    for m in range(DC):
                        for q in range(3):
                            if b:
                                pe.wait_ge(gate_ev, g * (B * 6) + ((b - 1) * 6 + m * 3 + q + 1))
                            for c in range(DC):
                                nc.tensor.matmul(ps_g[:, m * 3 + q, :], w[:, q, c, m * P:(m + 1) * P], xT[:, b, c, :],
                                                 start=(c == 0), stop=False)

                def c_part(b):
                    pe.wait_ge(c_ready, g * (B + 1) + (b + 1))
                    for m in range(DC):
                        for q in range(3):
                            for c in range(DC):
                                i = nc.tensor.matmul(ps_g[:, m * 3 + q, :], w[:, 4 + q, c, m * P:(m + 1) * P],
                                                     cT[:, c, :], start=False, stop=(c == DC - 1))
                            i.then_inc(gate_done, 1)

                x_part(0)
                for b in range(B):
                    if b + 1 < B:
                        pe_transposes(pe, g, b + 1)
                    c_part(b)
                    if b + 1 < B:
                        x_part(b + 1)
                pe.wait_ge(xT_ev, g * (B * DC) + B * DC)
                for n in range(NO):
                    b, h = divmod(n, GT // 2)
                    if n in (2, 3):
                        pe.wait_ge(gate_ev, g * (B * 6) + ((B - 1) * 6 + n + 1))
                    if n == 4:
                        pe.wait_ge(c_ready, g * (B + 1) + (B + 1))
                        for h2 in range(GT // 2):
                            for t in range(2):
                                for c in range(DC):
                                    j = 2 * h2 + t
                                    i = nc.tensor.matmul(ps_g[:, h2, t * D:(t + 1) * D], cT[:, c, j * P:(j + 1) * P],
                                                         w[:, 7, c, :], start=(c == 0), stop=(c == DC - 1))
                            i.then_inc(cf_done, 1)
                        if not last:
                            pe.wait_ge(gate_ev, g * (B * 6) + B * 6)
                            pe_transposes(pe, g + 1, 0)
                    if n >= 4:
                        pe.wait_ge(z_ready, g * NO + (n - 3))
                    for t in range(2):
                        for c in range(DC):
                            j = 2 * h + t
                            i = nc.tensor.matmul(out_bank(n)[:, t * D:(t + 1) * D], xT[:, b, c, j * P:(j + 1) * P],
                                                 w[:, 3, c, :], start=(c == 0), stop=(c == DC - 1))
                    i.then_inc(out_done, 1)
                pe.wait_ge(z_ready, g * NO + NO)

            def act_root(act, n):
                act.wait_ge(var_ready, n)
                nc.scalar.activation(sd[:], mv[:, :, 1], ACT.Sqrt, bias=epsc[:, 0:1]).then_inc(sd_ready, 1)

            def act_group(act, g, last):
                for b in range(B):
                    for m in range(DC):
                        for q in range(3):
                            n = b * 6 + m * 3 + q
                            act.wait_ge(gate_done, g * (B * 6) + (n + 1))
                            if q == 0 and n:
                                act.wait_ge(v, g * (B * DC * 3) + (b * DC + m) * 3)
                            nc.scalar.activation(gates[:, q, :], ps_g[:, m * 3 + q, :],
                                                 ACT.Tanh if q == 2 else ACT.Sigmoid, bias=bias[:, q, m:m + 1]
                                                 ).then_inc(gate_ev, 1)
                if not last:
                    act_root(act, g + 2)
                for n in range(NO):
                    act.wait_ge(z_ready, g * NO + (n + 1))
                    nc.scalar.activation(z[:, n % ZB], z[:, n % ZB], ACT.Tanh).then_inc(tanh_done, 1)
                act.wait_ge(v, (g + 1) * (B * DC * 3))

            def row(g, j):
                b, t = divmod(j, GT)
                return hres[:, bass.ds(g * GT + (b * T + t), 1), :].rearrange("p a d -> p (a d)")

            def dve_merge(dve, g, js):
                for j in js:
                    b, t = divmod(j, GT)
                    if t == 0:
                        dve.wait_ge(got[b], (g + 1) * (16 * GT))
                    nc.vector.tensor_tensor(row(g, j), row(g, j), raw[:, b, t, :], ALU.add).then_inc(merged, 1)
                dve.wait_ge(merged, g * M + (js[-1] + 1))
                nc.vector.memset(carry[:], 0.0)
                for j in js:
                    nc.vector.bn_stats(stats[:, j, :], row(g, j)).then_inc(stats_done, 1)
                dve.wait_ge(stats_done, g * M + (js[-1] + 1))
                nc.vector.memset(carry[:], 0.0)
                for j in js:
                    i = nc.vector.bn_aggr(mv[:, j, :], stats[:, j, :])
                if js[-1] == M - 1:
                    i.then_inc(var_ready, 1)

            def dve_rstd(dve, n):
                dve.wait_ge(sd_ready, n)
                nc.vector.reciprocal(rstd[:], sd[:]).then_inc(rstd_ready, 1)
                dve.wait_ge(rstd_ready, n)

            def dve_normalise(dve, g, b):
                for t in range(GT):
                    j = b * GT + t
                    i = nc.vector.tensor_scalar(stage[:, b % 2, t, :], row(g, j), mv[:, j, 0:1], rstd[:, j:j + 1],
                                                ALU.subtract, ALU.mult)
                i.then_inc(staged, 1)

            def dve_evacuate_x(dve, g, b):
                for c in range(DC):
                    dve.wait_ge(xT_done, g * (B * DC) + (b * DC + c + 1))
                    nc.vector.tensor_copy(xT[:, b, c, :], x_bank(b, c)).then_inc(xT_ev, 1)

            def dve_group(dve, g, last):
                nc.vector.memset(t1[:], 0.0).then_inc(c_init, 1)
                dve.wait_ge(c_init, g + 1)
                for c in range(DC):
                    i = nc.vector.tensor_scalar(cT[:, c, :], t1[:], bias[:, 3, c:c + 1], None, ALU.add)
                i.then_inc(c_ready, 1)

                dve_normalise(dve, g, 1)
                for b in range(B):
                    if b + 1 < B:
                        dve_evacuate_x(dve, g, b + 1)
                    if b + 2 < B:
                        dve_normalise(dve, g, b + 2)
                    if b >= 2 and not last:
                        dve.wait_ge(staged, g * B + B)
                        dve_merge(dve, g + 1, range((b - 2) * M // 2, (b - 1) * M // 2))
                    dve.wait_ge(gate_done, g * (B * 6) + (b + 1) * 6)
                    for m in range(DC):
                        k = (b * DC + m) * 3
                        dve.wait_ge(gate_ev, g * (B * 6) + (b * 6 + m * 3 + 3))
                        nc.vector.tensor_tensor(t1[:], gates[:, 1, :], gates[:, 2, :], ALU.mult).then_inc(v, 1)
                        nc.vector.tensor_tensor(cT[:, m, :], cT[:, m, :], gates[:, 0, :], ALU.mult).then_inc(v, 1)
                        dve.wait_ge(v, g * (B * DC * 3) + (k + 2))
                        i = nc.vector.tensor_tensor(cT[:, m, :], cT[:, m, :], t1[:], ALU.add)
                        i.then_inc(v, 1)
                    dve.wait_ge(v, g * (B * DC * 3) + (b + 1) * DC * 3)
                    nc.vector.tensor_copy(t1[:, 0:1], cT[:, 0, 0:1]).then_inc(c_ready, 1)
                if not last:
                    dve_rstd(dve, g + 2)
                    dve_normalise(dve, g + 1, 0)
                for h in range(GT // 2):
                    dve.wait_ge(cf_done, g * 2 + (h + 1))
                    nc.vector.tensor_tensor(cf[:, 2 * h:2 * h + 2, :], ps_g[:, h, :].rearrange("p (t d) -> p t d", t=2),
                                            bo[:].rearrange("p (o d) -> p o d", o=1).broadcast_to([P, 2, D]), ALU.add
                                            ).then_inc(cf_ev, 1)
                dve.wait_ge(cf_ev, g * 2 + 2)
                for n in range(NO):
                    b, h = divmod(n, GT // 2)
                    if n == 4 and not last:
                        dve_evacuate_x(dve, g + 1, 0)
                    dve.wait_ge(out_done, g * NO + (n + 1))
                    dve.wait_ge(y_ready, g * NO + (n + 1))
                    nc.vector.tensor_tensor(z[:, n % ZB], out_bank(n).rearrange("p (t d) -> p t d", t=2),
                                            cf[:, 2 * h:2 * h + 2, :], ALU.add).then_inc(z_ready, 1)

            def pool_gather(pool, g):
                nc.gpsimd.tensor_copy(idc[:], pos_v[:, :, bass.ds(g * GT, GT)]).then_inc(idx_copied, 1)
                pool.wait_ge(idx_copied, g + 1)
                pool.sem_inc(idx_settled, 1)
                for b in range(B):
                    for t in range(GT):
                        pool.indirect_dma_start(raw[:, b, t, :], None, heavy_rows,
                                                bass.IndirectOffsetOnAxis(ap=idc[:, b, t:t + 1], axis=0)
                                                ).then_inc(got[b], 16)

            def pool_group(pool, g, last):
                if not last:
                    pool.wait_ge(merged, (g + 1) * M)
                    pool_gather(pool, g + 1)
                for n in range(NO):
                    b, h = divmod(n, GT // 2)
                    pool.wait_ge(tanh_done, g * NO + (n + 1))
                    if n >= ZB:
                        pool.wait_ge(saved[n % ZB], g * (16 * NO // ZB) + 16 * (n // ZB))
                    nc.gpsimd.tensor_tensor(y[:, n % ZB].rearrange("p t d -> p (t d)"),
                                            z[:, n % ZB].rearrange("p t d -> p (t d)"),
                                            hres[:, bass.ds(g * GT + (b * T + 2 * h), 2), :].rearrange("p t d -> p (t d)"),
                                            ALU.add).then_inc(y_ready, 1)
                for k in range(ZB):
                    pool.wait_ge(saved[k], (g + 1) * (16 * NO // ZB))

            with nc.Block() as block:
                @block.sync
                def _(sp):
                    for dst, src in ((w[:], ap["ffn_w"]), (bias[:], ap["ffn_bias"]), (bo[:], ap["ffn_bo"])):
                        sp.dma_start(dst, src).then_inc(loaded, 16)
                    rows = out.rearrange("b (t p) d -> p (b t) d", p=P)
                    with sp.Fori(0, NG) as g:
                        for n in range(NO):
                            b, h = divmod(n, GT // 2)
                            sp.wait_ge(y_ready, g * NO + (FREE + n + 1))
                            sp.dma_start(rows[:, bass.ds(g * GT + (b * T + 2 * h), 2), :], y[:, n % ZB]).then_inc(saved[n % ZB], 16)
                    for k in range(ZB):
                        sp.wait_ge(saved[k], 16 * NG * NO // ZB)

                @block.tensor
                def _(pe):
                    pe.wait_ge(loaded, 48)
                    pe_transposes(pe, 0, 0)
                    with pe.Fori(0, NG - 1) as g:
                        pe_group(pe, g, False)
                    pe_group(pe, NG - 1, True)

                @block.scalar
                def _(act):
                    act.wait_ge(loaded, 48)
                    act.wait_ge(eps_set, 1)
                    act_root(act, 1)
                    with act.Fori(0, NG - 1) as g:
                        act_group(act, g, False)
                    act_group(act, NG - 1, True)

                @block.vector
                def _(dve):
                    nc.vector.memset(epsc[:], LN_EPS).then_inc(eps_set, 1)
                    dve.wait_ge(loaded, 48)
                    dve_merge(dve, 0, range(M))
                    dve_rstd(dve, 1)
                    dve_normalise(dve, 0, 0)
                    dve_evacuate_x(dve, 0, 0)
                    with dve.Fori(0, NG - 1) as g:
                        dve_group(dve, g, False)
                    dve_group(dve, NG - 1, True)

                @block.gpsimd
                def _(pool):
                    pool.sem_inc(y_ready, FREE)
                    pool_gather(pool, 0)
                    with pool.Fori(0, NG - 1) as g:
                        pool_group(pool, g, False)
                    pool_group(pool, NG - 1, True)

        with ExitStack() as ctx:
            ffn(ctx)


def constants():
    f = np.float32
    eps, _ = descent_eps()
    e = np.array(eps, np.float64)
    descent = np.stack([-1.0 / e, e, -e * LOGK]).astype(f)
    bits = np.array([1 << (SEARCH_BITS - 1 - i) for i in range(SEARCH_BITS)] + [0], np.uint32)
    col = np.arange(R * T)
    not_first = (col % T != 0).astype(f)
    row_base = ((col // T) * KSEL - B * KSEL).astype(f)
    p = np.arange(P)[:, None]
    tokid = (((col // T) % B) * N + (col % T) * P + p).astype(f)
    masks = np.zeros((P, 5, 2 * P), f)
    q = np.arange(P)[:, None]
    own = np.abs(q - np.arange(P)[None]) > W
    nxt = (P + np.arange(W)[None] - q) > W
    prv = (q - (np.arange(W)[None] + W - P)) > W
    for m in range(5):
        masks[:, m, 0:P][own] = NEG
        masks[:, m, P:P + W][nxt | (np.zeros_like(nxt) | (m == 4))] = NEG
        masks[:, m, P + W:][prv | (np.zeros_like(prv) | (m == 0))] = NEG
    ang = (np.arange(N, dtype=f)[:, None] * (1.0 / (10000.0 ** (np.arange(0, DH, 2) / DH))).astype(f)[None]).astype(f)
    bcast = lambda a: np.ascontiguousarray(np.broadcast_to(a, (P,) + a.shape))
    return {
        "descent": bcast(descent), "bits": bcast(bits), "row_consts": bcast(np.stack([not_first, row_base])),
        "tri": np.triu(np.ones((P, P), f), 1), "iota16": bcast(np.arange(16, dtype=f)), "tokid": tokid,
        "ident": np.eye(P, dtype=f),
        "masks": masks.astype(np.dtype("bfloat16")),
        "rope": np.concatenate([np.cos(ang.astype(np.float64)), np.sin(ang.astype(np.float64))], 1).astype(f),
    }


def kernel(**inputs):
    import concourse.bacc as bacc
    from concourse.bass_utils import run_bass_kernel_spmd as run

    a = {k: np.asarray(v) for k, v in inputs.items()}
    at = lambda n: a["L0_attn_" + n]
    ff = lambda n: a["L0_ffn_" + n]
    rows = lambda v: np.ascontiguousarray(np.broadcast_to(v, (P,) + v.shape))
    chunks = lambda v: v.reshape(DC, P).T
    mats = [ff("wf").T, ff("wi").T, ff("wc").T, ff("wo").T, ff("uf").T, ff("ui").T, ff("uc").T, ff("uo").T]
    kv = at("heavy_kv_w").reshape(H, 2, DH, D)
    null = at("heavy_null_kv")
    arrays = {
        "ids": a["x"].reshape(NT, P).T,
        "table": a["L0_tok_weight"].T,
        "tok_bias": rows(a["L0_tok_bias"]),
        "route_tok": rows(np.stack([at("q_route_tok"), at("kv_route_tok")])),
        "null_q": at("null_q_token").reshape(1, D),
        "wqkv": at("light_qkv_w"),
        "light_out_w": at("light_out_w"),
        "ln_affine": np.stack([chunks(at("ln_gamma")), chunks(at("ln_beta"))], 1),
        "heavy_q_w": at("heavy_q_w"),
        "heavy_kv_w": kv.transpose(3, 1, 0, 2).reshape(D, 2 * HD),
        "heavy_out_w": at("heavy_out_w"),
        "heavy_gamma": chunks(at("heavy_gamma")),
        "null_kT": null[0].reshape(HC, P).T.reshape(P, HC, 1),
        "null_v": rows(null[1].reshape(H, DH)),
        "ffn_w": np.stack([m.reshape(DC, P, D).transpose(1, 0, 2) for m in mats], 1),
        "ffn_bias": np.stack([chunks(ff("bf")), chunks(ff("bi")), chunks(ff("bc")), chunks(ff("in_c"))], 1),
        "ffn_bo": rows(ff("bo")),
    }
    arrays.update(constants())
    nc = bacc.Bacc("TRN2", target_bir_lowering=False, num_devices=1)
    ap, feeds = {}, {}
    for name, v in arrays.items():
        v = np.ascontiguousarray(v)
        feeds[f"in_{name}"] = v
        ap[name] = nc.dram_tensor(f"in_{name}", v.shape, mybir.dt.from_np(v.dtype), kind="ExternalInput").ap()
    out = nc.dram_tensor("out", (B, N, D), F32, kind="ExternalOutput").ap()
    lm_tower(nc, ap, out)
    return run(nc, [feeds], core_ids=[0]).results[0]["out"]
```

```python
from contextlib import ExitStack
import math

import numpy as np
import concourse.bass as bass
from concourse import mybir

P = 128
B, N, D = 4, 2048, 256
T = N // P
NT = B * T
DC = D // P
H, DH = 8, 64
HD = H * DH
HC = HD // P
KSEL = 256
W = 64
ITERS, EPS0, EPS_END, DECAY = 20, 4.0, 0.03, 0.7
SEARCH_BITS = 30
EB = 4
NB = B * (N // P) // EB
LOGK = math.log(min(KSEL * 9.0 / 8.0, N))
LN_EPS = 1e-5
SCALE = DH ** -0.5
R = 2 * B
NEG = -3.0e38

F32 = mybir.dt.float32
BF16 = mybir.dt.bfloat16
I32 = mybir.dt.int32
U32 = mybir.dt.uint32
ALU = mybir.AluOpType
ACT = mybir.ActivationFunctionType
AX = mybir.AxisListType.X


def descent_eps():
    out, cur = [], max(EPS0, EPS_END)
    for _ in range(ITERS):
        out.append(cur)
        cur = max(cur * DECAY, EPS_END)
    return out, cur


def past(v):
    return not (isinstance(v, int) and v < 1)


def lm_tower(nc, ap, out):
    with ExitStack() as top:
        def sb(name, shape, dt=F32, ctx=top):
            return ctx.enter_context(nc.sbuf_tensor(name, shape, dt))

        def dram(name, shape, dt=F32):
            return nc.dram_tensor(name, shape, dt, kind="Internal").ap()

        norm_rows = dram("norm_rows", [B * N, D])
        light_rows = dram("light_rows", [B * N, D])
        heavy_rows = [dram(f"heavy_rows{b}", [KSEL + 1, D]) for b in range(B)]
        list_idx = dram("list_idx", [R * KSEL, 1], I32)
        list_gain = dram("list_gain", [R * KSEL, 1])

        hres = sb("hres", [P, NT, D])
        ident = sb("ident", [P, P])
        pos = sb("pos", [P, B, T], I32)
        table_in = sb("table_in", [P, 1])
        sel_idx = sb("sel_idx", [P, R, KSEL // P], I32)
        sel_gain = sb("sel_gain", [P, R, KSEL // P])

        h_wkv = sb("h_wkv", [P, DC, 2 * HD])
        h_wqo = sb("h_wqo", [P, 2, DC * HD])
        h_rows0 = sb("h_rows0", [P, 2 * (KSEL // P), D])
        h_rope0 = sb("h_rope0", [P, 2 * (KSEL // P), DH])
        ridx = sb("ridx", [P, R, KSEL // P], I32)
        h_weights, idx_ready = top.enter_context(nc.semaphore("h_weights")), top.enter_context(nc.semaphore("h_idx_ready"))
        got_rows = [top.enter_context(nc.semaphore(f"h_got_rows{b}")) for b in range(B)]
        got_rope = [top.enter_context(nc.semaphore(f"h_got_rope{b}")) for b in range(B)]

        def gather_routed(pool, b, rows, rope):
            for r in range(2):
                for s in range(KSEL // P):
                    pool.indirect_dma_start(rows[:, r * (KSEL // P) + s, :], None, norm_rows,
                                            bass.IndirectOffsetOnAxis(ap=sel_idx[:, r * B + b, s:s + 1], axis=0)
                                            ).then_inc(got_rows[b], 16)
            for r in range(2):
                for s in range(KSEL // P):
                    pool.indirect_dma_start(rope[:, r * (KSEL // P) + s, :], None, ap["rope"],
                                            bass.IndirectOffsetOnAxis(ap=ridx[:, r * B + b, s:s + 1], axis=0)
                                            ).then_inc(got_rope[b], 16)

        def light(ctx):
            def sem(name):
                return ctx.enter_context(nc.semaphore(name))

            def st(name, shape, dt=F32):
                return sb(name, shape, dt, ctx)
            wqkv = st("wqkv", [P, DC, 3 * HD])
            wo = st("wo", [P, HC, D])
            gb = st("gb", [P, 2, DC])
            masks = st("masks", [P, 5, 2 * P], BF16)
            stage = st("stage", [P, 2, D])
            xT = st("xT", [P, DC, P])
            qT = st("qT", [P, HC, 2, P])
            kT = st("kT", [P, HC, 4, 2 * P])
            vown = st("vown", [P, 4, H, DH + 1])
            vnb = st("vnb", [P, 4, H, DH + 1])
            edge = st("edge", [P, 2, 2 * P], BF16)
            carry = st("carry", [P, 16])
            ids = st("ids", [P, NT], I32)
            idc = st("idc", [P, 2, EB], I32)
            tokb = h_rope0[:].rearrange("p a d -> p (a d)")
            rtok = st("rtok", [P, 2, D])
            epsc = st("epsc", [P, 1])
            raw = h_wkv[:].rearrange("p c (k d) -> p c k d", d=D)
            hn = h_wqo[:].rearrange("p c (k d) -> p c k d", d=D)
            xnb = h_rows0
            stats1 = st("stats1", [P, EB, 6])
            stats2 = st("stats2", [P, EB, 6])
            mv = st("mv", [P, 2 * EB, 2])
            sd = st("sd", [P, 2 * EB])
            rstd = st("rstd", [P, 2 * EB])
            nmr = st("nmr", [P, EB])
            srow = st("srow", [P, 2, EB])
            C = R * T
            eps_list, eps_last = descent_eps()
            dtab = st("dtab", [P, 3, ITERS])
            bits = st("bits", [P, SEARCH_BITS + 1], U32)
            not_first = st("not_first", [P, C])
            tri = st("tri", [P, P])
            ones = st("ones", [P, P])
            iota16 = st("iota16", [P, 16])
            tokid = st("tokid", [P, C])
            score_in = st("score_in", [P, R, T])
            smax, smax1 = st("smax", [P, R]), st("smax1", [P, R])
            shift, mk, part, lsum, lse, nega = (st(n, [P, R]) for n in ("shift", "mk", "part", "lsum", "lse", "nega"))
            thr, cand, kept, need = (st(n, [P, R]) for n in ("thr", "cand", "kept", "need"))
            work, expo, negu, score, eq, gt, sel = (st(n, [P, R, T]) for n in ("work", "expo", "negu", "score", "eq", "gt", "sel"))
            incl, rank, gain = st("incl", [P, C]), st("rank", [P, C]), st("gain", [P, C])
            pre = st("pre", [P, 2 * C])
            ri = st("ri", [P, 3, C], I32)
            rf = st("rf", [P, 2, C])
            hi1 = st("hi1", [P, C, 16])
            lo1 = st("lo1", [P, C, 32])
            junk = hi1[:].rearrange("p c s -> p (c s)").rearrange("p (a d) -> p a d", d=D)
            lists_f = st("lists_f", [16, R, 32])
            lists_i = st("lists_i", [16, R, 16], I32)
            mx = st("mx", [P, 2, 4])
            nmx = st("nmx", [P, 2, 4])
            prob = st("prob", [P, 2, 4, 2 * P])
            probT = st("probT", [P, 2, 2, 4, P])
            rden = st("rden", [P, 2, 4])
            o = st("o", [P, H, DH])
            oT = st("oT", [P, HC, P])
            ps_sim = ctx.enter_context(nc.psum_tensor("ps_sim", [P, 2, 4, 2 * P], F32))
            ps_pT = ctx.enter_context(nc.psum_tensor("ps_pT", [P, 2, 4, P], F32))
            ps_a = ctx.enter_context(nc.psum_tensor("ps_a", [P, 512], F32))
            ps_b = ctx.enter_context(nc.psum_tensor("ps_b", [P, 512], F32))
            loaded, first_loaded, sp_settled = sem("l_loaded"), sem("l_first_loaded"), sem("l_sp_settled")
            zeroed = sem("l_zeroed")
            edge_ready = sem("l_edge_ready")
            staged = [sem(f"l_staged{k}") for k in range(2)]
            xT_done, xT_ev = sem("l_xT_done"), sem("l_xT_ev")
            q_done, q_ev = sem("l_q_done"), sem("l_q_ev")
            k_done, k_ev = sem("l_k_done"), sem("l_k_ev")
            v_done, v_ev = sem("l_v_done"), sem("l_v_ev")
            sim_done, max_done, exp_done = sem("l_sim_done"), sem("l_max_done"), sem("l_exp_done")
            nmx_in = sem("l_nmx_in")
            ptA_done, ptB_done, ptA_ev, ptB_ev = sem("l_ptA_done"), sem("l_ptB_done"), sem("l_ptA_ev"), sem("l_ptB_ev")
            pv_done, pv_ev, rden_done = sem("l_pv_done"), sem("l_pv_ev"), sem("l_rden_done")
            oT_done, oT_ev = sem("l_oT_done"), sem("l_oT_ev")
            proj_done, proj_ev = sem("l_proj_done"), sem("l_proj_ev")
            id_copied, id_settled, added = sem("e_id_copied"), sem("e_id_settled"), sem("e_added")
            gathered = [[sem(f"e_gathered{par}{k}") for k in range(EB)] for par in range(2)]
            eps_set, stats1_in, stats2_in = sem("e_eps_set"), sem("e_stats1_in"), sem("e_stats2_in")
            var_ready, sd_ready, rstd_ready, nmr_ready = sem("e_var_ready"), sem("e_sd_ready"), sem("e_rstd_ready"), sem("e_nmr_ready")
            normed, xn_done, dots = sem("e_normed"), sem("e_xn_done"), sem("e_dots")
            hn_saved, xn_saved = sem("e_hn_saved"), sem("e_xn_saved")
            part_max, all_max, v = sem("r_part_max"), sem("r_all_max"), sem("r_v")
            diff_ready, exp_ready, sum_in = sem("r_diff_ready"), sem("r_exp_ready"), sem("r_sum_in")
            sum_out, ln_done = sem("r_sum_out"), sem("r_ln_done")
            score_args, score_done = sem("r_score_args"), sem("r_score_done")
            cnt_in, cnt_done, thr_ready = sem("r_cnt_in"), sem("r_cnt_done"), sem("r_thr_ready")
            mask_in, pref_out = sem("r_mask_in"), sem("r_pref_out")
            onehot, list_out, list_saved, list_back = sem("r_onehot"), sem("r_list_out"), sem("r_list_saved"), sem("r_list_back")
            null_saved = sem("r_null_saved")
            bc = lambda a: a.rearrange("p (r o) -> p r o", o=1).broadcast_to([P, R, T])
            flat2 = lambda a: a.rearrange("p r t -> p (r t)")

            def head(u, h):
                return 4 * u + 2 * (h % 2) + h // 2

            def pe_xT(pe, n, slot):
                pe.wait_ge(staged[slot % 2], n * 8 + (16 - 8 * (slot % 2)))
                for c in range(DC):
                    i = nc.tensor.transpose(ps_a[:, c * P:(c + 1) * P], stage[:, slot % 2, c * P:(c + 1) * P], ident[:])
                i.then_inc(xT_done, 1)

            def pe_xT_first(pe, n):
                pe.wait_ge(xn_done, 1)
                for c in range(DC):
                    i = nc.tensor.transpose(ps_a[:, c * P:(c + 1) * P], xnb[:, n, c * P:(c + 1) * P], ident[:])
                i.then_inc(xT_done, 1)

            def sp_stage(sp, n, slot):
                if past(n - 1):
                    sp.wait_ge(xT_done, n - 1)
                    sp.sem_inc(sp_settled, 1)
                sp.dma_start(stage[:, slot % 2, :].rearrange("p (a d) -> p a d", a=1),
                             rows_of(light_rows, n, 1)).then_inc(staged[slot % 2], 16)

            def rows_of(tensor, first, count):
                return tensor.rearrange("(g p) d -> p g d", p=P)[:, bass.ds(first, count), :]

            def pe_qk(pe, ps, col, done):
                for m in range(HC):
                    for c in range(DC):
                        i = nc.tensor.matmul(ps[:, m * P:(m + 1) * P], wqkv[:, c, col + m * P:col + (m + 1) * P], xT[:, c, :],
                                             start=(c == 0), stop=(c == DC - 1))
                i.then_inc(done, 1)

            def pe_v(pe):
                for c in range(DC):
                    i = nc.tensor.matmul(ps_b[:], xT[:, c, :], wqkv[:, c, 2 * HD:3 * HD], start=(c == 0), stop=(c == DC - 1))
                i.then_inc(v_done, 1)

            def pe_sim(pe, k, u):
                for l in range(2):
                    for e in range(2):
                        c = 2 * u + l
                        i = nc.tensor.matmul(ps_sim[:, u, 2 * e + l, :], qT[64 * e:64 * e + 64, c, k % 2, :],
                                             kT[64 * e:64 * e + 64, c, k, :], start=True, stop=True)
                i.then_inc(sim_done, 1)

            def pe_pT(pe, u):
                for blk, done in ((0, ptA_done), (1, ptB_done)):
                    for h in range(4):
                        i = nc.tensor.transpose(ps_pT[:, blk, h, :], prob[:, u, h, blk * P:(blk + 1) * P], ident[:])
                    i.then_inc(done, 1)

            def pe_pv(pe, ps, k, u, more=None):
                for h in range(4):
                    for blk, vals in ((0, vown), (1, vnb)):
                        i = nc.tensor.matmul(ps[:, (head(u, h) - 4 * u) * (DH + 1):(head(u, h) - 4 * u + 1) * (DH + 1)],
                                             probT[:, u, blk, h, :], vals[:, k, head(u, h), :],
                                             start=(blk == 0), stop=(blk == 1))
                if more:
                    i = more(pe)
                i.then_inc(pv_done, 1)

            def pe_oT(pe):
                flat = o[:].rearrange("p h d -> p (h d)")
                for c in range(HC):
                    i = nc.tensor.transpose(ps_b[:, c * P:(c + 1) * P], flat[:, c * P:(c + 1) * P], ident[:])
                i.then_inc(oT_done, 1)

            def pe_proj(pe, more=None):
                for c in range(HC):
                    i = nc.tensor.matmul(ps_b[:, 0:D], oT[:, c, :], wo[:, c, :], start=(c == 0), stop=(c == HC - 1))
                if more:
                    i = more(pe)
                i.then_inc(proj_done, 1)

            def upto(n):
                return min(n, NT) if isinstance(n, int) else n

            def pe_back(pe, g):
                pe.wait_ge(exp_done, 2 * g)
                pe_pT(pe, 1)

            def pe_tile(pe, g, k, extra=None, qkv=True):
                pe.wait_ge(k_ev, upto(g + 2))
                pe_sim(pe, k, 0)
                if past(g):
                    pe_back(pe, g)
                    pe.wait_ge(pv_ev, 2 * g - 1)
                if qkv:
                    pe_xT(pe, g + 2, k)
                pe_sim(pe, k, 1)
                pe.wait_ge(v_ev, upto(g + 2))
                if past(g):
                    pe.wait_ge(ptA_ev, 2 * g)
                    pe.wait_ge(ptB_ev, 2 * g)
                    pe_pv(pe, ps_b, (k + 3) % 4, 1)
                if qkv:
                    pe.wait_ge(xT_ev, g + 3)
                    pe_qk(pe, ps_a, 0, q_done)
                if past(g):
                    pe.wait_ge(pv_ev, 2 * g)
                    pe_oT(pe)
                pe.wait_ge(exp_done, 2 * g + 1)
                pe_pT(pe, 0)
                if qkv:
                    pe.wait_ge(q_ev, g + 3)
                    pe_qk(pe, ps_a, HD, k_done)
                if past(g):
                    pe.wait_ge(oT_ev, g)
                    pe_proj(pe, extra and extra.pe_proj)
                pe.wait_ge(ptA_ev, 2 * g + 1)
                pe.wait_ge(ptB_ev, 2 * g + 1)
                if qkv:
                    pe.wait_ge(k_ev, g + 3)
                pe_pv(pe, ps_a, k, 0, extra and extra.pe_pv)
                if past(g):
                    pe.wait_ge(proj_ev, g)
                if qkv:
                    pe_v(pe)

            def act_xT(act, n):
                act.wait_ge(xT_done, n)
                for c in range(DC):
                    i = nc.scalar.activation(xT[:, c, :], ps_a[:, c * P:(c + 1) * P], ACT.Identity,
                                             bias=gb[:, 1, c:c + 1], scale=gb[:, 0, c:c + 1])
                i.then_inc(xT_ev, 1)

            def act_q(act, n, slot):
                act.wait_ge(q_done, n)
                nc.scalar.copy(qT[:, :, slot % 2, :], ps_a[:].rearrange("p (m j) -> p m j", m=HC)).then_inc(q_ev, 1)

            def act_k(act, n, slot):
                act.wait_ge(k_done, n)
                src = ps_a[:].rearrange("p (m j) -> p m j", m=HC)
                nc.scalar.copy(kT[:, :, (slot + 3) % 4, P:P + DH], src[:, :, 0:DH])
                nc.scalar.copy(kT[:, :, (slot + 1) % 4, P + DH:2 * P], src[:, :, DH:P])
                nc.scalar.copy(kT[:, :, slot, 0:P], src).then_inc(k_ev, 1)

            def act_exp(act, n, u):
                act.wait_ge(max_done, n)
                for h in range(4):
                    i = nc.scalar.activation(prob[:, u, h, :], prob[:, u, h, :], ACT.Exp, bias=nmx[:, u, h:h + 1], scale=SCALE)
                i.then_inc(exp_done, 1)

            def act_ptB(act, n, u):
                act.wait_ge(ptB_done, n)
                nc.scalar.copy(probT[:, u, 1, :, :], ps_pT[:, 1, :, :]).then_inc(ptB_ev, 1)

            def act_tile(act, g, k, extra=None, qkv=True):
                if past(g):
                    act_ptB(act, 2 * g, 1)
                if qkv:
                    act_xT(act, g + 3)
                act_exp(act, 2 * g + 1, 0)
                if extra and extra.act_early:
                    extra.act_early(act)
                if qkv:
                    act_q(act, g + 3, (k + 2) % 4)
                act_exp(act, 2 * g + 2, 1)
                if extra and extra.act_mid:
                    extra.act_mid(act)
                act_ptB(act, 2 * g + 1, 0)
                if qkv:
                    act_k(act, g + 3, (k + 2) % 4)
                if extra and extra.act_end:
                    extra.act_end(act)

            def dve_max(dve, n, u, mask):
                dve.wait_ge(sim_done, n)
                nc.vector.memset(carry[:, u:u + 1], 0.0)
                for h in range(4):
                    i = nc.vector.tensor_tensor_reduce(prob[:, u, h, :], ps_sim[:, u, h, :], mask, 1.0, -3.4e38, ALU.add,
                                                       ALU.max, mx[:, u, h:h + 1])
                i.then_inc(nmx_in, 1)
                dve.wait_ge(nmx_in, n)
                nc.vector.tensor_scalar(nmx[:, u, :], mx[:, u, :], -SCALE, None, ALU.mult).then_inc(max_done, 1)

            def dve_ptA(dve, n, u):
                dve.wait_ge(ptA_done, n)
                nc.vector.tensor_copy(probT[:, u, 0, :, :], ps_pT[:, 0, :, :]).then_inc(ptA_ev, 1)

            def dve_pv(dve, ps, n, u, more=None):
                dve.wait_ge(pv_done, n)
                view = ps[:, 0:4 * (DH + 1)].rearrange("p (h d) -> p h d", h=4)
                nc.vector.reciprocal(rden[:, u, :], view[:, :, DH]).then_inc(rden_done, 1)
                dve.wait_ge(rden_done, n)
                i = nc.vector.tensor_tensor(o[:, 4 * u:4 * u + 4, :], view[:, :, 0:DH],
                                        rden[:, u, :].rearrange("p (h o) -> p h o", o=1).broadcast_to([P, 4, DH]),
                                        ALU.mult)
                i = more(dve) if more else i
                i.then_inc(pv_ev, 1)

            def dve_v(dve, n, slot):
                dve.wait_ge(v_done, n)
                src = ps_b[:].rearrange("p (h d) -> p h d", h=H)
                nc.vector.tensor_copy(vnb[0:DH, (slot + 3) % 4, :, 0:DH], src[0:DH])
                nc.vector.tensor_copy(vnb[DH:P, (slot + 1) % 4, :, 0:DH], src[DH:P])
                nc.vector.tensor_copy(vown[:, slot, :, 0:DH], src).then_inc(v_ev, 1)

            def dve_oT(dve, n):
                dve.wait_ge(oT_done, n)
                nc.vector.tensor_copy(oT[:].rearrange("p c j -> p (c j)"), ps_b[:]).then_inc(oT_ev, 1)

            def dve_proj(dve, n, g, more=None):
                dve.wait_ge(proj_done, n)
                if more:
                    more(dve)
                row = hres[:, bass.ds(g, 1), :].rearrange("p a d -> p (a d)")
                nc.vector.tensor_tensor(row, ps_b[:, 0:D], row, ALU.add).then_inc(proj_ev, 1)

            def dve_tile(dve, g, k, mask, extra=None, qkv=True):
                dve_max(dve, 2 * g + 1, 0, mask)
                if past(g):
                    dve_ptA(dve, 2 * g, 1)
                if extra and extra.dve_1:
                    extra.dve_1(dve)
                if past(g):
                    dve_pv(dve, ps_b, 2 * g, 1)
                dve_max(dve, 2 * g + 2, 1, mask)
                if extra and extra.dve_2:
                    extra.dve_2(dve)
                if past(g):
                    dve_oT(dve, g)
                dve_ptA(dve, 2 * g + 1, 0)
                if extra and extra.dve_3:
                    extra.dve_3(dve)
                if past(g):
                    dve_proj(dve, g, g - 1, extra and extra.dve_proj)
                if extra and extra.dve_4:
                    extra.dve_4(dve)
                dve_pv(dve, ps_a, 2 * g + 1, 0, extra and extra.dve_pv)
                if extra and extra.dve_5:
                    extra.dve_5(dve)
                if qkv:
                    dve_v(dve, g + 3, (k + 2) % 4)

            class Extra:
                pe_proj = pe_pv = act_early = act_mid = act_end = None
                dve_1 = dve_2 = dve_3 = dve_4 = dve_5 = dve_proj = dve_pv = None

            def pool_gather(pool, n, par):
                if past(n - 1):
                    pool.wait_ge(added, (n - 1) * EB)
                nc.gpsimd.tensor_copy(idc[:, par, :], ids[:, bass.ds(n * EB, EB)]).then_inc(id_copied, 1)
                pool.wait_ge(id_copied, n + 1)
                pool.sem_inc(id_settled, 1)
                for k in range(EB):
                    pool.indirect_dma_start(raw[:, par, k, :], None, ap["table"],
                                            bass.IndirectOffsetOnAxis(ap=idc[:, par, k:k + 1], axis=0)
                                            ).then_inc(gathered[par][k], 16)

            def pool_add(pool, n, par):
                for k in range(EB):
                    pool.wait_ge(gathered[par][k], n * 8 + (16 - 8 * par))
                    nc.gpsimd.tensor_tensor(hres[:, bass.ds(n * EB + k, 1), :].rearrange("p a d -> p (a d)"),
                                            raw[:, par, k, :], tokb, ALU.add).then_inc(added, 1)

            def tail(n):
                return isinstance(n, int) and n == NB

            def dve_stats(dve, n):
                if tail(n):
                    nc.vector.memset(carry[:, 2:3], 0.0).then_inc(var_ready, 1)
                    return
                dve.wait_ge(added, n * EB + EB)
                nc.vector.memset(carry[:, 3:4], 0.0)
                for k in range(EB):
                    i = nc.vector.bn_stats(stats1[:, k, :], hres[:, bass.ds(n * EB + k, 1), :].rearrange("p a d -> p (a d)"))
                i.then_inc(stats1_in, 1)
                dve.wait_ge(stats1_in, n + 1)
                nc.vector.memset(carry[:, 4:5], 0.0)
                for k in range(EB):
                    i = nc.vector.bn_aggr(mv[:, k, :], stats1[:, k, :])
                i.then_inc(var_ready, 1)

            def act_root(act, n):
                act.wait_ge(var_ready, n + 1)
                nc.scalar.activation(sd[:], mv[:, :, 1], ACT.Sqrt, bias=epsc[:, 0:1]).then_inc(sd_ready, 1)

            def dve_norm(dve, n, par):
                dve.wait_ge(sd_ready, n + 1)
                if past(n - 1):
                    dve.wait_ge(xn_done, n - 1)
                nc.vector.reciprocal(rstd[:], sd[:]).then_inc(rstd_ready, 1)
                dve.wait_ge(rstd_ready, n + 1)
                nc.vector.scalar_tensor_tensor(out=nmr[:], in0=mv[:, EB:2 * EB, 0], scalar=-1.0, in1=rstd[:, EB:2 * EB],
                                               op0=ALU.mult, op1=ALU.mult).then_inc(nmr_ready, 1)
                if tail(n):
                    return
                if past(n):
                    dve.wait_ge(hn_saved, n * 16)
                for k in range(EB):
                    i = nc.vector.tensor_scalar(hn[:, par, k, :], hres[:, bass.ds(n * EB + k, 1), :].rearrange("p a d -> p (a d)"),
                                                mv[:, k, 0:1], rstd[:, k:k + 1], ALU.subtract, ALU.mult)
                i.then_inc(normed, 1)

            def dve_stats2(dve, n, par):
                dve.wait_ge(normed, n + 1)
                nc.vector.memset(carry[:, 5:6], 0.0)
                for k in range(EB):
                    i = nc.vector.bn_stats(stats2[:, k, :], hn[:, par, k, :])
                i.then_inc(stats2_in, 1)
                dve.wait_ge(nmr_ready, n + 1)
                dve.wait_ge(stats2_in, n + 1)
                nc.vector.memset(carry[:, 6:7], 0.0)
                for k in range(EB):
                    nc.vector.bn_aggr(mv[:, EB + k, :], stats2[:, k, :])

            def dve_dots(dve, n, par, half):
                for k in range(2 * half, 2 * half + 2):
                    for r in range(2):
                        i = nc.vector.tensor_tensor_reduce(junk[:, 2 * k + r, :], hn[:, par, k, :], rtok[:, r, :], 1.0, 0.0,
                                                           ALU.mult, ALU.add, srow[:, r, k:k + 1])
                if half:
                    i.then_inc(dots, 1)
                    dve.wait_ge(dots, n + 1)
                    for r in range(2):
                        nc.vector.tensor_scalar(flat2(score_in[:])[:, bass.ds(n * EB + r * NT, EB)], srow[:, r, :], 1.0,
                                                None, ALU.mult)

            def act_norm2(act, n, par):
                act.wait_ge(nmr_ready, n + 1)
                if past(n - 1):
                    act.wait_ge(xn_saved, (n - 1) * 16)
                for k in range(EB):
                    i = nc.scalar.activation(xnb[:, k, :], hn[:, 1 - par, k, :], ACT.Identity, bias=nmr[:, k:k + 1],
                                             scale=rstd[:, EB + k:EB + k + 1])
                i.then_inc(xn_done, 1)

            def sp_embed(sp, n, par):
                if not tail(n):
                    sp.wait_ge(normed, n + 1)
                    sp.sem_inc(sp_settled, 1)
                    sp.dma_start(rows_of(norm_rows, n * EB, EB), hn[:, par, :, :]).then_inc(hn_saved, 16)
                if past(n):
                    sp.wait_ge(xn_done, n)
                    sp.sem_inc(sp_settled, 1)
                    sp.dma_start(rows_of(light_rows, (n - 1) * EB, EB), xnb[:]).then_inc(xn_saved, 16)

            def embed(n, k):
                e, par = Extra(), k % 2
                e.dve_1 = lambda dve: dve_stats(dve, n)
                e.act_early = lambda act: act_root(act, n)
                e.dve_2 = lambda dve: dve_dots(dve, n - 1, 1 - par, 0)
                e.dve_3 = lambda dve: dve_norm(dve, n, par)
                e.act_end = lambda act: act_norm2(act, n, par)
                if not tail(n):
                    e.dve_4 = lambda dve: dve_stats2(dve, n, par)
                e.dve_5 = lambda dve: dve_dots(dve, n - 1, 1 - par, 1)
                return e

            def pe_sum(pe, ps, at, n, given):
                pe.wait_ge(given, n)
                return nc.tensor.matmul(ps[:, at:at + R], ones[:], part[:], start=True, stop=True)

            def first_max():
                e = Extra()
                e.dve_1 = lambda dve: nc.vector.tensor_reduce(smax1[:], score_in[:], AX, ALU.max).then_inc(part_max, 1)

                def state(dve):
                    nc.vector.memset(mk[:], 0.0)
                    nc.vector.memset(thr[:], 0.0)
                    dve.wait_ge(all_max, 1)
                    nc.vector.memset(work[:], 0.0).then_inc(diff_ready, 1)
                e.dve_5 = state
                return e

            DS = 7

            def descend(i):
                e = Extra()
                base = i * DS

                def exps(act):
                    act.wait_ge(diff_ready, i + 1)
                    nc.scalar.activation(expo[:], work[:], ACT.Exp, scale=dtab[:, 0, bass.ds(i, 1)]).then_inc(exp_ready, 1)

                def sums(dve):
                    nc.vector.tensor_scalar(shift[:], mk[:], dtab[:, 2, bass.ds(i, 1)], None, ALU.add).then_inc(v, 1)
                    dve.wait_ge(exp_ready, i + 1)
                    nc.vector.tensor_reduce(part[:], expo[:], AX, ALU.add).then_inc(sum_in, 1)

                def logs(act):
                    act.wait_ge(sum_out, i + 1)
                    nc.scalar.activation(lse[:], lsum[:], ACT.Ln).then_inc(ln_done, 1)

                def update(dve):
                    dve.wait_ge(ln_done, i + 1)
                    dve.wait_ge(v, base + 1)
                    nc.vector.scalar_tensor_tensor(out=nega[:], in0=lse[:], scalar=dtab[:, 1, bass.ds(i, 1)], in1=shift[:],
                                                   op0=ALU.mult, op1=ALU.add).then_inc(v, 1)
                    dve.wait_ge(v, base + 2)
                    nc.vector.tensor_tensor(work[:], score_in[:], bc(nega[:]), ALU.subtract).then_inc(v, 1)
                    nc.vector.tensor_tensor(mk[:], smax[:], nega[:], ALU.min).then_inc(v, 1)
                    dve.wait_ge(v, base + 4)
                    nc.vector.scalar_tensor_tensor(out=negu[:], in0=work[:], scalar=0.0, in1=score_in[:],
                                                   op0=ALU.max, op1=ALU.subtract).then_inc(v, 1)
                    nc.vector.tensor_scalar(gt[:], work[:], 0.0, None, ALU.min).then_inc(v, 1)
                    dve.wait_ge(v, base + 6)
                    nc.vector.tensor_tensor(work[:], negu[:], bc(mk[:]), ALU.add).then_inc(v, 1)
                    dve.wait_ge(v, base + 7)
                    nc.vector.tensor_copy(carry[:, 15:16], mk[:, 0:1]).then_inc(diff_ready, 1)
                e.act_mid, e.dve_3, e.act_end, e.dve_5 = exps, sums, logs, update
                e.pe_proj = lambda pe: pe_sum(pe, ps_b, D, i + 1, sum_in)
                e.dve_proj = lambda dve: nc.vector.tensor_copy(lsum[:], ps_b[:, D:D + R]).then_inc(sum_out, 1)
                return e

            BS = 3
            PV_END = 4 * (DH + 1)

            def dve_test(dve, i):
                base = i * BS + ITERS * DS
                nc.vector.tensor_tensor(cand[:].bitcast(U32), thr[:].bitcast(U32),
                                        bits[:, bass.ds(i, 1)].broadcast_to([P, R]), ALU.bitwise_or).then_inc(v, 1)
                dve.wait_ge(v, base + 1)
                nc.vector.tensor_tensor(eq[:], score[:], bc(cand[:]), ALU.is_ge).then_inc(v, 1)
                dve.wait_ge(v, base + 2)
                nc.vector.tensor_reduce(part[:], eq[:], AX, ALU.add).then_inc(cnt_in, 1)

            def dve_decide(counts):
                return nc.vector.scalar_tensor_tensor(out=kept[:], in0=counts, scalar=float(KSEL), in1=cand[:],
                                                      op0=ALU.is_ge, op1=ALU.mult)

            def dve_next(dve, i):
                dve.wait_ge(v, i * BS + ITERS * DS + 3)
                nc.vector.tensor_tensor(thr[:], thr[:], kept[:], ALU.max).then_inc(thr_ready, 1)
                dve.wait_ge(thr_ready, i + 1)
                dve_test(dve, i + 1)

            def search(i, two):
                e = Extra()
                e.pe_proj = lambda pe: pe_sum(pe, ps_b, D, i + 1, cnt_in)
                e.dve_proj = lambda dve: dve_decide(ps_b[:, D:D + R]).then_inc(v, 1)
                e.dve_4 = lambda dve: dve_next(dve, i)
                if two:
                    e.pe_pv = lambda pe: pe_sum(pe, ps_a, PV_END, i + 2, cnt_in)
                    e.dve_5 = lambda dve: dve_next(dve, i + 1)

                    def decide(dve):
                        dve_decide(ps_a[:, PV_END:PV_END + R]).then_inc(v, 1)
                        return nc.vector.memset(carry[:, 7:8], 0.0)
                    e.dve_pv = decide
                return e

            cnt = [0]

            def link(dve, i):
                cnt[0] += 1
                i.then_inc(v, 1)
                dve.wait_ge(v, cnt[0])

            def masks_of(dve):
                cnt[0] = ITERS * DS + SEARCH_BITS * BS + 2
                dve.wait_ge(cnt_in, SEARCH_BITS + 1)
                nc.vector.tensor_tensor(eq[:], score[:], bc(thr[:]), ALU.is_equal).then_inc(mask_in, 1)
                link(dve, nc.vector.tensor_tensor(gt[:], score[:], bc(thr[:]), ALU.is_gt))
                nc.vector.tensor_reduce(part[:], gt[:], AX, ALU.add).then_inc(cnt_in, 1)

            def pe_prefix(pe, mask, j):
                pe.wait_ge(mask_in, j)
                nc.tensor.matmul(ps_b[:, D:D + C], tri[:], flat2(mask[:]), start=True, stop=True)
                return nc.tensor.matmul(ps_b[:, D + C:D + 2 * C], ones[:], flat2(mask[:]), start=True, stop=True)

            def dve_prefix(dve, j):
                dve.wait_ge(pref_out, j)
                link(dve, nc.vector.tensor_tensor_scan(incl[:], not_first[:], pre[:, C:2 * C], 0.0, ALU.mult, ALU.add))
                link(dve, nc.vector.tensor_tensor(rank[:], pre[:, 0:C], incl[:], ALU.add))
                link(dve, nc.vector.tensor_tensor(rank[:], rank[:], pre[:, C:2 * C], ALU.subtract))

            def take_prefix(dve):
                nc.vector.tensor_copy(pre[:], ps_b[:, D:D + 2 * C]).then_inc(pref_out, 1)

            def select_1():
                e = Extra()
                e.pe_proj = lambda pe: pe_prefix(pe, eq, 1)
                e.dve_proj = take_prefix
                e.pe_pv = lambda pe: pe_sum(pe, ps_a, PV_END, SEARCH_BITS + 2, cnt_in)

                def wanted(dve):
                    nc.vector.tensor_scalar(need[:], ps_a[:, PV_END:PV_END + R], -1.0, float(KSEL), ALU.mult, ALU.add)
                    return nc.vector.memset(carry[:, 8:9], 0.0)
                e.dve_pv = wanted

                def choose(dve):
                    dve_prefix(dve, 1)
                    rk = rank[:].rearrange("p (r t) -> p r t", r=R)
                    link(dve, nc.vector.tensor_tensor(sel[:], rk, bc(need[:]), ALU.is_lt))
                    link(dve, nc.vector.tensor_tensor(sel[:], sel[:], eq[:], ALU.mult))
                    nc.vector.tensor_tensor(sel[:], sel[:], gt[:], ALU.add).then_inc(mask_in, 1)
                    flat = flat2(score[:])
                    link(dve, nc.vector.tensor_scalar(gain[:], flat, -1.0, 1.0, ALU.mult, ALU.add))
                    link(dve, nc.vector.tensor_tensor(gain[:], gain[:], flat, ALU.add))
                e.dve_5 = choose
                return e

            io = iota16[:].rearrange("p (o s) -> p o s", o=1).broadcast_to([P, C, 16])
            wide = lambda a: a.rearrange("p (c o) -> p c o", o=1).broadcast_to([P, C, 16])

            def select_2():
                e = Extra()
                e.pe_proj = lambda pe: pe_prefix(pe, sel, 2)
                e.dve_proj = take_prefix

                def ranks(dve):
                    dve_prefix(dve, 2)
                    selq = sel[:, 0:B, :].rearrange("p r t -> p (r t)")
                    CQ = B * T
                    link(dve, nc.vector.tensor_scalar(rf[:, 0, 0:CQ], rank[:, 0:CQ], -float(KSEL), None, ALU.add))
                    link(dve, nc.vector.tensor_tensor(rf[:, 0, 0:CQ], rf[:, 0, 0:CQ], selq, ALU.mult))
                    link(dve, nc.vector.tensor_scalar(pos[:].rearrange("p b t -> p (b t)"), rf[:, 0, 0:CQ],
                                                      float(KSEL), None, ALU.add))
                    link(dve, nc.vector.tensor_scalar(incl[:], flat2(sel[:]), -4096.0, 4096.0, ALU.mult, ALU.add))
                    link(dve, nc.vector.tensor_tensor(rank[:], rank[:], incl[:], ALU.add))
                    link(dve, nc.vector.tensor_copy(ri[:, 0, :], rank[:]))
                    link(dve, nc.vector.tensor_scalar(ri[:, 1, :], ri[:, 0, :], 4, None, ALU.logical_shift_right))
                    link(dve, nc.vector.tensor_scalar(ri[:, 2, :], ri[:, 0, :], 15, None, ALU.bitwise_and))
                    link(dve, nc.vector.tensor_copy(rf[:], ri[:, 1:3, :]))
                e.dve_5 = ranks
                return e

            def select_3():
                e = Extra()
                e.dve_1 = lambda dve: link(dve, nc.vector.tensor_tensor(hi1[:], io, wide(rf[:, 0, :]), ALU.is_equal))
                e.dve_2 = lambda dve: link(dve, nc.vector.tensor_tensor(lo1[:, :, 0:16], io, wide(rf[:, 1, :]), ALU.is_equal))
                e.dve_3 = lambda dve: link(dve, nc.vector.tensor_tensor(lo1[:, :, 16:32], lo1[:, :, 0:16], wide(gain[:]),
                                                                        ALU.mult))
                e.dve_5 = lambda dve: nc.vector.tensor_tensor(lo1[:, :, 0:16], lo1[:, :, 0:16], wide(tokid[:]),
                                                              ALU.mult).then_inc(onehot, 1)
                return e

            def select_4():
                e = Extra()

                def products(pe):
                    pe.wait_ge(onehot, 1)
                    for r in range(R):
                        for t in range(T):
                            i = nc.tensor.matmul(ps_b[0:16, D + r * 32:D + r * 32 + 32], hi1[:, r * T + t, :],
                                                 lo1[:, r * T + t, :], start=(t == 0), stop=(t == T - 1))
                    return i

                def take(dve):
                    src = ps_b[0:16, D:D + R * 32].rearrange("p (r l) -> p r l", r=R)
                    nc.vector.tensor_copy(lists_f[:], src).then_inc(list_out, 1)
                    nc.vector.tensor_copy(lists_i[:], src[:, :, 0:16]).then_inc(list_out, 1)
                e.pe_proj, e.dve_proj = products, take
                return e

            def positions():
                e = Extra()

                def mask_low(dve):
                    dve.wait_ge(list_back, 64)
                    nc.vector.tensor_scalar(ridx[:], sel_idx[:], N - 1, None, ALU.bitwise_and).then_inc(idx_ready, 1)
                e.dve_5 = mask_low
                return e

            def sp_lists(sp):
                sp.wait_ge(list_out, 2)
                sp.dma_start(list_idx.rearrange("(r h l) o -> h r (l o)", r=R, h=16), lists_i[:]).then_inc(list_saved, 16)
                sp.dma_start(list_gain.rearrange("(r h l) o -> h r (l o)", r=R, h=16),
                             lists_f[:, :, 16:32]).then_inc(list_saved, 16)
                sp.wait_ge(list_saved, 32)
                with nc.allow_non_contiguous_dma(reason="2048 list entries, one per partition"):
                    for h in range(KSEL // P):
                        for src, dst in ((list_idx, sel_idx), (list_gain, sel_gain)):
                            sp.dma_start(dst[:, :, h], src.rearrange("(r h p) o -> h p (r o)", r=R, p=P)[h]
                                         ).then_inc(list_back, 16)
                sp.wait_ge(list_back, 64)

            FIRST = 2
            EMBED_END = NB // 4
            G_DESCENT = NB // 4
            G_SEARCH = G_DESCENT + ITERS // 4
            PER_GROUP = (2, 2, 1, 1)
            G_SELECT = G_SEARCH + SEARCH_BITS // sum(PER_GROUP)
            between = {EMBED_END - 1: {0: lambda: embed(NB - 2, 0), 1: lambda: embed(NB - 1, 1),
                                       2: lambda: embed(NB, 2), 3: first_max},
                       NT // 4 - 1: {1: positions},
                       G_SELECT: {0: select_1, 1: select_2, 2: select_3, 3: select_4}}

            def extra_of(it, k):
                if it == 0:
                    return embed(FIRST + k, k)
                return between[it][k]() if k in between.get(it, {}) else None

            def in_embed(it, k):
                return embed(it * 4 + (FIRST + k), k)

            def in_descent(it, k):
                return descend(it * 4 + (k - 4 * G_DESCENT))

            def in_search(it, k):
                return search(it * sum(PER_GROUP) + (sum(PER_GROUP[:k]) - sum(PER_GROUP) * G_SEARCH), PER_GROUP[k] == 2)

            def groups(eng, tile, before_search=None, before_select=None, group=None):
                def alone(it):
                    if group:
                        group(it)
                    for k in range(4):
                        tile(it, k, extra_of(it, k), it < NT // 4 - 1 or k < 2)

                def loop(first, end, kind):
                    with eng.Fori(first, end) as it:
                        if group:
                            group(it)
                        for k in range(4):
                            tile(it, k, kind(it, k), True)
                alone(0)
                loop(1, EMBED_END - 1, in_embed)
                alone(EMBED_END - 1)
                loop(G_DESCENT, G_SEARCH, in_descent)
                if before_search:
                    before_search()
                loop(G_SEARCH, G_SELECT, in_search)
                if before_select:
                    before_select()
                for it in range(G_SELECT, NT // 4):
                    alone(it)

            with nc.Block() as block:
                @block.sync
                def _(sp):
                    for dst, src in ((ids[:], ap["ids"]), (tokb, ap["tok_bias"]), (rtok[:], ap["route_tok"])):
                        sp.dma_start(dst, src).then_inc(first_loaded, 16)
                    for dst, src in ((ident[:], ap["ident"]),
                                     (wqkv[:], ap["wqkv"].rearrange("(c p) n -> p c n", p=P)),
                                     (wo[:], ap["light_out_w"].rearrange("(c p) n -> p c n", p=P)),
                                     (gb[:], ap["ln_affine"]), (masks[:], ap["masks"]),
                                     (dtab[:], ap["descent"]), (bits[:], ap["bits"]), (not_first[:], ap["not_first"]),
                                     (tri[:], ap["tri"]), (iota16[:], ap["iota16"]), (tokid[:], ap["tokid"])):
                        sp.dma_start(dst, src).then_inc(loaded, 16)
                    for b in range(B):
                        sp.dma_start(heavy_rows[b][KSEL:KSEL + 1, :], ap["null_q"]).then_inc(null_saved, 16)
                    for n in range(FIRST):
                        sp_embed(sp, n, n % 2)
                    sp.wait_ge(xn_saved, 16)
                    for n in range(2):
                        sp.sem_inc(staged[n], 16)
                    sp_stage(sp, 2, 2)

                    def sp_group(first, end, embeds):
                        with sp.Fori(first, end) as it:
                            for k in range(4):
                                sp_tile(sp, it * 4 + k, k, embeds)

                    def sp_tile(sp, g, k, embeds):
                        if embeds:
                            sp.wait_ge(xn_saved, g * 16 + (FIRST - 1) * 16)
                            sp.sem_inc(sp_settled, 1)
                        sp_stage(sp, g + 3, k + 3)
                        if embeds:
                            sp_embed(sp, g + FIRST, k % 2)
                    for k in range(4):
                        sp_tile(sp, k, k, True)
                    sp_group(1, EMBED_END - 1, True)
                    last_step = NB - FIRST
                    for g in range((EMBED_END - 1) * 4, EMBED_END * 4):
                        if g == last_step + 1:
                            sp.wait_ge(xn_saved, NB * 16)
                        sp_tile(sp, g, g % 4, g <= last_step)
                    sp_group(EMBED_END, NT // 4 - 1, False)
                    sp_stage(sp, NT - 1, NT - 1)
                    sp.wait_ge(added, NB * EB)
                    sp.wait_ge(dots, NB)
                    sp.wait_ge(xn_done, NB)
                    sp.wait_ge(hn_saved, NB * 16)
                    for dst, src in ((h_wkv[:], ap["heavy_kv_w"].rearrange("(c p) n -> p c n", p=P)),
                                     (h_wqo[:, 0].rearrange("p (c n) -> p c n", c=DC),
                                      ap["heavy_q_w"].rearrange("(c p) n -> p c n", p=P)),
                                     (h_wqo[:, 1].rearrange("p (c n) -> p c n", c=HC),
                                      ap["heavy_out_w"].rearrange("(c p) n -> p c n", p=P))):
                        sp.dma_start(dst, src).then_inc(h_weights, 16)
                    sp_lists(sp)
                    sp.wait_ge(null_saved, 16 * B)

                @block.gpsimd
                def _(pool):
                    pool.wait_ge(first_loaded, 48)
                    for n in range(2):
                        pool_gather(pool, n, n)
                    for n in range(2):
                        pool_add(pool, n, n)
                    pool_gather(pool, 2, 0)
                    with pool.Fori(1, NB // 2 - 1) as it:
                        for par in range(2):
                            pool_gather(pool, it * 2 + (par + 1), 1 - par)
                            pool_add(pool, it * 2 + par, par)
                    pool_gather(pool, NB - 1, 1)
                    pool_add(pool, NB - 2, 0)
                    pool_add(pool, NB - 1, 1)
                    pool.wait_ge(part_max, 1)
                    nc.gpsimd.partition_all_reduce(smax[:], smax1[:], P, bass.bass_isa.ReduceOp.max).then_inc(all_max, 1)
                    pool.wait_ge(idx_ready, 1)
                    pool.wait_ge(hn_saved, NB * 16)
                    pool.wait_ge(xn_saved, NB * 16)
                    gather_routed(pool, 0, h_rows0, h_rope0)

                @block.tensor
                def _(pe):
                    pe.wait_ge(loaded, 16 * 11)
                    pe.wait_ge(zeroed, 1)
                    for g in range(2):
                        if g:
                            pe.wait_ge(k_ev, g)
                        pe_xT_first(pe, g)
                        pe.wait_ge(xT_ev, g + 1)
                        pe_qk(pe, ps_a, 0, q_done)
                        pe.wait_ge(q_ev, g + 1)
                        pe_qk(pe, ps_a, HD, k_done)
                        if g:
                            pe.wait_ge(v_ev, g)
                        pe_v(pe)
                    groups(pe, lambda it, k, extra, qkv: pe_tile(pe, it * 4 + k, k, extra, qkv))
                    pe_back(pe, NT)
                    pe.wait_ge(ptA_ev, 2 * NT)
                    pe.wait_ge(ptB_ev, 2 * NT)
                    pe.wait_ge(v_ev, NT)
                    pe_pv(pe, ps_b, 3, 1)
                    pe.wait_ge(pv_ev, 2 * NT)
                    pe_oT(pe)
                    pe.wait_ge(oT_ev, NT)
                    pe_proj(pe)

                @block.scalar
                def _(act):
                    act.wait_ge(eps_set, 1)
                    nc.scalar.activation(table_in[:], epsc[:], ACT.Sqrt)
                    act.wait_ge(zeroed, 1)
                    for n in range(FIRST):
                        act_root(act, n)
                        if n:
                            act_norm2(act, n, n % 2)
                    act.wait_ge(loaded, 16 * 11)
                    for g in range(2):
                        act_xT(act, g + 1)
                        act_q(act, g + 1, g)
                        act_k(act, g + 1, g)

                    def scores():
                        act.wait_ge(score_args, 1)
                        nc.scalar.activation(score[:], gt[:], ACT.Exp, scale=1.0 / eps_last).then_inc(score_done, 1)
                    groups(act, lambda it, k, extra, qkv: act_tile(act, it * 4 + k, k, extra, qkv), scores)
                    act_ptB(act, 2 * NT, 1)

                @block.vector
                def _(dve):
                    nc.vector.memset(mv[:], 1.0)
                    nc.vector.memset(epsc[:], LN_EPS).then_inc(eps_set, 1)
                    nc.vector.memset(ones[:], 1.0)
                    nc.vector.memset(kT[:], 0.0)
                    nc.vector.memset(vown[:], 1.0)
                    nc.vector.memset(vnb[:], 1.0).then_inc(zeroed, 1)
                    dve.wait_ge(zeroed, 1)
                    dve.wait_ge(first_loaded, 48)
                    for n in range(FIRST):
                        dve_stats(dve, n)
                        dve_norm(dve, n, n % 2)
                        dve_stats2(dve, n, n % 2)
                        if n:
                            for half in range(2):
                                dve_dots(dve, n - 1, 1 - n % 2, half)
                    dve.wait_ge(loaded, 16 * 11)
                    for g in range(2):
                        dve_v(dve, g + 1, g)

                    def edges(it):
                        if isinstance(it, int) and it == 0:
                            return
                        for m in range(2):
                            i = nc.vector.tensor_copy(edge[:, m, :], masks[:, bass.ds(it % 4 + m, 1), :]
                                                      .rearrange("p a j -> p (a j)"))
                        i.then_inc(edge_ready, 1)
                        dve.wait_ge(edge_ready, it)

                    def tile(it, k, extra, qkv):
                        if isinstance(it, int) and it == 0:
                            mask = masks[:, 0 if k == 0 else 1, :]
                        else:
                            mask = edge[:, k // 3, :] if k in (0, 3) else masks[:, 1, :]
                        dve_tile(dve, it * 4 + k, k, mask, extra, qkv)

                    def first_test():
                        nc.vector.memset(carry[:, 14:15], 0.0).then_inc(score_args, 1)
                        dve.wait_ge(score_done, 1)
                        dve_test(dve, 0)
                    groups(dve, tile, first_test, lambda: masks_of(dve), edges)
                    dve_ptA(dve, 2 * NT, 1)
                    dve_pv(dve, ps_b, 2 * NT, 1)
                    dve_oT(dve, NT)
                    dve_proj(dve, NT, NT - 1)

        with ExitStack() as ctx:
            light(ctx)

        def heavy(ctx):
            def sem(name):
                return ctx.enter_context(nc.semaphore(name))

            def st(name, shape, dt=F32):
                return sb(name, shape, dt, ctx)
            S = KSEL // P
            HH = DH // 2
            UB = S * HC
            UNITS = B * UB
            TASKS = ["x0", "x1", "q0", "q1", "k0", "k1", "v0", "tq0", "tq1", "v1", "tk0", "tk1"]
            SPREAD = [2, 1, 1, 1, 2, 2, 2, 1]
            EACH = len(TASKS) // 2
            MERGE_STEPS = [UNITS - -0, UNITS - -1]
            wq = h_wqo[:, 0].rearrange("p (c n) -> p c n", c=DC)
            wkv = h_wkv
            wo = h_wqo[:, 1].rearrange("p (c n) -> p c n", c=HC)
            gam = st("hgam", [P, DC])
            later_rows = st("hrows", [P, B - 1, 2 * S, D])
            later_rope = st("hrope", [P, B - 1, 2 * S, DH])
            rows = [h_rows0[:]] + [later_rows[:, b] for b in range(B - 1)]
            rope = [h_rope0[:]] + [later_rope[:, b] for b in range(B - 1)]
            sq = st("hsq", [P, 2 * S, D])
            ss = st("hss", [P, B, 2 * S])
            rn = st("hrn", [P, B, 2 * S])
            xT = st("hxT", [P, DC, 2 * KSEL])
            qk = st("hqk", [P, 2 * S, H, 2, HH])
            rot = st("hrot", [P, 2, H, 2, HH])
            val = st("hval", [P, 2, S, H, DH + 1])
            nval = st("hnval", [P, H, DH + 1])
            qT = st("hqT", [P, 2, HC, KSEL])
            kT = st("hkT", [P, 2, HC, KSEL + 1])
            mx = st("hmx", [P, 2, 2])
            nmx = st("hnmx", [P, 2, 2])
            prob = st("hprob", [P, 4, 2, KSEL + 1])
            probT = st("hprobT", [P, 2, S, 2, P])
            acc = st("hacc", [P, 2, 2, DH + 1])
            rden = st("hrden", [P, 2, 2])
            o = st("ho", [P, 2, H, DH])
            oT = st("hoT", [P, HC, P])
            res = h_out
            ps_s = ctx.enter_context(nc.psum_tensor("hps_s", [P, 2, 2, 512], F32))
            ps_x = ctx.enter_context(nc.psum_tensor("hps_x", [P, 2, 512], F32))
            ps_p = ctx.enter_context(nc.psum_tensor("hps_p", [P, 512], F32))
            ps_v = ctx.enter_context(nc.psum_tensor("hps_v", [P, 512], F32))
            loaded, val_set = sem("h_loaded"), sem("h_val_set")
            ss_done, sqrt_done, rows_ready = sem("h_ss_done"), sem("h_sqrt_done"), sem("h_rows_ready")
            front_done = [sem(f"h_front_done{k}") for k in range(2)]
            front_ev = [sem(f"h_front_ev{k}") for k in range(2)]
            roped = sem("h_roped")
            sim_done, max_done, exp_done = sem("h_sim_done"), sem("h_max_done"), sem("h_exp_done")
            pT_done, pT_ev = sem("h_pT_done"), sem("h_pT_ev")
            pv_done, pv_ev = sem("h_pv_done"), sem("h_pv_ev")
            oT_done, oT_ev = sem("h_oT_done"), sem("h_oT_ev")
            pr_done, pr_ev = sem("h_pr_done"), sem("h_pr_ev")
            saved = h_saved
            v = sem("h_v")

            def unit(u):
                return u // UB, u % UB // HC, u % HC

            def front_tasks(step):
                b, i = divmod(step, UB)
                if b + 1 >= B:
                    return []
                first = sum(SPREAD[:i])
                return [(b + 1, n) for n in range(first, first + SPREAD[i])]

            def pe_front(pe, b, n):
                name, k = TASKS[n], n % 2
                j = int(name[-1])
                count = b * EACH + n // 2
                if count:
                    pe.wait_ge(front_ev[k], count)
                if name[0] == "x":
                    pe.wait_ge(rows_ready, b + 1)
                    for t in range(2 * S):
                        i = nc.tensor.transpose(ps_x[:, k, t * P:(t + 1) * P], rows[b][:, t, j * P:(j + 1) * P], ident[:])
                elif name[0] == "t":
                    t = j + (S if name[1] == "k" else 0)
                    pe.wait_ge(roped, b * 2 * S + t + 1)
                    flat = qk[:, t].rearrange("p h a d -> p (h a d)")
                    for c in range(HC):
                        i = nc.tensor.transpose(ps_x[:, k, c * P:(c + 1) * P], flat[:, c * P:(c + 1) * P], ident[:])
                else:
                    for bank in range(2):
                        pe.wait_ge(front_ev[bank], b * EACH + 1)
                    w = {"q": wq, "k": wkv[:, :, 0:HD], "v": wkv[:, :, HD:2 * HD]}[name[0]]
                    at = (0 if name[0] == "q" else KSEL) + j * P
                    for c in range(DC):
                        i = nc.tensor.matmul(ps_x[:, k, :], xT[:, c, at:at + P], w[:, c, :], start=(c == 0), stop=(c == DC - 1))
                i.then_inc(front_done[k], 1)

            def act_front(act, b, n):
                name, k = TASKS[n], n % 2
                if name[0] not in "vt":
                    return
                act.wait_ge(front_done[k], b * EACH + n // 2 + 1)
                j = int(name[-1])
                if name[0] == "v":
                    i = nc.scalar.activation(val[:, b % 2, j, :, 0:DH], ps_x[:, k, :].rearrange("p (h d) -> p h d", h=H),
                                             ACT.Copy, scale=sel_gain[:, B + b, j:j + 1])
                else:
                    dst = qT if name[1] == "q" else kT
                    i = nc.scalar.copy(dst[:, b % 2, :, j * P:(j + 1) * P], ps_x[:, k, :].rearrange("p (c j) -> p c j", c=HC))
                i.then_inc(front_ev[k], 1)

            with nc.Block() as block:
                @block.sync
                def _(sp):
                    for dst, src in ((gam[:], ap["heavy_gamma"]), (nval[:, :, 0:DH], ap["null_v"])):
                        sp.dma_start(dst, src).then_inc(loaded, 16)
                    with nc.allow_non_contiguous_dma(reason="one null key column of 4 words a partition"):
                        for k in range(2):
                            sp.dma_start(kT[:, k, :, KSEL:KSEL + 1], ap["null_kT"]).then_inc(loaded, 16)
                    for dst, src in ((f_w[:], ap["ffn_w"]), (f_bias[:], ap["ffn_bias"]), (f_bo[:], ap["ffn_bo"])):
                        sp.dma_start(dst, src).then_inc(f_loaded, 16)
                    for e in range(TILES):
                        sp.wait_ge(pr_ev, e + 1)
                        sp.dma_start(heavy_rows[e // S][e % S * P:(e % S + 1) * P, :], res[:, e % 2, :]).then_inc(saved[e], 16)

                @block.gpsimd
                def _(pool):
                    nc.gpsimd.memset(val[:], 1.0).then_inc(val_set, 1)
                    for b in range(1, B):
                        gather_routed(pool, b, rows[b], rope[b])
                    nc.gpsimd.tensor_copy(f_idc[:], pos[:, :, 0:GT]).then_inc(idx_copied, 1)
                    pool.wait_ge(idx_copied, 1)
                    for b in range(EARLY):
                        for s in range(S):
                            pool.wait_ge(saved[b * S + s], 16)
                        gather_group(pool, b)

                @block.scalar
                def _(act):
                    def act_norm(n, b0, b1):
                        act.wait_ge(ss_done, n)
                        nc.scalar.activation(ss[:, b0:b1], ss[:, b0:b1], ACT.Sqrt).then_inc(sqrt_done, 1)
                    nc.scalar.activation(table_in[:], ident[:, 0:1], ACT.Sqrt)
                    act_norm(1, 0, 1)
                    act.wait_ge(loaded, 64)
                    act.wait_ge(val_set, 1)
                    for n in range(len(TASKS)):
                        act_front(act, 0, n)
                    act_norm(2, 1, B)
                    for step in range(UNITS):
                        act.wait_ge(max_done, step + 1)
                        if step >= 4:
                            act.wait_ge(pv_ev, step - 3)
                        for e in range(2):
                            i = nc.scalar.activation(prob[:, step % 4, e, :], ps_s[:, step % 2, e, 0:KSEL + 1], ACT.Exp,
                                                     bias=nmx[:, step % 2, e:e + 1], scale=SCALE)
                        i.then_inc(exp_done, 1)
                        for b, n in front_tasks(step):
                            act_front(act, b, n)

                @block.tensor
                def _(pe):
                    pe.wait_ge(loaded, 64)
                    pe.wait_ge(h_weights, 48)
                    for n in range(len(TASKS)):
                        pe_front(pe, 0, n)
                    for step in range(UNITS + 4):
                        if step < UNITS:
                            b, s, c = unit(step)
                            if step % UB == 0:
                                for k in range(2):
                                    pe.wait_ge(front_ev[k], (b + 1) * EACH)
                            for e in range(2):
                                i = nc.tensor.matmul(ps_s[:, step % 2, e, 0:KSEL + 1],
                                                     qT[64 * e:64 * e + 64, b % 2, c, s * P:(s + 1) * P],
                                                     kT[64 * e:64 * e + 64, b % 2, c, :], start=True, stop=True)
                            i.then_inc(sim_done, 1)
                        if 1 <= step <= UNITS:
                            u = step - 1
                            pe.wait_ge(exp_done, u + 1)
                            if u:
                                pe.wait_ge(pT_ev, u)
                            if step >= 7 and (step - 7) % HC == 0:
                                pe.wait_ge(oT_ev, (step - 7) // HC + 1)
                            for e in range(2):
                                for j in range(S):
                                    i = nc.tensor.transpose(ps_p[:, (j * 2 + e) * P:(j * 2 + e + 1) * P],
                                                            prob[:, u % 4, e, j * P:(j + 1) * P], ident[:])
                            i.then_inc(pT_done, 1)
                        for b, n in front_tasks(step) if step < UNITS else []:
                            pe_front(pe, b, n)
                        if 2 <= step <= UNITS + 1:
                            u = step - 2
                            b, s, c = unit(u)
                            pe.wait_ge(pT_ev, u + 1)
                            if u:
                                pe.wait_ge(pv_ev, u)
                            if step >= 8 and (step - 8) % HC == 0:
                                pe.wait_ge(pr_ev, (step - 8) // HC + 1)
                            for e in range(2):
                                for j in range(S):
                                    i = nc.tensor.matmul(ps_v[:, e * (DH + 1):(e + 1) * (DH + 1)], probT[:, u % 2, j, e, :],
                                                         val[:, b % 2, j, 2 * c + e, :], start=(j == 0), stop=(j == S - 1))
                            i.then_inc(pv_done, 1)
                        if step == UNITS:
                            pe.wait_ge(f_loaded, 48)
                            for q in range(3):
                                for m in range(DC):
                                    for c in range(DC):
                                        i = nc.tensor.matmul(ps_x[:, 0, q * DC + m:q * DC + m + 1],
                                                             f_w[:, 4 + q, c, m * P:(m + 1) * P],
                                                             f_bias[:, 3, c:c + 1], start=(c == 0), stop=(c == DC - 1))
                            i.then_inc(state_part, 1)
                        if step >= 6 and (step - 6) % HC == 0:
                            e = (step - 6) // HC
                            pe.wait_ge(pv_ev, (e + 1) * HC)
                            pe.wait_ge(pT_ev, min(step, UNITS))
                            flat = o[:, e % 2].rearrange("p h d -> p (h d)")
                            for c in range(HC):
                                i = nc.tensor.transpose(ps_p[:, c * P:(c + 1) * P], flat[:, c * P:(c + 1) * P], ident[:])
                            i.then_inc(oT_done, 1)
                        if step >= 7 and (step - 7) % HC == 0:
                            e = (step - 7) // HC
                            pe.wait_ge(oT_ev, e + 1)
                            pe.wait_ge(pv_ev, min(step - 1, UNITS))
                            for c in range(HC):
                                i = nc.tensor.matmul(ps_v[:, 0:D], oT[:, c, :], wo[:, c, :], start=(c == 0), stop=(c == HC - 1))
                            i.then_inc(pr_done, 1)

                @block.vector
                def _(dve):
                    cnt = [0]

                    def link(i):
                        cnt[0] += 1
                        i.then_inc(v, 1)
                        dve.wait_ge(v, cnt[0])

                    def dve_norm(n, b0, b1):
                        for b in range(b0, b1):
                            dve.wait_ge(got_rows[b], 16 * 2 * S)
                            for t in range(2 * S):
                                i = nc.vector.tensor_tensor_reduce(sq[:, t, :], rows[b][:, t, :], rows[b][:, t, :], 1.0, 0.0,
                                                                   ALU.mult, ALU.add, ss[:, b, t:t + 1])
                            if b < b1 - 1:
                                link(i)
                        i.then_inc(ss_done, 1)
                        dve.wait_ge(sqrt_done, n)
                        link(nc.vector.tensor_scalar(ss[:, b0:b1], ss[:, b0:b1], 1e-12, None, ALU.max))
                        link(nc.vector.reciprocal(rn[:, b0:b1], ss[:, b0:b1]))
                        for b in range(b0, b1):
                            for t in range(2 * S):
                                i = nc.vector.tensor_scalar(rows[b][:, t, :], rows[b][:, t, :], rn[:, b, t:t + 1],
                                                            float(D) ** 0.5, ALU.mult, ALU.mult)
                            i.then_inc(rows_ready, 1)

                    def dve_front(b, n):
                        name, k = TASKS[n], n % 2
                        if name[0] not in "xqk":
                            return
                        dve.wait_ge(front_done[k], b * EACH + n // 2 + 1)
                        j = int(name[-1])
                        if name[0] == "x":
                            nc.vector.tensor_scalar(xT[:, j, :], ps_x[:, k, :], gam[:, j:j + 1], None, ALU.mult
                                                    ).then_inc(front_ev[k], 1)
                            return
                        t = j + (S if name[0] == "k" else 0)
                        if t == 0:
                            dve.wait_ge(got_rope[b], 16 * 2 * S)
                        src = ps_x[:, k, :].rearrange("p (h a d) -> p h a d", h=H, a=2)
                        cos = rope[b][:, t, 0:HH].rearrange("p (o d) -> p o d", o=1)
                        sin = rope[b][:, t, HH:DH].rearrange("p (o d) -> p o d", o=1).broadcast_to([P, H, HH])
                        turned = rot[:, t % 2]
                        nc.vector.tensor_tensor(qk[:, t].rearrange("p h a d -> p (h a) d"),
                                                src.rearrange("p h a d -> p (h a) d"),
                                                cos.broadcast_to([P, 2 * H, HH]), ALU.mult)
                        nc.vector.tensor_tensor(turned[:, :, 0, :], src[:, :, 1, :], sin, ALU.mult)
                        count = b * EACH + n // 2
                        nc.vector.tensor_tensor(turned[:, :, 1, :], src[:, :, 0, :], sin, ALU.mult).then_inc(front_ev[k], 1)
                        dve.wait_ge(front_ev[k], count + 1)
                        nc.vector.tensor_tensor(qk[:, t, :, 0, :], qk[:, t, :, 0, :], turned[:, :, 0, :], ALU.subtract)
                        nc.vector.tensor_tensor(qk[:, t, :, 1, :], qk[:, t, :, 1, :], turned[:, :, 1, :], ALU.add
                                                ).then_inc(roped, 1)

                    nc.vector.memset(nval[:, :, DH:DH + 1], 1.0)
                    dve_norm(1, 0, 1)
                    dve.wait_ge(loaded, 64)
                    for n in range(len(TASKS)):
                        dve_front(0, n)
                    dve_norm(2, 1, B)
                    for step in range(UNITS + 4):
                        if step < UNITS:
                            dve.wait_ge(sim_done, step + 1)
                            link(nc.vector.tensor_reduce(mx[:, step % 2, :], ps_s[:, step % 2, :, 0:KSEL + 1], AX, ALU.max))
                            nc.vector.tensor_scalar(nmx[:, step % 2, :], mx[:, step % 2, :], -SCALE, None, ALU.mult
                                                    ).then_inc(max_done, 1)
                        if 1 <= step <= UNITS:
                            u = step - 1
                            dve.wait_ge(pT_done, u + 1)
                            nc.vector.tensor_copy(probT[:, u % 2].rearrange("p j e q -> p (j e q)"), ps_p[:]).then_inc(pT_ev, 1)
                        for b, n in front_tasks(step) if step < UNITS else []:
                            dve_front(b, n)
                        if 2 <= step <= UNITS + 1:
                            u = step - 2
                            _, s, c = unit(u)
                            dve.wait_ge(pv_done, u + 1)
                            for e in range(2):
                                i = nc.vector.scalar_tensor_tensor(out=acc[:, u % 2, e, :], in0=nval[:, 2 * c + e, :],
                                                                   scalar=prob[:, u % 4, e, KSEL:KSEL + 1],
                                                                   in1=ps_v[:, e * (DH + 1):(e + 1) * (DH + 1)],
                                                                   op0=ALU.mult, op1=ALU.add)
                            link(i)
                            link(nc.vector.reciprocal(rden[:, u % 2, :], acc[:, u % 2, :, DH]))
                            nc.vector.tensor_tensor(o[:, (u // HC) % 2, 2 * c:2 * c + 2, :], acc[:, u % 2, :, 0:DH],
                                                    rden[:, u % 2, :].rearrange("p (h o) -> p h o", o=1)
                                                    .broadcast_to([P, 2, DH]), ALU.mult).then_inc(pv_ev, 1)
                        if step >= 6 and (step - 6) % HC == 0:
                            e = (step - 6) // HC
                            dve.wait_ge(oT_done, e + 1)
                            nc.vector.tensor_copy(oT[:].rearrange("p c j -> p (c j)"), ps_p[:]).then_inc(oT_ev, 1)
                        if step >= 7 and (step - 7) % HC == 0:
                            e = (step - 7) // HC
                            b, s = divmod(e, S)
                            dve.wait_ge(pr_done, e + 1)
                            if e >= 2:
                                dve.wait_ge(saved[e - 2], 16)
                            nc.vector.tensor_scalar(res[:, e % 2, :], ps_v[:, 0:D], sel_gain[:, b, s:s + 1], None, ALU.mult
                                                    ).then_inc(pr_ev, 1)
                        if step == UNITS + 1:
                            dve.wait_ge(state_part, 1)
                            nc.vector.tensor_tensor(bias0[:], ps_x[:, 0, 0:3 * DC].rearrange("p (q m) -> p q m", q=3),
                                                    f_bias[:, 0:3, :], ALU.add).then_inc(bias0_ready, 1)
                        if step in MERGE_STEPS:
                            b = MERGE_STEPS.index(step)
                            dve_merge(dve, 0, range(b * GT, (b + 1) * GT), b == EARLY - 1)

        late = top.enter_context(ExitStack())
        GT = 4
        f_w = sb("fw", [P, 8, DC, D], F32, late)
        f_bias = sb("fbias", [P, 4, DC], F32, late)
        f_bo = sb("fbo", [P, D], F32, late)
        f_idc = sb("fidc", [P, B, GT], I32, late)
        f_raw = sb("fraw", [P, B, GT, D], F32, late)
        f_loaded, idx_copied = late.enter_context(nc.semaphore("f_loaded")), late.enter_context(nc.semaphore("f_idx_copied"))
        got = [late.enter_context(nc.semaphore(f"f_got{b}")) for b in range(B)]

        M = B * GT
        TILES = B * KSEL // P
        EARLY = 2
        bias0 = sb("fbias0", [P, 3, DC], F32, late)
        state_part, bias0_ready = (late.enter_context(nc.semaphore(n)) for n in ("f_state_part", "f_bias0_ready"))
        h_out = sb("h_out", [P, 2, D], F32, late)
        h_saved = [late.enter_context(nc.semaphore(f"h_saved{e}")) for e in range(TILES)]
        stats = sb("fstats", [P, M, 6], F32, late)
        mv = sb("fmv", [P, M, 2], F32, late)
        carry = sb("fcarry", [P, 1], F32, late)
        merged, stats_done, var_ready = (late.enter_context(nc.semaphore(n)) for n in ("f_merged", "f_stats_done", "f_var_ready"))

        def row(g, j):
            b, t = divmod(j, GT)
            return hres[:, bass.ds(g * GT + (b * T + t), 1), :].rearrange("p a d -> p (a d)")

        def dve_merge(dve, g, js, done):
            for j in js:
                b, t = divmod(j, GT)
                if t == 0:
                    dve.wait_ge(got[b], (g + 1) * (16 * GT))
                nc.vector.tensor_tensor(row(g, j), row(g, j), f_raw[:, b, t, :], ALU.add).then_inc(merged, 1)
            dve.wait_ge(merged, g * M + (js[-1] + 1))
            nc.vector.memset(carry[:], 0.0)
            for j in js:
                nc.vector.bn_stats(stats[:, j, :], row(g, j)).then_inc(stats_done, 1)
            dve.wait_ge(stats_done, g * M + (js[-1] + 1))
            nc.vector.memset(carry[:], 0.0)
            for j in js:
                i = nc.vector.bn_aggr(mv[:, j, :], stats[:, j, :])
            if done:
                i.then_inc(var_ready, 1)

        def gather_group(pool, b):
            for t in range(GT):
                pool.indirect_dma_start(f_raw[:, b, t, :], None, heavy_rows[b],
                                        bass.IndirectOffsetOnAxis(ap=f_idc[:, b, t:t + 1], axis=0)
                                        ).then_inc(got[b], 16)

        with ExitStack() as ctx:
            heavy(ctx)

        def ffn(ctx):
            def sem(name):
                return ctx.enter_context(nc.semaphore(name))

            def st(name, shape, dt=F32):
                return sb(name, shape, dt, ctx)
            ZB = 4
            GN = GT * P
            NG = T // GT
            w, bias, bo, idc, raw, loaded = f_w, f_bias, f_bo, f_idc, f_raw, f_loaded
            epsc = st("fepsc", [P, 1])
            sd = st("fsd", [P, B * GT])
            rstd = st("frstd", [P, B * GT])
            stage = st("fstage", [P, 2, GT, D])
            xT = st("fxT", [P, B, DC, GN])
            cT = st("fcT", [P, DC, GN])
            gates = st("fgates", [P, 3, GN])
            t1 = st("ft1", [P, GN])
            cf = st("fcf", [P, GT, D])
            z = st("fz", [P, ZB, 2, D])
            y = st("fy", [P, ZB, 2, D])
            ps_g = ctx.enter_context(nc.psum_tensor("fps_g", [P, 6, 512], F32))
            ps_t = ctx.enter_context(nc.psum_tensor("fps_t", [P, 2, 512], F32))
            idx_settled = sem("f_idx_settled")
            eps_set, sd_ready, rstd_ready = sem("f_eps_set"), sem("f_sd_ready"), sem("f_rstd_ready")
            xT_done, xT_ev = sem("f_xT_done"), sem("f_xT_ev")
            gate_done, gate_ev = sem("f_gate_done"), sem("f_gate_ev")
            c_ready, v = sem("f_c_ready"), sem("f_v")
            staged = sem("f_staged")
            cf_done, cf_ev = sem("f_cf_done"), sem("f_cf_ev")
            out_done, z_ready, tanh_done, y_ready = (sem("f_out_done"), sem("f_z_ready"), sem("f_tanh_done"),
                                                     sem("f_y_ready"))
            saved = [sem(f"f_saved{k}") for k in range(ZB)]
            NO = B * GT // 2
            FREE = ZB

            def x_bank(b, c):
                return ps_t[:, c, :] if b else ps_g[:, 4 + c, :]

            def out_bank(n):
                return ps_t[:, n % 4, :] if n % 4 < 2 else ps_g[:, n % 4, :]

            def pe_transposes(pe, g, b):
                pe.wait_ge(staged, g * B + (b + 1))
                for c in range(DC):
                    if b > 1:
                        pe.wait_ge(xT_ev, g * (B * DC) + ((b - 1) * DC + c + 1))
                    for t in range(GT):
                        i = nc.tensor.transpose(x_bank(b, c)[:, t * P:(t + 1) * P],
                                                stage[:, b % 2, t, c * P:(c + 1) * P], ident[:])
                    i.then_inc(xT_done, 1)

            def pe_group(pe, g, last):

                def x_part(b):
                    pe.wait_ge(xT_ev, g * (B * DC) + (b + 1) * DC)
                    for m in range(DC):
                        for q in range(3):
                            if b:
                                pe.wait_ge(gate_ev, g * (B * 6) + ((b - 1) * 6 + m * 3 + q + 1))
                            for c in range(DC):
                                i = nc.tensor.matmul(ps_g[:, m * 3 + q, :], w[:, q, c, m * P:(m + 1) * P], xT[:, b, c, :],
                                                     start=(c == 0), stop=(b == 0 and c == DC - 1))
                            if b == 0:
                                i.then_inc(gate_done, 1)

                def c_part(b):
                    pe.wait_ge(c_ready, g * B + b)
                    for m in range(DC):
                        for q in range(3):
                            for c in range(DC):
                                i = nc.tensor.matmul(ps_g[:, m * 3 + q, :], w[:, 4 + q, c, m * P:(m + 1) * P],
                                                     cT[:, c, :], start=False, stop=(c == DC - 1))
                            i.then_inc(gate_done, 1)

                x_part(0)
                for b in range(B):
                    if b + 1 < B:
                        pe_transposes(pe, g, b + 1)
                    if b:
                        c_part(b)
                    if b + 1 < B:
                        x_part(b + 1)
                pe.wait_ge(xT_ev, g * (B * DC) + B * DC)
                for n in range(NO):
                    b, h = divmod(n, GT // 2)
                    if n in (2, 3):
                        pe.wait_ge(gate_ev, g * (B * 6) + ((B - 1) * 6 + n + 1))
                    if n == 4:
                        pe.wait_ge(c_ready, g * B + B)
                        for h2 in range(GT // 2):
                            for t in range(2):
                                for c in range(DC):
                                    j = 2 * h2 + t
                                    i = nc.tensor.matmul(ps_g[:, h2, t * D:(t + 1) * D], cT[:, c, j * P:(j + 1) * P],
                                                         w[:, 7, c, :], start=(c == 0), stop=(c == DC - 1))
                            i.then_inc(cf_done, 1)
                        if not last:
                            pe.wait_ge(gate_ev, g * (B * 6) + B * 6)
                            pe_transposes(pe, g + 1, 0)
                    if n >= 4:
                        pe.wait_ge(z_ready, g * NO + (n - 3))
                    for t in range(2):
                        for c in range(DC):
                            j = 2 * h + t
                            i = nc.tensor.matmul(out_bank(n)[:, t * D:(t + 1) * D], xT[:, b, c, j * P:(j + 1) * P],
                                                 w[:, 3, c, :], start=(c == 0), stop=(c == DC - 1))
                    i.then_inc(out_done, 1)
                pe.wait_ge(z_ready, g * NO + NO)

            def act_root(act, n, lo=0, hi=M):
                act.wait_ge(var_ready, n)
                nc.scalar.activation(sd[:, lo:hi], mv[:, lo:hi, 1], ACT.Sqrt, bias=epsc[:, 0:1]).then_inc(sd_ready, 1)

            def act_group(act, g, last):
                for b in range(B):
                    for m in range(DC):
                        for q in range(3):
                            n = b * 6 + m * 3 + q
                            act.wait_ge(gate_done, g * (B * 6) + (n + 1))
                            if q == 0 and n:
                                act.wait_ge(v, g * (B * DC * 3) + (b * DC + m) * 3)
                            nc.scalar.activation(gates[:, q, :], ps_g[:, m * 3 + q, :],
                                                 ACT.Tanh if q == 2 else ACT.Sigmoid,
                                                 bias=(bias if b else bias0)[:, q, m:m + 1]
                                                 ).then_inc(gate_ev, 1)
                if not last:
                    act_root(act, g + 3)
                for n in range(NO):
                    act.wait_ge(z_ready, g * NO + (n + 1))
                    nc.scalar.activation(z[:, n % ZB], z[:, n % ZB], ACT.Tanh).then_inc(tanh_done, 1)
                act.wait_ge(v, (g + 1) * (B * DC * 3))

            def dve_rstd(dve, n, lo=0, hi=M):
                dve.wait_ge(sd_ready, n)
                nc.vector.reciprocal(rstd[:, lo:hi], sd[:, lo:hi]).then_inc(rstd_ready, 1)
                dve.wait_ge(rstd_ready, n)

            def dve_normalise(dve, g, b):
                for t in range(GT):
                    j = b * GT + t
                    i = nc.vector.tensor_scalar(stage[:, b % 2, t, :], row(g, j), mv[:, j, 0:1], rstd[:, j:j + 1],
                                                ALU.subtract, ALU.mult)
                i.then_inc(staged, 1)

            def dve_evacuate_x(dve, g, b):
                for c in range(DC):
                    dve.wait_ge(xT_done, g * (B * DC) + (b * DC + c + 1))
                    nc.vector.tensor_copy(xT[:, b, c, :], x_bank(b, c)).then_inc(xT_ev, 1)

            def dve_group(dve, g, last, first=False):
                dve_normalise(dve, g, 1)
                if first:
                    dve_merge(dve, 0, range(EARLY * GT, M), True)
                    dve_rstd(dve, 2, EARLY * GT, M)
                for b in range(B):
                    if b + 1 < B:
                        dve_evacuate_x(dve, g, b + 1)
                    if b + 2 < B:
                        dve_normalise(dve, g, b + 2)
                    if b >= 2 and not last:
                        dve.wait_ge(staged, g * B + B)
                        dve_merge(dve, g + 1, range((b - 2) * M // 2, (b - 1) * M // 2), b == B - 1)
                    dve.wait_ge(gate_done, g * (B * 6) + (b + 1) * 6)
                    for m in range(DC):
                        k = (b * DC + m) * 3
                        dve.wait_ge(gate_ev, g * (B * 6) + (b * 6 + m * 3 + 3))
                        nc.vector.tensor_tensor(t1[:], gates[:, 1, :], gates[:, 2, :], ALU.mult).then_inc(v, 1)
                        if b:
                            nc.vector.tensor_tensor(cT[:, m, :], cT[:, m, :], gates[:, 0, :], ALU.mult).then_inc(v, 1)
                        else:
                            nc.vector.tensor_scalar(cT[:, m, :], gates[:, 0, :], bias[:, 3, m:m + 1], None, ALU.mult
                                                    ).then_inc(v, 1)
                        dve.wait_ge(v, g * (B * DC * 3) + (k + 2))
                        i = nc.vector.tensor_tensor(cT[:, m, :], cT[:, m, :], t1[:], ALU.add)
                        i.then_inc(v, 1)
                    dve.wait_ge(v, g * (B * DC * 3) + (b + 1) * DC * 3)
                    nc.vector.tensor_copy(t1[:, 0:1], cT[:, 0, 0:1]).then_inc(c_ready, 1)
                if not last:
                    dve_rstd(dve, g + 3)
                    dve_normalise(dve, g + 1, 0)
                for h in range(GT // 2):
                    dve.wait_ge(cf_done, g * 2 + (h + 1))
                    nc.vector.tensor_tensor(cf[:, 2 * h:2 * h + 2, :], ps_g[:, h, :].rearrange("p (t d) -> p t d", t=2),
                                            bo[:].rearrange("p (o d) -> p o d", o=1).broadcast_to([P, 2, D]), ALU.add
                                            ).then_inc(cf_ev, 1)
                dve.wait_ge(cf_ev, g * 2 + 2)
                for n in range(NO):
                    b, h = divmod(n, GT // 2)
                    if n == 4 and not last:
                        dve_evacuate_x(dve, g + 1, 0)
                    dve.wait_ge(out_done, g * NO + (n + 1))
                    dve.wait_ge(y_ready, g * NO + (n + 1))
                    nc.vector.tensor_tensor(z[:, n % ZB], out_bank(n).rearrange("p (t d) -> p t d", t=2),
                                            cf[:, 2 * h:2 * h + 2, :], ALU.add).then_inc(z_ready, 1)

            def pool_gather(pool, g):
                nc.gpsimd.tensor_copy(idc[:], pos[:, :, bass.ds(g * GT, GT)]).then_inc(idx_copied, 1)
                pool.wait_ge(idx_copied, g + 1)
                pool.sem_inc(idx_settled, 1)
                for b in range(B):
                    gather_group(pool, b)

            def pool_group(pool, g, last):
                if not last:
                    pool.wait_ge(merged, (g + 1) * M)
                    pool_gather(pool, g + 1)
                for n in range(NO):
                    b, h = divmod(n, GT // 2)
                    pool.wait_ge(tanh_done, g * NO + (n + 1))
                    if n >= ZB:
                        pool.wait_ge(saved[n % ZB], g * (16 * NO // ZB) + 16 * (n // ZB))
                    nc.gpsimd.tensor_tensor(y[:, n % ZB].rearrange("p t d -> p (t d)"),
                                            z[:, n % ZB].rearrange("p t d -> p (t d)"),
                                            hres[:, bass.ds(g * GT + (b * T + 2 * h), 2), :].rearrange("p t d -> p (t d)"),
                                            ALU.add).then_inc(y_ready, 1)
                for k in range(ZB):
                    pool.wait_ge(saved[k], (g + 1) * (16 * NO // ZB))

            with nc.Block() as block:
                @block.sync
                def _(sp):
                    rows = out.rearrange("b (t p) d -> p (b t) d", p=P)
                    with sp.Fori(0, NG) as g:
                        for n in range(NO):
                            b, h = divmod(n, GT // 2)
                            sp.wait_ge(y_ready, g * NO + (FREE + n + 1))
                            sp.dma_start(rows[:, bass.ds(g * GT + (b * T + 2 * h), 2), :], y[:, n % ZB]).then_inc(saved[n % ZB], 16)
                    for k in range(ZB):
                        sp.wait_ge(saved[k], 16 * NG * NO // ZB)

                @block.tensor
                def _(pe):
                    pe.wait_ge(loaded, 48)
                    pe_transposes(pe, 0, 0)
                    with pe.Fori(0, NG - 1) as g:
                        pe_group(pe, g, False)
                    pe_group(pe, NG - 1, True)

                @block.scalar
                def _(act):
                    act.wait_ge(loaded, 48)
                    act.wait_ge(eps_set, 1)
                    nc.scalar.activation(table_in[:], ident[:, 0:1], ACT.Sqrt)
                    act_root(act, 1, 0, EARLY * GT)
                    act.wait_ge(bias0_ready, 1)
                    act_root(act, 2, EARLY * GT, M)
                    act_group(act, 0, False)
                    with act.Fori(1, NG - 1) as g:
                        act_group(act, g, False)
                    act_group(act, NG - 1, True)

                @block.vector
                def _(dve):
                    nc.vector.memset(epsc[:], LN_EPS).then_inc(eps_set, 1)
                    dve.wait_ge(loaded, 48)
                    dve_rstd(dve, 1, 0, EARLY * GT)
                    dve_normalise(dve, 0, 0)
                    dve_evacuate_x(dve, 0, 0)
                    dve_group(dve, 0, False, True)
                    with dve.Fori(1, NG - 1) as g:
                        dve_group(dve, g, False)
                    dve_group(dve, NG - 1, True)

                @block.gpsimd
                def _(pool):
                    pool.sem_inc(y_ready, FREE)
                    for b in range(EARLY, B):
                        for s in range(KSEL // P):
                            pool.wait_ge(h_saved[b * (KSEL // P) + s], 16)
                        gather_group(pool, b)
                    with pool.Fori(0, NG - 1) as g:
                        pool_group(pool, g, False)
                    pool_group(pool, NG - 1, True)

        with ExitStack() as ctx:
            ffn(ctx)


def constants():
    f = np.float32
    eps, _ = descent_eps()
    e = np.array(eps, np.float64)
    descent = np.stack([-1.0 / e, e, -e * LOGK]).astype(f)
    bits = np.array([1 << (SEARCH_BITS - 1 - i) for i in range(SEARCH_BITS)] + [0], np.uint32)
    col = np.arange(R * T)
    not_first = (col % T != 0).astype(f)
    p = np.arange(P)[:, None]
    tokid = (((col // T) % B) * N + (col % T) * P + p).astype(f)
    masks = np.zeros((P, 5, 2 * P), f)
    q = np.arange(P)[:, None]
    own = np.abs(q - np.arange(P)[None]) > W
    nxt = (P + np.arange(W)[None] - q) > W
    prv = (q - (np.arange(W)[None] + W - P)) > W
    for m in range(5):
        masks[:, m, 0:P][own] = NEG
        masks[:, m, P:P + W][nxt | (np.zeros_like(nxt) | (m == 4))] = NEG
        masks[:, m, P + W:][prv | (np.zeros_like(prv) | (m == 0))] = NEG
    ang = (np.arange(N, dtype=f)[:, None] * (1.0 / (10000.0 ** (np.arange(0, DH, 2) / DH))).astype(f)[None]).astype(f)
    bcast = lambda a: np.ascontiguousarray(np.broadcast_to(a, (P,) + a.shape))
    return {
        "descent": bcast(descent), "bits": bcast(bits), "not_first": bcast(not_first),
        "tri": np.triu(np.ones((P, P), f), 1), "iota16": bcast(np.arange(16, dtype=f)), "tokid": tokid,
        "ident": np.eye(P, dtype=f),
        "masks": masks.astype(np.dtype("bfloat16")),
        "rope": np.concatenate([np.cos(ang.astype(np.float64)), np.sin(ang.astype(np.float64))], 1).astype(f),
    }


def kernel(**inputs):
    import concourse.bacc as bacc
    from concourse.bass_utils import run_bass_kernel_spmd as run

    a = {k: np.asarray(v) for k, v in inputs.items()}
    at = lambda n: a["L0_attn_" + n]
    ff = lambda n: a["L0_ffn_" + n]
    rows = lambda v: np.ascontiguousarray(np.broadcast_to(v, (P,) + v.shape))
    chunks = lambda v: v.reshape(DC, P).T
    mats = [ff("wf").T, ff("wi").T, ff("wc").T, ff("wo").T, ff("uf").T, ff("ui").T, ff("uc").T, ff("uo").T]
    kv = at("heavy_kv_w").reshape(H, 2, DH, D)
    null = at("heavy_null_kv")
    arrays = {
        "ids": a["x"].reshape(NT, P).T,
        "table": a["L0_tok_weight"].T,
        "tok_bias": rows(a["L0_tok_bias"]),
        "route_tok": rows(np.stack([at("q_route_tok"), at("kv_route_tok")])),
        "null_q": at("null_q_token").reshape(1, D),
        "wqkv": at("light_qkv_w"),
        "light_out_w": at("light_out_w"),
        "ln_affine": np.stack([chunks(at("ln_gamma")), chunks(at("ln_beta"))], 1),
        "heavy_q_w": at("heavy_q_w"),
        "heavy_kv_w": kv.transpose(3, 1, 0, 2).reshape(D, 2 * HD),
        "heavy_out_w": at("heavy_out_w"),
        "heavy_gamma": chunks(at("heavy_gamma")),
        "null_kT": null[0].reshape(HC, P).T.reshape(P, HC, 1),
        "null_v": rows(null[1].reshape(H, DH)),
        "ffn_w": np.stack([m.reshape(DC, P, D).transpose(1, 0, 2) for m in mats], 1),
        "ffn_bias": np.stack([chunks(ff("bf")), chunks(ff("bi")), chunks(ff("bc")), chunks(ff("in_c"))], 1),
        "ffn_bo": rows(ff("bo")),
    }
    arrays.update(constants())
    nc = bacc.Bacc("TRN2", target_bir_lowering=False, num_devices=1)
    ap, feeds = {}, {}
    for name, v in arrays.items():
        v = np.ascontiguousarray(v)
        feeds[f"in_{name}"] = v
        ap[name] = nc.dram_tensor(f"in_{name}", v.shape, mybir.dt.from_np(v.dtype), kind="ExternalInput").ap()
    out = nc.dram_tensor("out", (B, N, D), F32, kind="ExternalOutput").ap()
    lm_tower(nc, ap, out)
    return run(nc, [feeds], core_ids=[0]).results[0]["out"]
```
